# Optimizing a Trainium2 kernel written in Bass

```python
import numpy as np
import jax
import jax.numpy as jnp

def _softmax(x, axis=-1):
    return jax.nn.softmax(x, axis=axis)

def _gelu(x):
    return jax.nn.gelu(x, approximate=True)

def _silu(x):
    return jax.nn.silu(x)

def _sigmoid(x):
    return jax.nn.sigmoid(x)

def _layernorm(x, axis=-1, eps=1e-05):
    m = jnp.mean(x, axis=axis, keepdims=True)
    v = jnp.var(x, axis=axis, keepdims=True)
    return (x - m) / jnp.sqrt(v + eps)

def _scatter_add(tgt, idx, src, axis=0):
    return tgt.at[idx].add(src)

def _segment_sum(src, seg, n):
    return jax.ops.segment_sum(src, seg, n)
kernel_name = 'mk_gnn_preln_d2_gnn_r64_ee099b'

def setup_inputs(seed: int=0):
    np.random.seed(seed)
    _w = jnp.asarray

    def _rec_inputs():
        import jax
        import jax.numpy as jnp
        _gk = jax.random.key(seed)
        x = -0.0004402 + 1 * jax.random.normal(jax.random.fold_in(_gk, 1), (100000, 16), jnp.float32)
        src = jax.random.randint(jax.random.fold_in(_gk, 2), (50000,), 0, 100000, jnp.int32)
        dst = jax.random.randint(jax.random.fold_in(_gk, 3), (50000,), 0, 100000, jnp.int32)
        _o = jnp.argsort(dst, stable=True)
        src = src[_o]
        dst = dst[_o]
        edge_attr_16 = -3.57403e-05 + 0.999761 * jax.random.normal(jax.random.fold_in(_gk, 12), (50000, 16), jnp.float32)
        return (x, src, dst, edge_attr_16)
    x, src, dst, edge_attr_16 = _rec_inputs()

    def _L0_gnn_setup():
        import jax, jax.numpy as jnp
        import numpy as np
        N_NODES = 30000
        N_EDGES = 300000
        IN_FEATS = 16
        OUT_FEATS = 16
        EDGE_DIM = 16
        key = jax.random.key(seed)
        ks = jax.random.split(key, 8)
        feat = jax.random.normal(ks[0], (N_NODES, IN_FEATS), dtype=jnp.float32)
        efeat = jax.random.normal(ks[1], (N_EDGES, EDGE_DIM), dtype=jnp.float32)
        W_msg = jax.random.normal(ks[2], (EDGE_DIM, IN_FEATS * OUT_FEATS), dtype=jnp.float32) * 0.1
        b_msg = jnp.zeros((IN_FEATS * OUT_FEATS,), dtype=jnp.float32)
        W_attn = jax.random.normal(ks[3], (EDGE_DIM, IN_FEATS * OUT_FEATS), dtype=jnp.float32) * 0.1
        b_attn = jnp.zeros((IN_FEATS * OUT_FEATS,), dtype=jnp.float32)
        src = jax.random.randint(ks[4], (N_EDGES,), 0, N_NODES, dtype=jnp.int32)
        dst = jax.random.randint(ks[5], (N_EDGES,), 0, N_NODES, dtype=jnp.int32)
        return {'feat': feat, 'efeat': efeat, 'W_msg': W_msg, 'b_msg': b_msg, 'W_attn': W_attn, 'b_attn': b_attn, 'src': src, 'dst': dst}
    _L0_gnn_all = _L0_gnn_setup()
    _L0_gnn_in = {k: v for k, v in _L0_gnn_all.items() if k in ('W_msg', 'b_msg', 'W_attn', 'b_attn')}
    del _L0_gnn_all

    def _L1_gnn_setup():
        import jax, jax.numpy as jnp
        import numpy as np
        N_NODES = 100000
        N_EDGES = 25000

        def _sage_conv(x, edge_index, W_l, b, W_r, num_nodes):
            src, dst = (edge_index[0], edge_index[1])
            msg_sum = jax.ops.segment_sum(x[src], dst, num_segments=num_nodes)
            deg = jax.ops.segment_sum(jnp.ones((edge_index.shape[1],), x.dtype), dst, num_segments=num_nodes)
            agg = msg_sum / jnp.maximum(deg, 1.0)[:, None]
            return agg @ W_l + b + x @ W_r
        key = jax.random.key(seed)
        ks = jax.random.split(key, 8)
        x = jax.random.normal(ks[0], (N_NODES, 16), dtype=jnp.float32)
        edge_index = jax.random.randint(ks[1], (2, N_EDGES), 0, N_NODES, dtype=jnp.int64)
        s1 = 1.0 / np.sqrt(16.0)
        s2 = 1.0 / np.sqrt(32.0)
        W1_l = jax.random.normal(ks[2], (16, 32), dtype=jnp.float32) * s1
        b1 = jax.random.normal(ks[3], (32,), dtype=jnp.float32) * s1
        W1_r = jax.random.normal(ks[4], (16, 32), dtype=jnp.float32) * s1
        W2_l = jax.random.normal(ks[5], (32, 16), dtype=jnp.float32) * s2
        b2 = jax.random.normal(ks[6], (16,), dtype=jnp.float32) * s2
        W2_r = jax.random.normal(ks[7], (32, 16), dtype=jnp.float32) * s2
        return {'x': x, 'edge_index': edge_index, 'W1_l': W1_l, 'b1': b1, 'W1_r': W1_r, 'W2_l': W2_l, 'b2': b2, 'W2_r': W2_r}
    _L1_gnn_all = _L1_gnn_setup()
    _L1_gnn_in = {k: v for k, v in _L1_gnn_all.items() if k in ('W1_l', 'b1', 'W1_r', 'W2_l', 'b2', 'W2_r')}
    del _L1_gnn_all
    return {'x': x, 'src': src, 'dst': dst, 'edge_attr_16': edge_attr_16, 'L0_gnn_W_msg': _L0_gnn_in['W_msg'], 'L0_gnn_b_msg': _L0_gnn_in['b_msg'], 'L0_gnn_W_attn': _L0_gnn_in['W_attn'], 'L0_gnn_b_attn': _L0_gnn_in['b_attn'], 'L1_gnn_W1_l': _L1_gnn_in['W1_l'], 'L1_gnn_b1': _L1_gnn_in['b1'], 'L1_gnn_W1_r': _L1_gnn_in['W1_r'], 'L1_gnn_W2_l': _L1_gnn_in['W2_l'], 'L1_gnn_b2': _L1_gnn_in['b2'], 'L1_gnn_W2_r': _L1_gnn_in['W2_r']}

def reference(x, src, dst, edge_attr_16, L0_gnn_W_msg, L0_gnn_b_msg, L0_gnn_W_attn, L0_gnn_b_attn, L1_gnn_W1_l, L1_gnn_b1, L1_gnn_W1_r, L1_gnn_W2_l, L1_gnn_b2, L1_gnn_W2_r):
    import jax
    import jax.numpy as jnp

    def _L0_gnn_ref(feat, efeat, W_msg, b_msg, W_attn, b_attn, src, dst):
        import jax, jax.numpy as jnp
        import numpy as np
        N_NODES = 30000
        N_EDGES = 300000
        IN_FEATS = 16
        OUT_FEATS = 16
        EDGE_DIM = 16
        N, in_f = feat.shape
        E = efeat.shape[0]
        w_m = (efeat @ W_msg + b_msg).reshape(E, in_f, -1)
        w_a = (efeat @ W_attn + b_attn).reshape(E, in_f, -1)
        h_src = feat[src][:, :, None]
        e1 = w_m * h_src
        e2 = w_a * h_src
        seg_max = jax.ops.segment_max(e2, dst, num_segments=N)
        ex = jnp.exp(e2 - seg_max[dst])
        denom = jax.ops.segment_sum(ex, dst, num_segments=N)
        attn = ex / denom[dst]
        ft = jax.ops.segment_sum(e1 * attn, dst, num_segments=N)
        return ft.sum(axis=1)

    def _L1_gnn_ref(x, edge_index, W1_l, b1, W1_r, W2_l, b2, W2_r):
        import jax, jax.numpy as jnp
        import numpy as np
        N_NODES = 100000
        N_EDGES = 25000

        def _sage_conv(x, edge_index, W_l, b, W_r, num_nodes):
            src, dst = (edge_index[0], edge_index[1])
            msg_sum = jax.ops.segment_sum(x[src], dst, num_segments=num_nodes)
            deg = jax.ops.segment_sum(jnp.ones((edge_index.shape[1],), x.dtype), dst, num_segments=num_nodes)
            agg = msg_sum / jnp.maximum(deg, 1.0)[:, None]
            return agg @ W_l + b + x @ W_r
        n = x.shape[0]
        h = _sage_conv(x, edge_index, W1_l, b1, W1_r, n)
        h = jax.nn.relu(h)
        out = _sage_conv(h, edge_index, W2_l, b2, W2_r, n)
        return out
    edge_index = jnp.stack([src, dst])
    h = jnp.maximum(_layernorm(x, axis=-1), 0.0)
    x = x + _L0_gnn_ref(h, edge_attr_16, L0_gnn_W_msg, L0_gnn_b_msg, L0_gnn_W_attn, L0_gnn_b_attn, src, dst)
    h = jnp.maximum(_layernorm(x, axis=-1), 0.0)
    x = x + _L1_gnn_ref(h, edge_index, L1_gnn_W1_l, L1_gnn_b1, L1_gnn_W1_r, L1_gnn_W2_l, L1_gnn_b2, L1_gnn_W2_r)
    return x

_drawn_inputs = setup_inputs


def setup_inputs(seed=0):
    import zlib

    import numpy as np

    out = dict(_drawn_inputs(seed))
    spreads = {'L0_gnn_b_msg': (0.0, 0.1), 'L0_gnn_b_attn': (0.0, 0.698)}
    factors = {}
    for name, (base, spread) in spreads.items():
        noise = np.random.default_rng([zlib.crc32(name.encode()), seed]).standard_normal(out[name].shape)
        drawn = base * np.exp(spread * noise) if base else spread * noise
        out[name] = jnp.asarray(drawn.astype(out[name].dtype))
    for name, factor in factors.items():
        out[name] = (out[name] * factor).astype(out[name].dtype)
    return out
```

```python
from contextlib import ExitStack

import concourse.bass as bass
from concourse import mybir
import numpy as np

f32 = mybir.dt.float32
bf16 = mybir.dt.bfloat16
i32 = mybir.dt.int32
ALU = mybir.AluOpType
ACT = mybir.ActivationFunctionType
AX = mybir.AxisListType

P = 128
N, E, F = 100000, 50000, 16
HID = 32
CH = F * F
CHUNK = 512
J = CHUNK // P
Q = 2
T = Q * J
ITE = Q * CHUNK
NI = -(-E // ITE)
EP = NI * ITE
NC = EP // CHUNK
EK = F + 1
HB0 = 32
LK = 2 * F + 1
HK = HID + 1
RW = 3 * F
NT = -(-N // (P * 8))
BIG = 1.0e30
EPS = 1.0e-5


class It:

    def __init__(self, use, slot):
        self.use, self.slot = use, slot
        self.i = 2 * use + slot

    def ahead(self, d):
        n = self.slot + d
        return It(self.use + n // 2 if n // 2 else self.use, n % 2)


def run_loop(eng, total, body, tail, head=3):
    pairs = (total - head - tail) // 2
    for n in range(head):
        body(It(n // 2, n % 2), tail)
    with eng.Fori(0, pairs) as k:
        body(It(k + head // 2, 1), tail)
        body(It(k + head // 2 + 1, 0), tail)
    for n in range(head + 2 * pairs, total):
        body(It(n // 2, n % 2), min(tail, total - 1 - n))


def edge_view(t):
    return t[0:EP, :].rearrange("(i q p j) f -> i p q (j f)", q=Q, p=P, j=J)


def spread(ap, n):
    return ap.unsqueeze(2).broadcast_to([ap.shape[0], ap.shape[1], n])


def gnn_program(nc, x, src, dst, efeat, w_msg, b_msg, w_attn, b_attn, w1l, b1, w1r, w2l, b2, w2r, out):
    meta = nc.dram_tensor("meta", (NC * P, 3 * J), i32).ap()
    keep_d = nc.dram_tensor("keep_d", (1, EP), f32).ap()
    mask_d = nc.dram_tensor("mask_d", (1, EP), f32).ap()
    maskb_d = nc.dram_tensor("maskb_d", (1, EP), bf16).ap()
    last_edge = nc.dram_tensor("last_edge", (N + EP, 1), i32).ap()
    row_of = nc.dram_tensor("row_of", (EP, 1), i32).ap()
    xs_d = nc.dram_tensor("xs_d", (EP, F), f32).ap()
    h_d = nc.dram_tensor("h_d", (EP, F), f32).ap()
    f_tab = nc.dram_tensor("f_tab", (EP + P, F), f32).ap()
    a_tab = nc.dram_tensor("a_tab", (EP + P, F), f32).ap()
    node_tab = nc.dram_tensor("node_tab", (N + EP, RW), f32).ap()

    meta_v = meta.rearrange("(i q p) f -> i p q f", q=Q, p=P)
    row_v, xs_v, h_v = edge_view(row_of), edge_view(xs_d), edge_view(h_d)
    f_v, a_v = edge_view(f_tab), edge_view(a_tab)

    with ExitStack() as ctx:
        def sb(name, shape, dt=f32):
            return ctx.enter_context(nc.sbuf_tensor(name, shape, dt))

        def sem(name):
            return ctx.enter_context(nc.semaphore(name))

        gate, pool_gate = sem("gate"), sem("pool_gate")
        ident = sb("ident", [P, P])
        neg_ident = sb("neg_ident", [P, P])
        ones_row = sb("ones_row", [1, P], bf16)
        in_sel = sb("in_sel", [HB0 + F, CH])
        out_sum = sb("out_sum", [P, F])
        wa = sb("wa", [EK, CH])
        wm = sb("wm", [EK, CH])
        w1 = sb("w1", [LK, HK])
        w2g = sb("w2g", [HK, F + 1])
        w2n = sb("w2n", [HK, F])

        setup(nc, sem, x, src, dst, meta, keep_d, mask_d, maskb_d, last_edge, f_tab, a_tab,
              w_msg, b_msg, w_attn, b_attn, w1l, b1, w1r, w2l, b2, w2r,
              ident, neg_ident, ones_row, in_sel, out_sum, wa, wm, w1, w2g, w2n)
        edge_softmax(nc, sem, gate, pool_gate, x, efeat, meta_v, xs_v, row_v, f_v, mask_d, maskb_d, last_edge, node_tab,
                     ident, neg_ident, ones_row, in_sel, out_sum, wa, wm)
        first_hop(nc, sem, gate, pool_gate, row_v, xs_v, h_v, a_v, f_tab, keep_d, ident)
        second_hop(nc, sem, gate, pool_gate, row_v, meta_v, h_v, f_v, a_v, a_tab, keep_d, node_tab, ident, w1, w2g)
        node_pass(nc, sem, gate, pool_gate, x, node_tab, out, ident, w1, w2n)


def setup(nc, sem, x, src, dst, meta, keep_d, mask_d, maskb_d, last_edge, f_tab, a_tab,
          w_msg, b_msg, w_attn, b_attn, w1l, b1, w1r, w2l, b2, w2r,
          ident, neg_ident, ones_row, in_sel, out_sum, wa, wm, w1, w2g, w2n):
    full = E // CHUNK
    rest = E - full * CHUNK
    with ExitStack() as ctx:
        def sb(name, shape, dt=f32):
            return ctx.enter_context(nc.sbuf_tensor(name, shape, dt))

        dstn = sb("dstn", [NC, CHUNK + 2], i32)
        srcn = sb("srcn", [NC, CHUNK], i32)
        keep = sb("keep", [NC, CHUNK])
        mask = sb("mask", [NC, CHUNK])
        maskb = sb("maskb", [NC, CHUNK], bf16)
        is_end = sb("is_end", [NC, CHUNK])
        edge_no = sb("edge_no", [NC, CHUNK], i32)
        off = sb("off", [NC, CHUNK])
        metan = sb("metan", [NC, P, 3, J], i32)
        none_row = sb("none_row", [125, N // 125], i32)
        zrow = sb("zrow", [P, F])

        filled, loaded, w_loaded, iotas, selected = (sem(n) for n in ("filled", "loaded", "w_loaded", "iotas", "selected"))
        v_keep, v_end, v_off, v_offn, v_prod, v_row, v_idn, v_out = (
            sem(n) for n in ("v_keep", "v_end", "v_off", "v_offn", "v_prod", "v_row", "v_idn", "v_out"))
        stored = sem("setup_stored")
        ctx.enter_context(nc.allow_non_contiguous_dma(reason="one edge before and after each chunk"))
        with nc.Block() as block:
            @block.sync
            def _(sp):
                sp.wait_ge(filled, 7)
                sp.dma_start(dstn[0:full, 1:CHUNK + 1], dst[0:full * CHUNK].rearrange("(c e) -> c e", e=CHUNK)).then_inc(loaded, 16)
                sp.dma_start(dstn[full:NC, 1:rest + 1], dst[full * CHUNK:E].rearrange("(c e) -> c e", c=1)).then_inc(loaded, 16)
                sp.dma_start(dstn[1:NC, 0:1], dst[CHUNK - 1:CHUNK * (NC - 1):CHUNK].rearrange("(c e) -> c e", e=1)).then_inc(loaded, 16)
                sp.dma_start(dstn[0:NC - 1, CHUNK + 1:CHUNK + 2], dst[CHUNK:CHUNK * (NC - 1) + 1:CHUNK].rearrange("(c e) -> c e", e=1)).then_inc(loaded, 16)
                sp.dma_start(srcn[0:full, :], src[0:full * CHUNK].rearrange("(c e) -> c e", e=CHUNK)).then_inc(loaded, 16)
                sp.dma_start(srcn[full:NC, 0:rest], src[full * CHUNK:E].rearrange("(c e) -> c e", c=1)).then_inc(loaded, 16)
                sp.wait_ge(iotas, 2)
                sp.dma_start(last_edge[0:N, :].rearrange("(p n) o -> p (n o)", p=125), none_row[:, :]).then_inc(stored, 16)
                sp.dma_start(f_tab[EP:EP + P, :], zrow[:, :]).then_inc(stored, 16)
                sp.dma_start(a_tab[EP:EP + P, :], zrow[:, :]).then_inc(stored, 16)
                sp.wait_ge(v_out, 5)
                sp.dma_start(meta.rearrange("(c p) f -> c (p f)", p=P), metan[:, :, :, :].rearrange("c p f j -> c (p f j)")).then_inc(stored, 16)
                sp.dma_start(keep_d.rearrange("o (c e) -> (o c) e", e=CHUNK), keep[:, :]).then_inc(stored, 16)
                sp.dma_start(mask_d.rearrange("o (c e) -> (o c) e", e=CHUNK), mask[:, :]).then_inc(stored, 16)
                sp.dma_start(maskb_d.rearrange("o (c e) -> (o c) e", e=CHUNK), maskb[:, :]).then_inc(stored, 16)
                sp.wait_ge(stored, 16 * 7)

            @block.scalar
            def _(act):
                act.wait_ge(filled, 7)
                loads = [(wa[0:F, :], w_attn), (wa[F:EK, :], b_attn.rearrange("(o c) -> o c", o=1)),
                         (wm[0:F, :], w_msg), (wm[F:EK, :], b_msg.rearrange("(o c) -> o c", o=1)),
                         (w1[0:F, 0:HID], w1r), (w1[F:2 * F, 0:HID], w1l), (w1[2 * F:LK, 0:HID], b1.rearrange("(o c) -> o c", o=1)),
                         (w2g[0:HID, 0:F], w2l), (w2n[0:HID, :], w2r), (w2n[HID:HK, :], b2.rearrange("(o c) -> o c", o=1))]
                for to, frm in loads:
                    act.dma_start(to, frm).then_inc(w_loaded, 16)
                act.wait_ge(w_loaded, 16 * len(loads))

            @block.gpsimd
            def _(pool):
                nc.gpsimd.iota(edge_no[:, :], [[1, CHUNK]], base=0, channel_multiplier=CHUNK).then_inc(iotas, 1)
                nc.gpsimd.iota(none_row[:, :], [[0, N // 125]], base=EP, channel_multiplier=1).then_inc(iotas, 1)
                nc.gpsimd.memset(ident[:, :], 0.0).then_inc(selected, 1)
                pool.wait_ge(selected, 1)
                nc.gpsimd.affine_select(out=ident[:, :], in_=ident[:, :], compare_op=ALU.not_equal, fill=1.0,
                                        base=0, pattern=[[-1, P]], channel_multiplier=1).then_inc(selected, 1)

            @block.vector
            def _(dve):
                nc.vector.memset(dstn[:, :], -2).then_inc(filled, 1)
                nc.vector.memset(srcn[:, :], 0).then_inc(filled, 1)
                nc.vector.memset(w1[:, :], 0.0).then_inc(filled, 1)
                nc.vector.memset(w2g[:, :], 0.0).then_inc(filled, 1)
                dve.wait_ge(filled, 4)
                nc.vector.memset(w1[2 * F:LK, HID:HK], 1.0).then_inc(filled, 1)
                nc.vector.memset(w2g[HID:HK, F:F + 1], 1.0).then_inc(filled, 1)
                nc.vector.memset(zrow[:, :], 0.0).then_inc(filled, 1)
                nc.vector.memset(ones_row[:, :], 1.0)
                dve.wait_ge(loaded, 16 * 6)
                dve.wait_ge(iotas, 2)
                here = dstn[:, 1:CHUNK + 1]
                nc.vector.tensor_tensor(keep[:, :], here, dstn[:, 0:CHUNK], ALU.is_equal).then_inc(v_keep, 1)
                nc.vector.tensor_tensor(is_end[:, :], here, dstn[:, 2:CHUNK + 2], ALU.not_equal).then_inc(v_end, 1)
                nc.vector.tensor_tensor(off[:, :], here, edge_no[:, :], ALU.subtract).then_inc(v_off, 1)
                dve.wait_ge(v_off, 1)
                nc.vector.tensor_scalar(off[:, :], off[:, :], -float(N), None, ALU.add).then_inc(v_offn, 1)
                dve.wait_ge(v_offn, 1)
                dve.wait_ge(v_end, 1)
                nc.vector.tensor_tensor(off[:, :], off[:, :], is_end[:, :], ALU.mult).then_inc(v_prod, 1)
                dve.wait_ge(v_prod, 1)
                nc.vector.tensor_tensor(off[:, :], off[:, :], edge_no[:, :], ALU.add).then_inc(v_row, 1)
                dve.wait_ge(v_row, 1)
                fold = lambda ap: ap.rearrange("c (p j) -> c p j", j=J)
                nc.vector.tensor_scalar(metan[:, :, 1, :], fold(off[:, :]), float(N), None, ALU.add).then_inc(v_out, 1)
                nc.vector.tensor_copy(metan[:, :, 0, :], fold(srcn[:, :])).then_inc(v_out, 1)
                nc.vector.tensor_copy(metan[:, :, 2, :], fold(edge_no[:, :])).then_inc(v_out, 1)
                dve.wait_ge(v_keep, 1)
                nc.vector.tensor_scalar(mask[:, :], keep[:, :], -1.0, BIG, ALU.add, ALU.mult).then_inc(v_out, 1)
                nc.vector.tensor_scalar(maskb[:, :], keep[:, :], -1.0, BIG, ALU.add, ALU.mult).then_inc(v_out, 1)
                dve.wait_ge(selected, 2)
                nc.vector.tensor_scalar(neg_ident[:, :], ident[:, :], -1.0, None, ALU.mult).then_inc(v_idn, 1)
                nc.vector.tensor_reduce(out_sum[:, :], ident[:, :].rearrange("p (i o) -> p o i", o=F), AX.X, ALU.add).then_inc(v_idn, 1)
                nc.vector.tensor_copy(in_sel[HB0:HB0 + F, :].rearrange("k (i o) -> k i o", o=F),
                                      spread(ident[HB0:HB0 + F, HB0:HB0 + F], F)).then_inc(v_idn, 1)


def layernorm_sems(sem, tag):
    return {k: sem(f"{tag}_{k}") for k in ("sum", "mean", "cent", "sq", "sqsum", "var", "ln", "rstd", "h")}


def layernorm_stats(nc, dve, s, n, rows, sm, nm, cc, sq, vs, ve):
    nc.vector.tensor_reduce(sm, rows, AX.X, ALU.add).then_inc(s["sum"], 1)
    dve.wait_ge(s["sum"], n)
    nc.vector.tensor_scalar(nm, sm, -1.0 / F, None, ALU.mult).then_inc(s["mean"], 1)
    dve.wait_ge(s["mean"], n)
    nc.vector.tensor_tensor(cc, rows, spread(nm, F), ALU.add).then_inc(s["cent"], 1)
    dve.wait_ge(s["cent"], n)
    nc.vector.tensor_tensor(sq, cc, cc, ALU.mult).then_inc(s["sq"], 1)
    dve.wait_ge(s["sq"], n)
    nc.vector.tensor_reduce(vs, sq, AX.X, ALU.add).then_inc(s["sqsum"], 1)
    dve.wait_ge(s["sqsum"], n)
    nc.vector.tensor_scalar(ve, vs, 1.0 / F, EPS, ALU.mult, ALU.add).then_inc(s["var"], 1)


def layernorm_rstd(nc, act, s, n, ve, ln, rs):
    act.wait_ge(s["var"], n)
    nc.scalar.activation(ln, ve, ACT.Ln).then_inc(s["ln"], 1)
    act.wait_ge(s["ln"], n)
    nc.scalar.activation(rs, ln, ACT.Exp, scale=-0.5).then_inc(s["rstd"], 1)


def layernorm_out(nc, dve, s, n, h, cc, rs):
    dve.wait_ge(s["rstd"], n)
    nc.vector.scalar_tensor_tensor(h, cc, 0.0, spread(rs, F), ALU.max, ALU.mult).then_inc(s["h"], 1)


def edge_softmax(nc, sem, gate, pool_gate, x, efeat, meta_v, xs_v, row_v, f_v, mask_d, maskb_d, last_edge, node_tab,
                 ident, neg_ident, ones_row, in_sel, out_sum, wa, wm):
    UN = 2 * Q
    ZW = 3200
    ctx = ExitStack()
    with ctx:
        def sb(name, shape, dt=f32):
            return ctx.enter_context(nc.sbuf_tensor(name, shape, dt))

        def ps(name, shape):
            return ctx.enter_context(nc.psum_tensor(name, shape, f32))

        meta_b = sb("meta_b", [P, 2, Q, 3 * J], i32)
        gx = sb("gx", [P, 2, Q, J * F])
        row_b = sb("row_b", [P, 2, Q, J], i32)
        zeros = sb("zeros", [P, ZW])
        xs_b = sb("xs_b", [P, 2, T, F])
        stage = sb("stage", [P, 2, T, HB0 + F])
        mask_b = sb("mask_b", [P, 2, ITE])
        maskb_b = sb("maskb_b", [1, 2, ITE], bf16)
        rows = sb("rows", [HB0 + F, 2, Q, CHUNK])
        sm, nm, vs, ve, lnv, rs = (sb(f"l0_{n}", [P, T]) for n in ("sm", "nm", "vs", "ve", "lnv", "rs"))
        cc, sq = (sb(f"l0_{n}", [P, T, F]) for n in ("cc", "sq"))
        hb = sb("hb", [P, 2, CHUNK])
        e2 = sb("e2", [P, 2, CHUNK])
        r = sb("r", [P, 2, CHUNK])
        a = sb("a", [P, 2, CHUNK])
        m = sb("m", [P, UN, CHUNK + 1])
        s = sb("s", [P, UN, CHUNK])
        n = sb("n", [P, UN, CHUNK])
        rec = sb("rec", [P, 2, CHUNK])
        ratio = sb("ratio", [P, UN, CHUNK])
        f_b = sb("f_b", [P, 2, Q, J * F])

        p_wa = ps("p_wa", [P, CHUNK])
        p_wm = ps("p_wm", [P, CHUNK])
        p_hb = ps("p_hb", [P, CHUNK])
        p_d = ps("p_d", [P, CHUNK])
        p_t = ps("p_t", [HB0 + F, Q, J, P])
        p_fb = ps("p_f", [P, Q, CHUNK])
        p_f = p_fb[:, :, 0:J * F].rearrange("p q (j f) -> p q j f", f=F)

        meta_full, gx_full, xs_stored, pos_done, row_full, row_stored, ef_full, xs_full, mask_full, maskb_full, f_stored = (
            [sem(f"{nm}{k}") for k in range(2)] for nm in
            ("meta_full", "gx_full", "xs_stored", "pos_done", "row_full", "row_stored", "ef_full", "xs_full",
             "mask_full", "maskb_full", "f_stored"))
        zeros_set, zero_stored, cleared = sem("zeros_set"), sem("zero_stored"), sem("cleared")
        ls = layernorm_sems(sem, "l0")
        tr_done, rows_done = sem("tr_done"), sem("rows_done")
        w_ready, hb_done, e2_done, e1_done, m0_done, m_done, q_done, d_ready = (
            sem(f"u_{k}") for k in ("w_ready", "hb_done", "e2_done", "e1_done", "m0_done", "m_done", "q_done", "d_ready"))
        p_done, a_done, r_done, s_done, n_done, rec_done, ratio_done = (
            sem(f"u_{k}") for k in ("p_done", "a_done", "r_done", "s_done", "n_done", "rec_done", "ratio_done"))
        f_sum, f_copied = ([sem(f"{k}{q}") for q in range(Q)] for k in ("f_sum", "f_copied"))

        def unit(it, u):
            return it.i * UN + u + 1

        with nc.Block() as block:
            @block.sync
            def _(sp):
                def load_meta(it):
                    sp.dma_start(meta_b[:, it.slot, :, :], meta_v[it.i]).then_inc(meta_full[it.slot], 16)

                for k in range(2):
                    load_meta(It(0, k))

                def first(it, left):
                    sp.wait_ge(gx_full[it.slot], 16 * T * (it.use + 1))
                    sp.dma_start(xs_v[it.i], gx[:, it.slot, :, :]).then_inc(xs_stored[it.slot], 16)
                    if left >= 2:
                        sp.wait_ge(pos_done[it.slot], 16 * T * (it.use + 1))
                        load_meta(it.ahead(2))
                run_loop(sp, NI, first, 2)
                sp.wait_ge(zeros_set, 1)
                zv = node_tab[0:N, :].rearrange("(p a) f -> p (a f)", p=125)
                for z in range(N * RW // 125 // ZW):
                    sp.dma_start(zv[:, z * ZW:(z + 1) * ZW], zeros[0:125, :]).then_inc(zero_stored, 16)
                for k in range(2):
                    sp.wait_ge(pos_done[k], 16 * T * ((NI + 1 - k) // 2))
                    load_meta(It(0, k))

                def second(it, left):
                    sp.wait_ge(row_full[it.slot], 16 * T * (it.use + 1))
                    sp.dma_start(row_v[it.i], row_b[:, it.slot, :, :]).then_inc(row_stored[it.slot], 16)
                    if left >= 2:
                        load_meta(it.ahead(2))
                run_loop(sp, NI, second, 2)
                for k in range(2):
                    sp.wait_ge(xs_stored[k], 16 * ((NI + 1 - k) // 2))
                    sp.wait_ge(row_stored[k], 16 * ((NI + 1 - k) // 2))
                sp.wait_ge(zero_stored, 16 * (N * RW // 125 // ZW))

            @block.gpsimd
            def _(pool):
                nc.gpsimd.memset(zeros[:, :], 0.0).then_inc(zeros_set, 1)

                def first(it, left):
                    pool.wait_ge(meta_full[it.slot], 16 * (it.use + 1))
                    pool.wait_ge(xs_stored[it.slot], 16 * it.use)
                    pool.sem_inc(pool_gate, 1)
                    for q in range(Q):
                        for j in range(J):
                            pool.indirect_dma_start(gx[:, it.slot, q, j * F:(j + 1) * F], None, x,
                                                    bass.IndirectOffsetOnAxis(ap=meta_b[:, it.slot, q, j:j + 1], axis=0)) \
                                .then_inc(gx_full[it.slot], 16)
                    for q in range(Q):
                        for j in range(J):
                            pool.indirect_dma_start(last_edge, bass.IndirectOffsetOnAxis(ap=meta_b[:, it.slot, q, J + j:J + j + 1], axis=0),
                                                    meta_b[:, it.slot, q, 2 * J + j:2 * J + j + 1], None) \
                                .then_inc(pos_done[it.slot], 16)
                run_loop(pool, NI, first, 2)
                for k in range(2):
                    pool.wait_ge(pos_done[k], 16 * T * ((NI + 1 - k) // 2))

                def second(it, left):
                    pool.wait_ge(meta_full[it.slot], 16 * (it.use + 1 + (NI + 1 - it.slot) // 2))
                    pool.wait_ge(row_stored[it.slot], 16 * it.use)
                    pool.sem_inc(pool_gate, 1)
                    for q in range(Q):
                        for j in range(J):
                            pool.indirect_dma_start(row_b[:, it.slot, q, j:j + 1], None, last_edge,
                                                    bass.IndirectOffsetOnAxis(ap=meta_b[:, it.slot, q, j:j + 1], axis=0)) \
                                .then_inc(row_full[it.slot], 16)
                run_loop(pool, NI, second, 2)

            @block.scalar
            def _(act):
                efv = edge_view_part(efeat)

                def load(it, partial):
                    k = it.slot
                    if partial:
                        lastq = E - (NI - 1) * ITE - CHUNK
                        act.dma_start(stage[:, k, 0:J, 0:F], efeat[E - lastq - CHUNK:E - lastq, :].rearrange("(p j) f -> p j f", j=J)).then_inc(ef_full[k], 16)
                        act.dma_start(stage[0:lastq // J, k, J:T, 0:F], efeat[E - lastq:E, :].rearrange("(p j) f -> p j f", j=J)).then_inc(ef_full[k], 16)
                    else:
                        for q in range(Q):
                            act.dma_start(stage[:, k, q * J:(q + 1) * J, 0:F], efv[it.i][q]).then_inc(ef_full[k], 16)
                    act.wait_ge(xs_stored[k], 16 * (it.use + 1))
                    act.dma_start(xs_b[:, k, :, :].rearrange("p (q j) f -> p q (j f)", q=Q), xs_v[it.i]).then_inc(xs_full[k], 16)
                    act.dma_start(mask_b[:, k, :], row_slice(mask_d, it.i, P)).then_inc(mask_full[k], 16)
                    act.dma_start(maskb_b[:, k, :], row_slice(maskb_d, it.i, 1)).then_inc(maskb_full[k], 16)

                def copy_rows(it):
                    act.wait_ge(tr_done, it.i + 1)
                    for q in range(Q):
                        act.activation(rows[:, it.slot, q, :].rearrange("k (p j) -> k j p", j=J), p_t[:, q, :, :], ACT.Copy).then_inc(rows_done, 1)

                def copy_f(it, q):
                    act.wait_ge(f_sum[q], it.i + 1)
                    if q == 0:
                        act.wait_ge(f_stored[it.slot], 16 * it.use)
                    act.activation(f_b[:, it.slot, q, :], p_f[:, q, :, :].rearrange("p j f -> p (j f)"), ACT.Copy).then_inc(f_copied[q], 1)

                def store_f(it):
                    copy_f(it, 1)
                    act.wait_ge(f_copied[0], it.i + 1)
                    act.wait_ge(f_copied[1], it.i + 1)
                    act.dma_start(f_v[it.i], f_b[:, it.slot, :, :]).then_inc(f_stored[it.slot], 16)

                def exps(it, u):
                    c = unit(it, u)
                    act.wait_ge(w_ready, c)
                    if not (type(it.i) is int and it.i * UN + u < 2):
                        act.wait_ge(e1_done, c - 2)
                    act.activation(hb[:, u % 2, :], p_hb[:, :], ACT.Copy).then_inc(hb_done, 1)
                    act.wait_ge(q_done, c)
                    act.activation(e2[:, u % 2, :], e2[:, u % 2, :], ACT.Exp).then_inc(p_done, 1)
                    act.wait_ge(d_ready, c)
                    if not (type(it.i) is int and it.i * UN + u < 2):
                        act.wait_ge(n_done, c - 2)
                    act.activation(a[:, u % 2, :], p_d[:, :], ACT.Exp).then_inc(a_done, 1)

                act.wait_ge(cleared, 5)
                load(It(0, 0), False)
                load(It(0, 1), False)
                layernorm_rstd(nc, act, ls, 1, ve[:, :], lnv[:, :], rs[:, :])
                copy_rows(It(0, 0))

                def body(it, left):
                    nxt = it.ahead(1)
                    exps(it, 0)
                    if left:
                        layernorm_rstd(nc, act, ls, nxt.i + 1, ve[:, :], lnv[:, :], rs[:, :])
                    exps(it, 1)
                    if left:
                        copy_rows(nxt)
                    if not (type(it.i) is int and it.i == 0):
                        store_f(it.ahead(-1))
                    exps(it, 2)
                    exps(it, 3)
                    copy_f(it, 0)
                    if left >= 2:
                        load(it.ahead(2), left == 2 and type(it.i) is int and it.i == NI - 3)
                run_loop(act, NI, body, 3)
                end = It((NI - 1) // 2, (NI - 1) % 2)
                store_f(end)
                for k in range(2):
                    act.wait_ge(f_stored[k], 16 * ((NI + 1 - k) // 2))

            @block.tensor
            def _(pe):
                def transposes(it):
                    pe.wait_ge(ls["h"], it.i + 1)
                    extra = 16 if type(it.i) is int and it.i == NI - 1 else 0
                    pe.wait_ge(ef_full[it.slot], 32 * (it.use + 1))
                    if not (type(it.i) is int and it.i == 0):
                        pe.wait_ge(rows_done, Q * it.i)
                    pe.sem_inc(gate, 1)
                    for t in range(T):
                        last = nc.tensor.transpose(p_t[:, t // J, t % J, :], stage[:, it.slot, t, :], ident[:, :])
                    last.then_inc(tr_done, 1)

                def products(it, u):
                    c = unit(it, u)
                    q, half = u // 2, u % 2
                    if u == 0:
                        pe.wait_ge(rows_done, Q * (it.i + 1))
                    if not (type(it.i) is int and it.i == 0 and u == 0):
                        pe.wait_ge(e1_done, c - 1)
                        pe.wait_ge(e2_done, c - 1)
                        pe.wait_ge(hb_done, c - 1)
                    pe.sem_inc(gate, 1)
                    cols = slice(half * P, (half + 1) * P)
                    nc.tensor.matmul(p_hb[:, :], in_sel[HB0:HB0 + F, cols], rows[HB0:HB0 + F, it.slot, q, :], start=True, stop=True)
                    nc.tensor.matmul(p_wa[:, :], wa[:, cols], rows[0:EK, it.slot, q, :], start=True, stop=True)
                    nc.tensor.matmul(p_wm[:, :], wm[:, cols], rows[0:EK, it.slot, q, :], start=True, stop=True).then_inc(w_ready, 1)

                def steps(it, u):
                    c = unit(it, u)
                    pe.wait_ge(m_done, c)
                    pe.wait_ge(m0_done, c)
                    if u == 0:
                        pe.wait_ge(maskb_full[it.slot], 16 * (it.use + 1))
                    if not (type(it.i) is int and it.i == 0 and u == 0):
                        pe.wait_ge(a_done, c - 1)
                    pe.sem_inc(gate, 1)
                    q = u // 2
                    nc.tensor.matmul(p_d[:, :], ones_row[:, :], maskb_b[:, it.slot, q * CHUNK:(q + 1) * CHUNK], start=True, stop=False)
                    nc.tensor.matmul(p_d[:, :], ident[:, :], m[:, u, 0:CHUNK], start=False, stop=False)
                    nc.tensor.matmul(p_d[:, :], neg_ident[:, :], m[:, u, 1:CHUNK + 1], start=False, stop=True).then_inc(d_ready, 1)

                def sums(it, q):
                    pe.wait_ge(ratio_done, unit(it, 2 * q + 1))
                    if not (type(it.i) is int and it.i == 0):
                        pe.wait_ge(f_copied[q], it.i)
                    pe.sem_inc(gate, 1)
                    for j in range(J):
                        for half in range(2):
                            last = nc.tensor.matmul(p_f[:, q, j, :], ratio[:, 2 * q + half, j:CHUNK:J], out_sum[:, :],
                                                    start=(half == 0), stop=(half == 1))
                    last.then_inc(f_sum[q], 1)

                transposes(It(0, 0))

                def body(it, left):
                    products(it, 0)
                    steps(it, 0)
                    products(it, 1)
                    if not (type(it.i) is int and it.i == 0):
                        sums(it.ahead(-1), 1)
                    steps(it, 1)
                    if left:
                        transposes(it.ahead(1))
                    products(it, 2)
                    steps(it, 2)
                    products(it, 3)
                    sums(it, 0)
                    steps(it, 3)
                run_loop(pe, NI, body, 3)
                sums(It((NI - 1) // 2, (NI - 1) % 2), 1)

            @block.vector
            def _(dve):
                nc.vector.memset(stage[:, :, :, :], 0.0).then_inc(cleared, 1)
                dve.wait_ge(cleared, 1)
                nc.vector.memset(stage[:, :, :, F:EK], 1.0).then_inc(cleared, 1)
                nc.vector.memset(m[:, :, :], 0.0).then_inc(cleared, 1)
                nc.vector.memset(s[:, :, :], 0.0).then_inc(cleared, 1)
                nc.vector.memset(n[:, :, :], 0.0).then_inc(cleared, 1)
                dve.wait_ge(cleared, 5)

                def front(it, u):
                    c = unit(it, u)
                    k, half, q = u % 2, u % 2, u // 2
                    before = (u + 2) % UN
                    first = type(it.i) is int and it.i == 0
                    if not (first and u < 2):
                        dve.wait_ge(m_done, c - 2)
                        dve.wait_ge(d_ready, c - 2)
                        dve.wait_ge(r_done, c - 2)
                        dve.wait_ge(n_done, c - 2)
                    nc.vector.tensor_copy(m[:, u, 0:1], m[:, before, CHUNK:CHUNK + 1]).then_inc(m0_done, 1)
                    dve.wait_ge(hb_done, c)
                    nc.vector.tensor_tensor(e2[:, k, :], p_wa[:, :], hb[:, k, :], ALU.mult).then_inc(e2_done, 1)
                    nc.vector.tensor_tensor(r[:, k, :], p_wm[:, :], hb[:, k, :], ALU.mult).then_inc(e1_done, 1)
                    if u == 0:
                        dve.wait_ge(mask_full[it.slot], 16 * (it.use + 1))
                    dve.wait_ge(m0_done, c)
                    dve.wait_ge(e2_done, c)
                    nc.vector.tensor_tensor_scan(m[:, u, 1:CHUNK + 1], mask_b[:, it.slot, q * CHUNK:(q + 1) * CHUNK], e2[:, k, :],
                                                 m[:, u, 0:1], ALU.add, ALU.max).then_inc(m_done, 1)
                    dve.wait_ge(m_done, c)
                    nc.vector.tensor_tensor(e2[:, k, :], e2[:, k, :], m[:, u, 1:CHUNK + 1], ALU.subtract).then_inc(q_done, 1)

                def back(it, u):
                    c = unit(it, u)
                    k = u % 2
                    before = (u + 2) % UN
                    first = type(it.i) is int and it.i == 0
                    dve.wait_ge(p_done, c)
                    dve.wait_ge(e1_done, c)
                    nc.vector.tensor_tensor(r[:, k, :], r[:, k, :], e2[:, k, :], ALU.mult).then_inc(r_done, 1)
                    dve.wait_ge(a_done, c)
                    if not (first and u < 2):
                        dve.wait_ge(s_done, c - 2)
                    nc.vector.tensor_tensor_scan(s[:, u, :], a[:, k, :], e2[:, k, :], s[:, before, CHUNK - 1:CHUNK], ALU.mult, ALU.add).then_inc(s_done, 1)
                    dve.wait_ge(r_done, c)
                    nc.vector.tensor_tensor_scan(n[:, u, :], a[:, k, :], r[:, k, :], n[:, before, CHUNK - 1:CHUNK], ALU.mult, ALU.add).then_inc(n_done, 1)
                    dve.wait_ge(s_done, c)
                    nc.vector.reciprocal(rec[:, k, :], s[:, u, :]).then_inc(rec_done, 1)
                    if not first:
                        dve.wait_ge(f_sum[u // 2], it.i)
                    dve.wait_ge(rec_done, c)
                    dve.wait_ge(n_done, c)
                    nc.vector.tensor_tensor(ratio[:, u, :], n[:, u, :], rec[:, k, :], ALU.mult).then_inc(ratio_done, 1)

                def stats(it):
                    dve.wait_ge(xs_full[it.slot], 16 * (it.use + 1))
                    if not (type(it.i) is int and it.i == 0):
                        dve.wait_ge(ls["h"], it.i)
                    layernorm_stats(nc, dve, ls, it.i + 1, xs_b[:, it.slot, :, :], sm[:, :], nm[:, :], cc[:, :, :], sq[:, :, :], vs[:, :], ve[:, :])

                def normed(it):
                    layernorm_out(nc, dve, ls, it.i + 1, stage[:, it.slot, :, HB0:HB0 + F], cc[:, :, :], rs[:, :])

                stats(It(0, 0))
                normed(It(0, 0))

                def body(it, left):
                    nxt = it.ahead(1)
                    front(it, 0)
                    if left:
                        stats(nxt)
                    if not (type(it.i) is int and it.i == 0):
                        back(it.ahead(-1), 3)
                    front(it, 1)
                    if left:
                        normed(nxt)
                    back(it, 0)
                    front(it, 2)
                    back(it, 1)
                    front(it, 3)
                    back(it, 2)
                run_loop(dve, NI, body, 3)
                back(It((NI - 1) // 2, (NI - 1) % 2), 3)


def edge_view_part(t):
    whole = E // ITE
    return Chunks(t[0:whole * ITE, :].rearrange("(i q p j) f -> i q p j f", q=Q, p=P, j=J))


class Chunks:
    def __init__(self, view):
        self.view = view

    def __getitem__(self, i):
        return [self.view[i, q] for q in range(Q)]


def row_slice(row, i, parts):
    one = row.rearrange("o (i e) -> (o i) e", e=ITE)[i].rearrange("(o e) -> o e", o=1)
    return one.broadcast_to([parts, ITE])


def first_hop(nc, sem, gate, pool_gate, row_v, xs_v, h_v, a_v, f_tab, keep_d, ident):
    ctx = ExitStack()
    with ctx:
        def sb(name, shape, dt=f32):
            return ctx.enter_context(nc.sbuf_tensor(name, shape, dt))

        row_b = sb("h1_row", [P, 2, Q, J], i32)
        g = sb("h1_g", [P, 2, T, F])
        xs_b = sb("h1_xs", [P, 2, T, F])
        keep_b = sb("h1_keep", [EK, 2, ITE])
        x1 = sb("h1_x1", [P, 2, T, F])
        h_b = sb("h1_h", [P, 2, T, EK])
        sm, nm, vs, ve, lnv, rs = (sb(f"h1_{n}", [P, T]) for n in ("sm", "nm", "vs", "ve", "lnv", "rs"))
        cc, sq = (sb(f"h1_{n}", [P, T, F]) for n in ("cc", "sq"))
        rows = sb("h1_rows", [EK, 2, ITE])
        acc = sb("h1_acc", [EK, 2, ITE])
        rc = sb("h1_rc", [P, T])
        mean = sb("h1_mean", [P, 2, T, F])
        p_t = ctx.enter_context(nc.psum_tensor("h1_pt", [EK, Q, J, P], f32))
        p_b = ctx.enter_context(nc.psum_tensor("h1_pb", [P, T, EK], f32))

        row_full, g_full, xs_full, keep_full, h_stored, mean_stored = (
            [sem(f"h1_{n}{k}") for k in range(2)] for n in ("row_full", "g_full", "xs_full", "keep_full", "h_stored", "mean_stored"))
        ls = layernorm_sems(sem, "h1")
        cleared, x1_done, tr_done, rows_done, acc_done, bk_done, rc_done, mean_done = (
            sem(f"h1_{n}") for n in ("cleared", "x1_done", "tr_done", "rows_done", "acc_done", "bk_done", "rc_done", "mean_done"))

        h_v2 = Chunks(h_d_view(h_v))
        with nc.Block() as block:
            @block.sync
            def _(sp):
                def load(it):
                    k = it.slot
                    sp.dma_start(row_b[:, k, :, :], row_v[it.i]).then_inc(row_full[k], 16)
                    sp.dma_start(xs_b[:, k, :, :].rearrange("p (q j) f -> p q (j f)", q=Q), xs_v[it.i]).then_inc(xs_full[k], 16)
                    sp.dma_start(keep_b[:, k, :], row_slice(keep_d, it.i, EK)).then_inc(keep_full[k], 16)
                load(It(0, 0))
                load(It(0, 1))

                def body(it, left):
                    sp.wait_ge(ls["h"], it.i + 1)
                    sp.dma_start(h_v2[it.i][0], h_b[:, it.slot, 0:J, 0:F]).then_inc(h_stored[it.slot], 16)
                    sp.dma_start(h_v2[it.i][1], h_b[:, it.slot, J:T, 0:F]).then_inc(h_stored[it.slot], 16)
                    sp.wait_ge(mean_done, it.i + 1)
                    sp.dma_start(a_v[it.i], mean[:, it.slot, :, :].rearrange("p (q j) f -> p q (j f)", q=Q)).then_inc(mean_stored[it.slot], 16)
                    if left >= 2:
                        sp.wait_ge(g_full[it.slot], 16 * T * (it.use + 1))
                        sp.wait_ge(x1_done, it.i + 1)
                        load(it.ahead(2))
                run_loop(sp, NI, body, 2)
                for k in range(2):
                    sp.wait_ge(h_stored[k], 32 * ((NI + 1 - k) // 2))
                    sp.wait_ge(mean_stored[k], 16 * ((NI + 1 - k) // 2))


            @block.gpsimd
            def _(pool):
                def body(it, left):
                    pool.wait_ge(row_full[it.slot], 16 * (it.use + 1))
                    if not (type(it.i) is int and it.i < 2):
                        pool.wait_ge(x1_done, it.i - 1)
                    pool.sem_inc(pool_gate, 1)
                    for t in range(T):
                        pool.indirect_dma_start(g[:, it.slot, t, :], None, f_tab,
                                                bass.IndirectOffsetOnAxis(ap=row_b[:, it.slot, t // J, t % J:t % J + 1], axis=0)) \
                            .then_inc(g_full[it.slot], 16)
                run_loop(pool, NI, body, 2)

            @block.scalar
            def _(act):
                def body(it, left):
                    layernorm_rstd(nc, act, ls, it.i + 1, ve[:, :], lnv[:, :], rs[:, :])
                    act.wait_ge(tr_done, it.i + 1)
                    if not (type(it.i) is int and it.i < 2):
                        act.wait_ge(acc_done, it.i - 1)
                    for q in range(Q):
                        act.activation(rows[:, it.slot, q * CHUNK:(q + 1) * CHUNK].rearrange("k (p j) -> k j p", j=J), p_t[:, q, :, :], ACT.Copy) \
                            .then_inc(rows_done, 1)
                run_loop(act, NI, body, 2)

            @block.tensor
            def _(pe):
                def forth(it):
                    pe.wait_ge(ls["h"], it.i + 1)
                    if not (type(it.i) is int and it.i == 0):
                        pe.wait_ge(rows_done, Q * it.i)
                    pe.sem_inc(gate, 1)
                    for t in range(T):
                        last = nc.tensor.transpose(p_t[:, t // J, t % J, :], h_b[:, it.slot, t, :], ident[:, :])
                    last.then_inc(tr_done, 1)

                def back(it):
                    pe.wait_ge(acc_done, it.i + 1)
                    if not (type(it.i) is int and it.i == 0):
                        pe.wait_ge(mean_done, it.i)
                    pe.sem_inc(gate, 1)
                    for t in range(T):
                        q, j = t // J, t % J
                        last = nc.tensor.transpose(p_b[:, t, :], acc[:, it.slot, q * CHUNK + j:(q + 1) * CHUNK:J], ident[0:EK, 0:EK])
                    last.then_inc(bk_done, 1)

                def body(it, left):
                    forth(it)
                    if not (type(it.i) is int and it.i == 0):
                        back(it.ahead(-1))
                run_loop(pe, NI, body, 2)
                back(It((NI - 1) // 2, (NI - 1) % 2))

            @block.vector
            def _(dve):
                nc.vector.memset(acc[:, :, :], 0.0).then_inc(cleared, 1)
                nc.vector.memset(h_b[:, :, :, F:EK], 1.0).then_inc(cleared, 1)
                dve.wait_ge(cleared, 2)

                def norm(it):
                    c = it.i + 1
                    first = type(it.i) is int and it.i == 0
                    dve.wait_ge(g_full[it.slot], 16 * T * (it.use + 1))
                    dve.wait_ge(xs_full[it.slot], 16 * (it.use + 1))
                    nc.vector.tensor_tensor(x1[:, it.slot, :, :], g[:, it.slot, :, :], xs_b[:, it.slot, :, :], ALU.add).then_inc(x1_done, 1)
                    dve.wait_ge(x1_done, c)
                    if not first:
                        dve.wait_ge(ls["h"], it.i)
                    layernorm_stats(nc, dve, ls, c, x1[:, it.slot, :, :], sm[:, :], nm[:, :], cc[:, :, :], sq[:, :, :], vs[:, :], ve[:, :])

                def normed(it):
                    dve.wait_ge(h_stored[it.slot], 32 * it.use)
                    if not (type(it.i) is int and it.i < 2):
                        dve.wait_ge(tr_done, it.i - 1)
                    layernorm_out(nc, dve, ls, it.i + 1, h_b[:, it.slot, :, 0:F], cc[:, :, :], rs[:, :])

                def scan(it):
                    c = it.i + 1
                    dve.wait_ge(rows_done, Q * c)
                    dve.wait_ge(keep_full[it.slot], 16 * (it.use + 1))
                    if not (type(it.i) is int and it.i < 2):
                        dve.wait_ge(bk_done, it.i - 1)
                    if not (type(it.i) is int and it.i == 0):
                        dve.wait_ge(acc_done, it.i)
                    nc.vector.tensor_tensor_scan(acc[:, it.slot, :], keep_b[:, it.slot, :], rows[:, it.slot, :],
                                                 acc[:, 1 - it.slot, ITE - 1:ITE], ALU.mult, ALU.add).then_inc(acc_done, 1)

                def means(it):
                    c = it.i + 1
                    dve.wait_ge(bk_done, c)
                    if not (type(it.i) is int and it.i == 0):
                        dve.wait_ge(mean_done, it.i)
                    nc.vector.reciprocal(rc[:, :].unsqueeze(2), p_b[:, :, F:EK]).then_inc(rc_done, 1)
                    dve.wait_ge(rc_done, c)
                    dve.wait_ge(mean_stored[it.slot], 16 * it.use)
                    nc.vector.tensor_tensor(mean[:, it.slot, :, :], p_b[:, :, 0:F], spread(rc[:, :], F), ALU.mult).then_inc(mean_done, 1)

                def body(it, left):
                    norm(it)
                    if not (type(it.i) is int and it.i == 0):
                        scan(it.ahead(-1))
                    normed(it)
                    if not (type(it.i) is int and it.i == 0):
                        means(it.ahead(-1))
                run_loop(dve, NI, body, 2)
                end = It((NI - 1) // 2, (NI - 1) % 2)
                scan(end)
                means(end)


def h_d_view(h_v):
    return h_v.rearrange("i p q (j f) -> i q p j f", f=F)


def second_hop(nc, sem, gate, pool_gate, row_v, meta_v, h_v, f_v, a_v, a_tab, keep_d, node_tab, ident, w1, w2g):
    ctx = ExitStack()
    with ctx:
        def sb(name, shape, dt=f32):
            return ctx.enter_context(nc.sbuf_tensor(name, shape, dt))

        def ps(name, shape):
            return ctx.enter_context(nc.psum_tensor(name, shape, f32))

        row_b = sb("h2_row", [P, 2, Q, J], i32)
        meta_b = sb("h2_meta", [P, 2, Q, 3 * J], i32)
        stage = sb("h2_stage", [P, 2, T, LK])
        keep_b = sb("h2_keep", [EK, 2, ITE])
        node_b = sb("h2_node", [P, 2, T, RW])
        rows = sb("h2_rows", [LK, Q, CHUNK])
        hid = sb("h2_hid", [HK, Q, CHUNK])
        acc = sb("h2_acc", [EK, 2, ITE])
        rc = sb("h2_rc", [P, T])
        p_t = ps("h2_pt", [LK, Q, J, P])
        p_h = ps("h2_ph", [HK, Q, CHUNK])
        p_g = ps("h2_pg", [EK, Q, CHUNK])
        p_b = ps("h2_pb", [P, T, EK])

        row_full, meta_full, h_full, g_full, keep_full, node_full, sent = (
            [sem(f"h2_{n}{k}") for k in range(2)] for n in ("row_full", "meta_full", "h_full", "g_full", "keep_full", "node_full", "sent"))
        cleared, tr_done, rows_done, hid_ready, hid_done, g_ready, acc_done, bk_done, rc_done, mean_done = (
            sem(f"h2_{n}") for n in ("cleared", "tr_done", "rows_done", "hid_ready", "hid_done", "g_ready", "acc_done", "bk_done",
                                     "rc_done", "mean_done"))
        uses = [(NI + 1) // 2, NI // 2]
        hc, fc, ac = Chunks(h_d_view(h_v)), Chunks(h_d_view(f_v)), Chunks(h_d_view(a_v))

        with nc.Block() as block:
            @block.sync
            def _(sp):
                def load_in(it):
                    k = it.slot
                    sp.dma_start(row_b[:, k, :, :], row_v[it.i]).then_inc(row_full[k], 16)
                    for q in range(Q):
                        sp.dma_start(stage[:, k, q * J:(q + 1) * J, 0:F], hc[it.i][q]).then_inc(h_full[k], 16)
                    sp.dma_start(keep_b[:, k, :], row_slice(keep_d, it.i, EK)).then_inc(keep_full[k], 16)

                def load_out(it):
                    k = it.slot
                    sp.dma_start(meta_b[:, k, :, :], meta_v[it.i]).then_inc(meta_full[k], 16)
                    for q in range(Q):
                        sp.dma_start(node_b[:, k, q * J:(q + 1) * J, 0:F], fc[it.i][q]).then_inc(node_full[k], 16)
                        sp.dma_start(node_b[:, k, q * J:(q + 1) * J, F:2 * F], ac[it.i][q]).then_inc(node_full[k], 16)
                for k in range(2):
                    load_in(It(0, k))
                    load_out(It(0, k))

                def body(it, left):
                    if left >= 2:
                        sp.wait_ge(g_full[it.slot], 16 * T * (it.use + 1))
                        sp.wait_ge(tr_done, it.i + 1)
                        sp.wait_ge(acc_done, it.i + 1)
                        load_in(it.ahead(2))
                        sp.wait_ge(sent[it.slot], 16 * T * (it.use + 1))
                        load_out(it.ahead(2))
                run_loop(sp, NI, body, 2)

            @block.gpsimd
            def _(pool):
                def gather(it):
                    k = it.slot
                    pool.wait_ge(row_full[k], 16 * (it.use + 1))
                    if not (type(it.i) is int and it.i < 2):
                        pool.wait_ge(tr_done, it.i - 1)
                    pool.sem_inc(pool_gate, 1)
                    for t in range(T):
                        pool.indirect_dma_start(stage[:, k, t, F:2 * F], None, a_tab,
                                                bass.IndirectOffsetOnAxis(ap=row_b[:, k, t // J, t % J:t % J + 1], axis=0)) \
                            .then_inc(g_full[k], 16)

                def scatter(it):
                    k = it.slot
                    pool.wait_ge(meta_full[k], 16 * (it.use + 1))
                    pool.wait_ge(node_full[k], 64 * (it.use + 1))
                    pool.wait_ge(mean_done, it.i + 1)
                    pool.sem_inc(pool_gate, 1)
                    for t in range(T):
                        pool.indirect_dma_start(node_tab, bass.IndirectOffsetOnAxis(ap=meta_b[:, k, t // J, J + t % J:J + t % J + 1], axis=0),
                                                node_b[:, k, t, :], None).then_inc(sent[k], 16)

                def body(it, left):
                    gather(it)
                    if not (type(it.i) is int and it.i == 0):
                        scatter(it.ahead(-1))
                pool.wait_ge(cleared, 2)
                run_loop(pool, NI, body, 2)
                scatter(It((NI - 1) // 2, (NI - 1) % 2))
                for k in range(2):
                    pool.wait_ge(sent[k], 16 * T * uses[k])

            @block.scalar
            def _(act):
                def body(it, left):
                    c = it.i + 1
                    first = type(it.i) is int and it.i == 0
                    act.wait_ge(tr_done, c)
                    if not first:
                        act.wait_ge(hid_ready, it.i)
                    for q in range(Q):
                        act.activation(rows[:, q, :].rearrange("k (p j) -> k j p", j=J), p_t[:, q, :, :], ACT.Copy).then_inc(rows_done, 1)
                    act.wait_ge(hid_ready, c)
                    if not first:
                        act.wait_ge(g_ready, it.i)
                    act.activation(hid[:, :, :], p_h[:, :, :], ACT.Relu).then_inc(hid_done, 1)
                run_loop(act, NI, body, 2)

            @block.tensor
            def _(pe):
                def forth(it):
                    c = it.i + 1
                    first = type(it.i) is int and it.i == 0
                    pe.wait_ge(g_full[it.slot], 16 * T * (it.use + 1))
                    pe.wait_ge(h_full[it.slot], 32 * (it.use + 1))
                    if not first:
                        pe.wait_ge(rows_done, Q * it.i)
                    pe.sem_inc(gate, 1)
                    for t in range(T):
                        last = nc.tensor.transpose(p_t[:, t // J, t % J, :], stage[:, it.slot, t, :], ident[:, :])
                    last.then_inc(tr_done, 1)
                    pe.wait_ge(rows_done, Q * c)
                    if not first:
                        pe.wait_ge(hid_done, it.i)
                    pe.sem_inc(gate, 1)
                    for q in range(Q):
                        last = nc.tensor.matmul(p_h[:, q, :], w1[:, :], rows[:, q, :], start=True, stop=True)
                    last.then_inc(hid_ready, 1)
                    pe.wait_ge(hid_done, c)
                    if not first:
                        pe.wait_ge(acc_done, it.i)
                    pe.sem_inc(gate, 1)
                    for q in range(Q):
                        last = nc.tensor.matmul(p_g[:, q, :], w2g[:, :], hid[:, q, :], start=True, stop=True)
                    last.then_inc(g_ready, 1)

                def back(it):
                    pe.wait_ge(acc_done, it.i + 1)
                    if not (type(it.i) is int and it.i == 0):
                        pe.wait_ge(mean_done, it.i)
                    pe.sem_inc(gate, 1)
                    for t in range(T):
                        q, j = t // J, t % J
                        last = nc.tensor.transpose(p_b[:, t, :], acc[:, it.slot, q * CHUNK + j:(q + 1) * CHUNK:J], ident[0:EK, 0:EK])
                    last.then_inc(bk_done, 1)

                pe.wait_ge(cleared, 2)

                def body(it, left):
                    forth(it)
                    back(it)
                run_loop(pe, NI, body, 2)

            @block.vector
            def _(dve):
                nc.vector.memset(acc[:, :, :], 0.0).then_inc(cleared, 1)
                nc.vector.memset(stage[:, :, :, 2 * F:LK], 1.0).then_inc(cleared, 1)
                dve.wait_ge(cleared, 2)

                def body(it, left):
                    c = it.i + 1
                    first = type(it.i) is int and it.i == 0
                    dve.wait_ge(g_ready, c)
                    dve.wait_ge(keep_full[it.slot], 16 * (it.use + 1))
                    if not first:
                        dve.wait_ge(acc_done, it.i)
                    nc.vector.tensor_tensor_scan(acc[:, it.slot, :], keep_b[:, it.slot, :], p_g[:, :, :].rearrange("k q e -> k (q e)"),
                                                 acc[:, 1 - it.slot, ITE - 1:ITE], ALU.mult, ALU.add).then_inc(acc_done, 1)
                    dve.wait_ge(bk_done, c)
                    nc.vector.reciprocal(rc[:, :].unsqueeze(2), p_b[:, :, F:EK]).then_inc(rc_done, 1)
                    dve.wait_ge(rc_done, c)
                    dve.wait_ge(sent[it.slot], 16 * T * it.use)
                    nc.vector.tensor_tensor(node_b[:, it.slot, :, 2 * F:RW], p_b[:, :, 0:F], spread(rc[:, :], F), ALU.mult).then_inc(mean_done, 1)
                run_loop(dve, NI, body, 2)


def node_pass(nc, sem, gate, pool_gate, x, node_tab, out, ident, w1, w2n):
    K = 8
    whole = N // (P * K)
    rest = (N - whole * P * K) // K
    xv = x[0:whole * P * K, :].rearrange("(i p k) f -> i p (k f)", p=P, k=K)
    ov = out[0:whole * P * K, :].rearrange("(i p k) f -> i p (k f)", p=P, k=K)
    nv = node_tab[0:whole * P * K, :].rearrange("(i p k) f -> i p (k f)", p=P, k=K)
    tail_of = lambda t: t[whole * P * K:N, :].rearrange("(p k) f -> p (k f)", k=K)
    ctx = ExitStack()
    with ctx:
        def sb(name, shape, dt=f32):
            return ctx.enter_context(nc.sbuf_tensor(name, shape, dt))

        def ps(name, shape):
            return ctx.enter_context(nc.psum_tensor(name, shape, f32))

        x_b = sb("n_x", [P, 2, K, F])
        t_b = sb("n_t", [P, 2, K, RW])
        x1 = sb("n_x1", [P, 2, K, F])
        x2 = sb("n_x2", [P, 2, K, F])
        stage = sb("n_stage", [P, 2, K, LK])
        sm, nm, vs, ve, lnv, rs = (sb(f"n_{n}", [P, K]) for n in ("sm", "nm", "vs", "ve", "lnv", "rs"))
        cc, sq = (sb(f"n_{n}", [P, K, F]) for n in ("cc", "sq"))
        rows = sb("n_rows", [LK, 2, K * P])
        hid = sb("n_hid", [HK, 2, K * P])
        o_b = sb("n_o", [P, 2, K, F])
        p_t = ps("n_pt", [LK, K * P])
        p_h = ps("n_ph", [HK, K * P])
        p_o = ps("n_po", [P, K, F])

        x_full, t_full, stored = ([sem(f"n_{n}{k}") for k in range(2)] for n in ("x_full", "t_full", "stored"))
        ls = layernorm_sems(sem, "n")
        cleared, x1_done, x2_done, mean_done, tr_done, rows_done, hid_ready, hid_done, o_ready, o_done = (
            sem(f"n_{n}") for n in ("cleared", "x1_done", "x2_done", "mean_done", "tr_done", "rows_done", "hid_ready", "hid_done", "o_ready", "o_done"))
        uses = [(NT + 1) // 2, NT // 2]

        def is_last(it):
            return type(it.i) is int and it.i == NT - 1

        with nc.Block() as block:
            @block.sync
            def _(sp):
                def load(it):
                    k = it.slot
                    if is_last(it):
                        sp.dma_start(x_b[0:rest, k, :, :].rearrange("p k f -> p (k f)"), tail_of(x)).then_inc(x_full[k], 16)
                        sp.dma_start(t_b[0:rest, k, :, :].rearrange("p k f -> p (k f)"), tail_of(node_tab)).then_inc(t_full[k], 16)
                    else:
                        sp.dma_start(x_b[:, k, :, :].rearrange("p k f -> p (k f)"), xv[it.i]).then_inc(x_full[k], 16)
                        sp.dma_start(t_b[:, k, :, :].rearrange("p k f -> p (k f)"), nv[it.i]).then_inc(t_full[k], 16)
                load(It(0, 0))
                load(It(0, 1))

                def body(it, left):
                    if left >= 2:
                        sp.wait_ge(x2_done, it.i + 1)
                        sp.wait_ge(mean_done, it.i + 1)
                        load(it.ahead(2))
                run_loop(sp, NT, body, 3)

            @block.scalar
            def _(act):
                def tops(it):
                    c = it.i + 1
                    layernorm_rstd(nc, act, ls, c, ve[:, :], lnv[:, :], rs[:, :])
                    act.wait_ge(tr_done, c)
                    if not (type(it.i) is int and it.i < 2):
                        act.wait_ge(hid_ready, it.i - 1)
                    act.activation(rows[:, it.slot, :], p_t[:, :], ACT.Copy).then_inc(rows_done, 1)
                    act.wait_ge(hid_ready, c)
                    if not (type(it.i) is int and it.i < 2):
                        act.wait_ge(o_ready, it.i - 1)
                    act.activation(hid[:, it.slot, :], p_h[:, :], ACT.Relu).then_inc(hid_done, 1)

                def store(it):
                    act.wait_ge(o_done, it.i + 1)
                    k = it.slot
                    if is_last(it):
                        act.dma_start(tail_of(out), o_b[0:rest, k, :, :].rearrange("p k f -> p (k f)")).then_inc(stored[k], 16)
                    else:
                        act.dma_start(ov[it.i], o_b[:, k, :, :].rearrange("p k f -> p (k f)")).then_inc(stored[k], 16)

                def body(it, left):
                    tops(it)
                    if not (type(it.i) is int and it.i == 0):
                        store(it.ahead(-1))
                run_loop(act, NT, body, 3)
                store(It((NT - 1) // 2, (NT - 1) % 2))
                for k in range(2):
                    act.wait_ge(stored[k], 16 * uses[k])

            @block.gpsimd
            def _(pool):
                def body(it, left):
                    c = it.i + 1
                    k = it.slot
                    pool.wait_ge(t_full[k], 16 * (it.use + 1))
                    if not (type(it.i) is int and it.i < 2):
                        pool.wait_ge(tr_done, it.i - 1)
                        pool.wait_ge(o_done, it.i - 1)
                    pool.sem_inc(pool_gate, 1)
                    nc.gpsimd.tensor_copy(stage[:, k, :, F:2 * F], t_b[:, k, :, F:2 * F]).then_inc(mean_done, 1)
                    pool.wait_ge(x1_done, c)
                    pool.sem_inc(pool_gate, 1)
                    nc.gpsimd.tensor_tensor(x2[:, k, :, :], x1[:, k, :, :], t_b[:, k, :, 2 * F:RW], ALU.add).then_inc(x2_done, 1)
                run_loop(pool, NT, body, 3)

            @block.tensor
            def _(pe):
                pe.wait_ge(cleared, 1)

                def hidden(it):
                    c = it.i + 1
                    first = type(it.i) is int and it.i == 0
                    pe.wait_ge(ls["h"], c)
                    pe.wait_ge(mean_done, c)
                    if not first:
                        pe.wait_ge(rows_done, it.i)
                    pe.sem_inc(gate, 1)
                    for t in range(K):
                        last = nc.tensor.transpose(p_t[:, t * P:(t + 1) * P], stage[:, it.slot, t, :], ident[:, :])
                    last.then_inc(tr_done, 1)
                    pe.wait_ge(rows_done, c)
                    if not first:
                        pe.wait_ge(hid_done, it.i)
                    pe.sem_inc(gate, 1)
                    for t in range(K * P // CHUNK):
                        cols = slice(t * CHUNK, (t + 1) * CHUNK)
                        last = nc.tensor.matmul(p_h[:, cols], w1[:, :], rows[:, it.slot, cols], start=True, stop=True)
                    last.then_inc(hid_ready, 1)

                def finish(it):
                    pe.wait_ge(hid_done, it.i + 1)
                    if not (type(it.i) is int and it.i == 0):
                        pe.wait_ge(o_done, it.i)
                    pe.sem_inc(gate, 1)
                    for t in range(K):
                        last = nc.tensor.matmul(p_o[:, t, :], hid[:, it.slot, t * P:(t + 1) * P], w2n[:, :], start=True, stop=True)
                    last.then_inc(o_ready, 1)

                def body(it, left):
                    hidden(it)
                    finish(it)
                run_loop(pe, NT, body, 3)

            @block.vector
            def _(dve):
                nc.vector.memset(stage[:, :, :, 2 * F:LK], 1.0).then_inc(cleared, 1)
                dve.wait_ge(cleared, 1)

                def norm(it):
                    c = it.i + 1
                    k = it.slot
                    dve.wait_ge(x_full[k], 16 * (it.use + 1))
                    dve.wait_ge(t_full[k], 16 * (it.use + 1))
                    if not (type(it.i) is int and it.i < 2):
                        dve.wait_ge(x2_done, it.i - 1)
                        dve.wait_ge(tr_done, it.i - 1)
                    nc.vector.tensor_tensor(x1[:, k, :, :], x_b[:, k, :, :], t_b[:, k, :, 0:F], ALU.add).then_inc(x1_done, 1)
                    dve.wait_ge(x1_done, c)
                    if not (type(it.i) is int and it.i == 0):
                        dve.wait_ge(ls["h"], it.i)
                    layernorm_stats(nc, dve, ls, c, x1[:, k, :, :], sm[:, :], nm[:, :], cc[:, :, :], sq[:, :, :], vs[:, :], ve[:, :])
                    layernorm_out(nc, dve, ls, c, stage[:, k, :, 0:F], cc[:, :, :], rs[:, :])

                def finish(it):
                    k = it.slot
                    dve.wait_ge(o_ready, it.i + 1)
                    dve.wait_ge(x2_done, it.i + 1)
                    dve.wait_ge(stored[k], 16 * it.use)
                    nc.vector.tensor_tensor(o_b[:, k, :, :], p_o[:, :, :], x2[:, k, :, :], ALU.add).then_inc(o_done, 1)

                def body(it, left):
                    norm(it)
                    if not (type(it.i) is int and it.i == 0):
                        finish(it.ahead(-1))
                run_loop(dve, NT, body, 3)
                finish(It((NT - 1) // 2, (NT - 1) % 2))


_INS = ["x", "src", "dst", "edge_attr_16", "L0_gnn_W_msg", "L0_gnn_b_msg", "L0_gnn_W_attn", "L0_gnn_b_attn",
        "L1_gnn_W1_l", "L1_gnn_b1", "L1_gnn_W1_r", "L1_gnn_W2_l", "L1_gnn_b2", "L1_gnn_W2_r"]


def kernel(**inputs):
    import numpy as _np
    import concourse.bacc as _bacc
    from concourse import mybir as _mybir
    from concourse.bass_utils import run_bass_kernel_spmd as _run

    nc = _bacc.Bacc("TRN2", target_bir_lowering=False, num_devices=1)
    arrays, args = {}, []
    for name in _INS:
        arr = _np.ascontiguousarray(inputs[name])
        arrays[f"in_{name}"] = arr
        args.append(nc.dram_tensor(f"in_{name}", arr.shape, _mybir.dt.from_np(arr.dtype), kind="ExternalInput").ap())
    args.append(nc.dram_tensor("out_0", (N, F), _mybir.dt.float32, kind="ExternalOutput").ap())
    gnn_program(nc, *args)
    r = _run(nc, [arrays], core_ids=[0])
    return r.results[0]["out_0"]
```

```python
from contextlib import ExitStack

import concourse.bass as bass
from concourse import mybir
import numpy as np

f32 = mybir.dt.float32
bf16 = mybir.dt.bfloat16
i32 = mybir.dt.int32
ALU = mybir.AluOpType
ACT = mybir.ActivationFunctionType
AX = mybir.AxisListType

P = 128
N, E, F = 100000, 50000, 16
HID = 32
CH = F * F
CHUNK = 512
J = CHUNK // P
Q = 2
T = Q * J
ITE = Q * CHUNK
NI = -(-E // ITE)
EP = NI * ITE
NC = EP // CHUNK
EK = F + 1
X_PARTS = (0, 0, 0, 1, 1, 2)
W_PARTS = (0, 1, 2, 0, 1, 0)
NP = len(X_PARTS)
XK = NP * EK
HS = 3 * F
LK = 2 * F
G = P // LK
RW = 3 * F
NK = 32
NT = -(-N // (P * NK))
BIG = 1.0e30
EPS = 1.0e-5


class It:

    def __init__(self, use, slot):
        self.use, self.slot = use, slot
        self.i = 2 * use + slot

    def ahead(self, d):
        n = self.slot + d
        return It(self.use + n // 2 if n // 2 else self.use, n % 2)


def run_loop(eng, total, body, tail, head=3):
    pairs = (total - head - tail) // 2
    for n in range(head):
        body(It(n // 2, n % 2), tail)
    with eng.Fori(0, pairs) as k:
        body(It(k + head // 2, 1), tail)
        body(It(k + head // 2 + 1, 0), tail)
    for n in range(head + 2 * pairs, total):
        body(It(n // 2, n % 2), min(tail, total - 1 - n))


def edge_view(t):
    return t[0:EP, :].rearrange("(i q p j) f -> i p q (j f)", q=Q, p=P, j=J)


def spread(ap, n):
    return ap.unsqueeze(2).broadcast_to([ap.shape[0], ap.shape[1], n])


def gnn_program(nc, x, src, dst, efeat, w_msg, b_msg, w_attn, b_attn, w1l, b1, w1r, w2l, b2, w2r, out):
    meta = nc.dram_tensor("meta", (NC * P, 3 * J), i32).ap()
    keep_d = nc.dram_tensor("keep_d", (1, EP), f32).ap()
    mask_d = nc.dram_tensor("mask_d", (1, EP), f32).ap()
    rc_d = nc.dram_tensor("rc_d", (NI, P, T), f32).ap()
    last_edge = nc.dram_tensor("last_edge", (N + EP, 1), i32).ap()
    row_of = nc.dram_tensor("row_of", (EP, 1), i32).ap()
    xs_d = nc.dram_tensor("xs_d", (EP, F), f32).ap()
    h_d = nc.dram_tensor("h_d", (EP, F), f32).ap()
    f_tab = nc.dram_tensor("f_tab", (EP + P, F), f32).ap()
    a_tab = nc.dram_tensor("a_tab", (EP + P, F), f32).ap()
    node_tab = nc.dram_tensor("node_tab", (N + EP, RW), f32).ap()

    meta_v = meta.rearrange("(i q p) f -> i p q f", q=Q, p=P)
    row_v, xs_v, h_v = edge_view(row_of), edge_view(xs_d), edge_view(h_d)
    f_v, a_v = edge_view(f_tab), edge_view(a_tab)

    with ExitStack() as ctx:
        def sb(name, shape, dt=f32):
            return ctx.enter_context(nc.sbuf_tensor(name, shape, dt))

        def sem(name):
            return ctx.enter_context(nc.semaphore(name))

        gate, pool_gate = sem("gate"), sem("pool_gate")
        ident = sb("ident", [P, P])
        identb = sb("identb", [P, P], bf16)
        ones_row = sb("ones_row", [1, P])
        in_sel = sb("in_sel", [HS, CH], bf16)
        out_sum = sb("out_sum", [P, F])
        wa = sb("wa", [XK, CH], bf16)
        wm = sb("wm", [XK, CH], bf16)
        w1 = sb("w1", [P, P])
        b1c = sb("b1c", [P, 1])
        w2g = sb("w2g", [P, G, F])
        w2n = sb("w2n", [P, G * F])
        b2r = sb("b2r", [1, NK * F])

        setup(nc, x, src, dst, meta, keep_d, mask_d, last_edge, f_tab, a_tab,
              w_msg, b_msg, w_attn, b_attn, w1l, b1, w1r, w2l, b2, w2r,
              ident, identb, ones_row, in_sel, out_sum, wa, wm, w1, b1c, w2g, w2n, b2r)
        edge_softmax(nc, sem, gate, pool_gate, x, efeat, meta_v, xs_v, row_v, f_v, mask_d, last_edge, node_tab,
                     identb, in_sel, out_sum, wa, wm)
        first_hop(nc, sem, gate, pool_gate, row_v, xs_v, h_v, a_v, rc_d, f_tab, keep_d, ident)
        second_hop(nc, sem, gate, pool_gate, row_v, meta_v, h_v, f_v, a_v, rc_d, a_tab, keep_d, node_tab, ident, w1, b1c, w2g)
        node_pass(nc, sem, gate, pool_gate, x, node_tab, out, ident, ones_row, w1, b1c, w2n, b2r)


def setup(nc, x, src, dst, meta, keep_d, mask_d, last_edge, f_tab, a_tab,
          w_msg, b_msg, w_attn, b_attn, w1l, b1, w1r, w2l, b2, w2r,
          ident, identb, ones_row, in_sel, out_sum, wa, wm, w1, b1c, w2g, w2n, b2r):
    full = E // CHUNK
    rest = E - full * CHUNK
    with ExitStack() as ctx:
        used = []

        def sb(name, shape, dt=f32):
            return ctx.enter_context(nc.sbuf_tensor(name, shape, dt))

        def sem(name):
            used.append(ctx.enter_context(nc.semaphore(name)))
            return used[-1]

        dstn = sb("dstn", [NC, CHUNK + 2], i32)
        srcn = sb("srcn", [NC, CHUNK], i32)
        keep = sb("keep", [NC, CHUNK])
        mask = sb("mask", [NC, CHUNK])
        wf = sb("wf", [EK, 2, CH])
        wp = sb("wp", [EK, 3, 2, CH], bf16)
        sel = sb("sel", [F, CH], bf16)
        is_end = sb("is_end", [NC, CHUNK])
        edge_no = sb("edge_no", [NC, CHUNK], i32)
        off = sb("off", [NC, CHUNK])
        metan = sb("metan", [NC, P, 3, J], i32)
        none_row = sb("none_row", [125, N // 125], i32)
        zrow = sb("zrow", [P, F])

        filled, loaded, w_loaded, iotas, selected = (sem(n) for n in ("filled", "loaded", "w_loaded", "iotas", "selected"))
        v_keep, v_end, v_off, v_offn, v_prod, v_row, v_idn, v_out, v_part, v_left = (
            sem(n) for n in ("v_keep", "v_end", "v_off", "v_offn", "v_prod", "v_row", "v_idn", "v_out", "v_part", "v_left"))
        stored, m_loaded, stacked = sem("setup_stored"), sem("m_loaded"), sem("stacked")
        ctx.enter_context(nc.allow_non_contiguous_dma(reason="one edge before and after each chunk"))
        with nc.Block() as block:
            @block.sync
            def _(sp):
                sp.wait_ge(filled, 6)
                sp.dma_start(dstn[0:full, 1:CHUNK + 1], dst[0:full * CHUNK].rearrange("(c e) -> c e", e=CHUNK)).then_inc(loaded, 16)
                sp.dma_start(dstn[full:NC, 1:rest + 1], dst[full * CHUNK:E].rearrange("(c e) -> c e", c=1)).then_inc(loaded, 16)
                sp.dma_start(dstn[1:NC, 0:1], dst[CHUNK - 1:CHUNK * (NC - 1):CHUNK].rearrange("(c e) -> c e", e=1)).then_inc(loaded, 16)
                sp.dma_start(dstn[0:NC - 1, CHUNK + 1:CHUNK + 2], dst[CHUNK:CHUNK * (NC - 1) + 1:CHUNK].rearrange("(c e) -> c e", e=1)).then_inc(loaded, 16)
                sp.dma_start(srcn[0:full, :], src[0:full * CHUNK].rearrange("(c e) -> c e", e=CHUNK)).then_inc(loaded, 16)
                sp.dma_start(srcn[full:NC, 0:rest], src[full * CHUNK:E].rearrange("(c e) -> c e", c=1)).then_inc(loaded, 16)
                sp.wait_ge(iotas, 2)
                sp.dma_start(last_edge[0:N, :].rearrange("(p n) o -> p (n o)", p=125), none_row[:, :]).then_inc(stored, 16)
                sp.dma_start(f_tab[EP:EP + P, :], zrow[:, :]).then_inc(stored, 16)
                sp.dma_start(a_tab[EP:EP + P, :], zrow[:, :]).then_inc(stored, 16)
                sp.wait_ge(v_keep, 1)
                sp.wait_ge(v_out, 4)
                sp.dma_start(meta.rearrange("(c p) f -> c (p f)", p=P), metan[:, :, :, :].rearrange("c p f j -> c (p f j)")).then_inc(stored, 16)
                sp.dma_start(keep_d.rearrange("o (c e) -> (o c) e", e=CHUNK), keep[:, :]).then_inc(stored, 16)
                sp.dma_start(mask_d.rearrange("o (c e) -> (o c) e", e=CHUNK), mask[:, :]).then_inc(stored, 16)
                sp.wait_ge(stored, 16 * 6)

            @block.scalar
            def _(act):
                act.wait_ge(filled, 6)
                loads = [(wf[0:F, 0, :], w_attn), (wf[F:EK, 0, :], b_attn.rearrange("(o c) -> o c", o=1)),
                         (wf[0:F, 1, :], w_msg), (wf[F:EK, 1, :], b_msg.rearrange("(o c) -> o c", o=1))]
                for to, frm in loads:
                    act.dma_start(to, frm).then_inc(w_loaded, 16)
                more = [(b2r[:, :].rearrange("o (k f) -> o k f", f=F), b2.rearrange("(o k f) -> o k f", o=1, k=1).broadcast_to([1, NK, F]))]
                for g in range(G):
                    lo = g * LK
                    more += [(w1[lo:lo + F, lo:lo + HID], w1r), (w1[lo + F:lo + LK, lo:lo + HID], w1l),
                             (b1c[lo:lo + HID, :], b1.rearrange("(k o) -> k o", o=1)),
                             (w2g[lo:lo + HID, g, :], w2l), (w2n[lo:lo + HID, g * F:(g + 1) * F], w2r)]
                for to, frm in more:
                    act.dma_start(to, frm).then_inc(m_loaded, 16)
                act.wait_ge(v_part, 3)
                for k, part in enumerate(W_PARTS):
                    act.dma_start(wa[k * EK:(k + 1) * EK, :], wp[:, part, 0, :]).then_inc(stacked, 16)
                    act.dma_start(wm[k * EK:(k + 1) * EK, :], wp[:, part, 1, :]).then_inc(stacked, 16)
                act.wait_ge(v_idn, 3)
                for k in range(3):
                    act.dma_start(in_sel[k * F:(k + 1) * F, :], sel[:, :]).then_inc(stacked, 16)
                act.wait_ge(m_loaded, 16 * len(more))
                act.wait_ge(stacked, 16 * (2 * NP + 3))

            @block.gpsimd
            def _(pool):
                nc.gpsimd.iota(edge_no[:, :], [[1, CHUNK]], base=0, channel_multiplier=CHUNK).then_inc(iotas, 1)
                nc.gpsimd.iota(none_row[:, :], [[0, N // 125]], base=EP, channel_multiplier=1).then_inc(iotas, 1)
                nc.gpsimd.memset(ident[:, :], 0.0).then_inc(selected, 1)
                pool.wait_ge(selected, 1)
                nc.gpsimd.affine_select(out=ident[:, :], in_=ident[:, :], compare_op=ALU.not_equal, fill=1.0,
                                        base=0, pattern=[[-1, P]], channel_multiplier=1).then_inc(selected, 1)

            @block.vector
            def _(dve):
                nc.vector.memset(dstn[:, :], -2).then_inc(filled, 1)
                nc.vector.memset(srcn[:, :], 0).then_inc(filled, 1)
                nc.vector.memset(w1[:, :], 0.0).then_inc(filled, 1)
                nc.vector.memset(w2g[:, :, :], 0.0).then_inc(filled, 1)
                nc.vector.memset(w2n[:, :], 0.0).then_inc(filled, 1)
                nc.vector.memset(zrow[:, :], 0.0).then_inc(filled, 1)
                nc.vector.memset(ones_row[:, :], 1.0)
                dve.wait_ge(loaded, 16 * 6)
                dve.wait_ge(iotas, 2)
                here = dstn[:, 1:CHUNK + 1]
                nc.vector.tensor_tensor(keep[:, :], here, dstn[:, 0:CHUNK], ALU.is_equal).then_inc(v_keep, 1)
                nc.vector.tensor_tensor(is_end[:, :], here, dstn[:, 2:CHUNK + 2], ALU.not_equal).then_inc(v_end, 1)
                nc.vector.tensor_tensor(off[:, :], here, edge_no[:, :], ALU.subtract).then_inc(v_off, 1)
                dve.wait_ge(v_off, 1)
                nc.vector.tensor_scalar(off[:, :], off[:, :], -float(N), None, ALU.add).then_inc(v_offn, 1)
                dve.wait_ge(v_offn, 1)
                dve.wait_ge(v_end, 1)
                nc.vector.tensor_tensor(off[:, :], off[:, :], is_end[:, :], ALU.mult).then_inc(v_prod, 1)
                dve.wait_ge(v_prod, 1)
                nc.vector.tensor_tensor(off[:, :], off[:, :], edge_no[:, :], ALU.add).then_inc(v_row, 1)
                dve.wait_ge(v_row, 1)
                fold = lambda ap: ap.rearrange("c (p j) -> c p j", j=J)
                nc.vector.tensor_scalar(metan[:, :, 1, :], fold(off[:, :]), float(N), None, ALU.add).then_inc(v_out, 1)
                nc.vector.tensor_copy(metan[:, :, 0, :], fold(srcn[:, :])).then_inc(v_out, 1)
                nc.vector.tensor_copy(metan[:, :, 2, :], fold(edge_no[:, :])).then_inc(v_out, 1)
                dve.wait_ge(v_end, 1)
                nc.vector.tensor_scalar(mask[:, :], is_end[:, :], -BIG, None, ALU.mult).then_inc(v_out, 1)
                dve.wait_ge(w_loaded, 16 * 4)
                for part in range(3):
                    nc.vector.tensor_copy(wp[:, part, :, :], wf[:, :, :]).then_inc(v_part, 1)
                    dve.wait_ge(v_part, part + 1)
                    if part < 2:
                        nc.vector.tensor_tensor(wf[:, :, :], wf[:, :, :], wp[:, part, :, :], ALU.subtract).then_inc(v_left, 1)
                        dve.wait_ge(v_left, part + 1)
                dve.wait_ge(selected, 2)
                nc.vector.tensor_copy(identb[:, :], ident[:, :]).then_inc(v_idn, 1)
                nc.vector.tensor_reduce(out_sum[:, :], ident[:, :].rearrange("p (i o) -> p o i", o=F), AX.X, ALU.add).then_inc(v_idn, 1)
                nc.vector.tensor_copy(sel[:, :].rearrange("k (i o) -> k i o", o=F), spread(ident[0:F, 0:F], F)).then_inc(v_idn, 1)
        with nc.Block() as block:
            @block.sync
            def _(sp):
                for one in used:
                    sp.sem_clear(one)


def layernorm_sems(sem, tag):
    return {k: sem(f"{tag}_{k}") for k in ("sum", "mean", "cent", "sq", "sqsum", "var", "ln", "rstd", "h")}


def layernorm_stats(nc, dve, s, n, rows, sm, nm, cc, sq, vs, ve):
    nc.vector.tensor_reduce(sm, rows, AX.X, ALU.add).then_inc(s["sum"], 1)
    dve.wait_ge(s["sum"], n)
    nc.vector.tensor_scalar(nm, sm, -1.0 / F, None, ALU.mult).then_inc(s["mean"], 1)
    dve.wait_ge(s["mean"], n)
    nc.vector.tensor_tensor(cc, rows, spread(nm, F), ALU.add).then_inc(s["cent"], 1)
    dve.wait_ge(s["cent"], n)
    nc.vector.tensor_tensor(sq, cc, cc, ALU.mult).then_inc(s["sq"], 1)
    dve.wait_ge(s["sq"], n)
    nc.vector.tensor_reduce(vs, sq, AX.X, ALU.add).then_inc(s["sqsum"], 1)
    dve.wait_ge(s["sqsum"], n)
    nc.vector.tensor_scalar(ve, vs, 1.0 / F, EPS, ALU.mult, ALU.add).then_inc(s["var"], 1)


def layernorm_rstd(nc, act, s, n, ve, ln, rs):
    act.wait_ge(s["var"], n)
    nc.scalar.activation(ln, ve, ACT.Ln).then_inc(s["ln"], 1)
    act.wait_ge(s["ln"], n)
    nc.scalar.activation(rs, ln, ACT.Exp, scale=-0.5).then_inc(s["rstd"], 1)


def layernorm_out(nc, dve, s, n, h, cc, rs):
    dve.wait_ge(s["rstd"], n)
    nc.vector.scalar_tensor_tensor(h, cc, 0.0, spread(rs, F), ALU.max, ALU.mult).then_inc(s["h"], 1)


def edge_softmax(nc, sem, gate, pool_gate, x, efeat, meta_v, xs_v, row_v, f_v, mask_d, last_edge, node_tab,
                 identb, in_sel, out_sum, wa, wm):
    UN = 2 * Q
    ZN = -(-N // (NI * P))
    zero_v = node_tab[0:NI * P * ZN, :].rearrange("(i p a) f -> i p (a f)", p=P, a=ZN)
    ctx = ExitStack()
    with ctx:
        def sb(name, shape, dt=f32):
            return ctx.enter_context(nc.sbuf_tensor(name, shape, dt))

        def ps(name, shape):
            return ctx.enter_context(nc.psum_tensor(name, shape, f32))

        meta_b = sb("meta_b", [P, 2, Q, 3 * J], i32)
        gx = sb("gx", [P, 2, Q, J * F])
        row_b = sb("row_b", [P, 2, Q, J], i32)
        zeros = sb("zeros", [P, ZN * RW])
        xs_b = sb("xs_b", [P, 2, T, F])
        ef_b = sb("ef_b", [P, 2, T, F])
        left = sb("left", [P, T, F])
        hf = sb("hf", [P, T, F])
        xstage = sb("xstage", [P, 2, T, NP, EK], bf16)
        hstage = sb("hstage", [P, 2, T, 3, F], bf16)
        mask_b = sb("mask_b", [P, 2, ITE])
        xrows = sb("xrows", [XK, 2, Q, CHUNK], bf16)
        hrows = sb("hrows", [HS, 2, Q, CHUNK], bf16)
        sm, nm, vs, ve, lnv, rs = (sb(f"l0_{n}", [P, T]) for n in ("sm", "nm", "vs", "ve", "lnv", "rs"))
        cc, sq = (sb(f"l0_{n}", [P, T, F]) for n in ("cc", "sq"))
        hb = sb("hb", [P, 2, CHUNK])
        e2 = sb("e2", [P, 2, CHUNK])
        r = sb("r", [P, 2, CHUNK])
        a = sb("a", [P, 2, CHUNK])
        w = sb("w", [P, UN, CHUNK + 1])
        s = sb("s", [P, UN, CHUNK])
        n = sb("n", [P, UN, CHUNK])
        rec = sb("rec", [P, 2, CHUNK])
        ratio = sb("ratio", [P, UN, CHUNK])
        f_b = sb("f_b", [P, 2, Q, J * F])

        p_wa = ps("p_wa", [P, CHUNK])
        p_wm = ps("p_wm", [P, CHUNK])
        p_hb = ps("p_hb", [P, 2, CHUNK])
        p_x = ctx.enter_context(nc.psum_tensor("p_x", [XK, Q, J, P], bf16))
        p_h = ctx.enter_context(nc.psum_tensor("p_h", [HS, Q, J, P], bf16))
        p_fb = ps("p_f", [P, Q, CHUNK])
        p_f = p_fb[:, :, 0:J * F].rearrange("p q (j f) -> p q j f", f=F)

        meta_full, gx_full, xs_stored, pos_done, row_full, row_stored, ef_full, xs_full, mask_full, f_stored = (
            [sem(f"{nm}{k}") for k in range(2)] for nm in
            ("meta_full", "gx_full", "xs_stored", "pos_done", "row_full", "row_stored", "ef_full", "xs_full",
             "mask_full", "f_stored"))
        zeros_set, zero_stored, cleared = sem("zeros_set"), sem("zero_stored"), sem("cleared")
        ls = layernorm_sems(sem, "l0")
        tr_done, rows_done = sem("tr_done"), sem("rows_done")
        x_p, x_l, h_p, h_l = ([sem(f"{nm}{k}") for k in range(3)] for nm in ("x_part", "x_left", "h_part", "h_left"))
        hb_ready = sem("u_hb_ready")
        w_ready, hb_done, e2_done, e1_done, w0_done, w_done, d_done, dpos_done, dneg_done = (
            sem(f"u_{k}") for k in ("w_ready", "hb_done", "e2_done", "e1_done", "w0_done", "w_done", "d_done", "pos_dn", "neg_dn"))
        p_done, a_done, r_done, s_done, n_done, log_done, rec_done, ratio_done = (
            sem(f"u_{k}") for k in ("p_done", "a_done", "r_done", "s_done", "n_done", "log_done", "rec_done", "ratio_done"))
        f_sum, f_copied = ([sem(f"{k}{q}") for q in range(Q)] for k in ("f_sum", "f_copied"))

        def unit(it, u):
            return it.i * UN + u + 1

        with nc.Block() as block:
            @block.sync
            def _(sp):
                def load_meta(it):
                    sp.dma_start(meta_b[:, it.slot, :, :], meta_v[it.i]).then_inc(meta_full[it.slot], 16)

                for k in range(2):
                    load_meta(It(0, k))

                def first(it, left):
                    sp.wait_ge(gx_full[it.slot], 16 * T * (it.use + 1))
                    sp.dma_start(xs_v[it.i], gx[:, it.slot, :, :]).then_inc(xs_stored[it.slot], 16)
                    if left >= 2:
                        sp.wait_ge(pos_done[it.slot], 16 * T * (it.use + 1))
                        load_meta(it.ahead(2))
                run_loop(sp, NI, first, 2)
                sp.wait_ge(zeros_set, 1)
                for k in range(2):
                    sp.wait_ge(pos_done[k], 16 * T * ((NI + 1 - k) // 2))
                    load_meta(It(0, k))

                def second(it, left):
                    sp.dma_start(zero_v[it.i], zeros[:, :]).then_inc(zero_stored, 16)
                    sp.wait_ge(row_full[it.slot], 16 * T * (it.use + 1))
                    sp.dma_start(row_v[it.i], row_b[:, it.slot, :, :]).then_inc(row_stored[it.slot], 16)
                    if left >= 2:
                        load_meta(it.ahead(2))
                run_loop(sp, NI, second, 2)
                for k in range(2):
                    sp.wait_ge(xs_stored[k], 16 * ((NI + 1 - k) // 2))
                    sp.wait_ge(row_stored[k], 16 * ((NI + 1 - k) // 2))
                sp.wait_ge(zero_stored, 16 * NI)

            @block.gpsimd
            def _(pool):
                nc.gpsimd.memset(zeros[:, :], 0.0).then_inc(zeros_set, 1)

                def first(it, left):
                    pool.wait_ge(meta_full[it.slot], 16 * (it.use + 1))
                    pool.wait_ge(xs_stored[it.slot], 16 * it.use)
                    pool.sem_inc(pool_gate, 1)
                    for q in range(Q):
                        for j in range(J):
                            pool.indirect_dma_start(gx[:, it.slot, q, j * F:(j + 1) * F], None, x,
                                                    bass.IndirectOffsetOnAxis(ap=meta_b[:, it.slot, q, j:j + 1], axis=0)) \
                                .then_inc(gx_full[it.slot], 16)
                    for q in range(Q):
                        for j in range(J):
                            pool.indirect_dma_start(last_edge, bass.IndirectOffsetOnAxis(ap=meta_b[:, it.slot, q, J + j:J + j + 1], axis=0),
                                                    meta_b[:, it.slot, q, 2 * J + j:2 * J + j + 1], None) \
                                .then_inc(pos_done[it.slot], 16)
                run_loop(pool, NI, first, 2)
                for k in range(2):
                    pool.wait_ge(pos_done[k], 16 * T * ((NI + 1 - k) // 2))

                def second(it, left):
                    pool.wait_ge(meta_full[it.slot], 16 * (it.use + 1 + (NI + 1 - it.slot) // 2))
                    pool.wait_ge(row_stored[it.slot], 16 * it.use)
                    pool.sem_inc(pool_gate, 1)
                    for q in range(Q):
                        for j in range(J):
                            pool.indirect_dma_start(row_b[:, it.slot, q, j:j + 1], None, last_edge,
                                                    bass.IndirectOffsetOnAxis(ap=meta_b[:, it.slot, q, j:j + 1], axis=0)) \
                                .then_inc(row_full[it.slot], 16)
                run_loop(pool, NI, second, 2)

            def static_first(it, u, n):
                return type(it.i) is int and it.i * UN + u < n

            @block.scalar
            def _(act):
                act.preload_act_table_set("natural_log_exp_and_others")
                efv = edge_view_part(efeat)

                def load(it, partial):
                    k = it.slot
                    ef_q = ef_b[:, k, :, :].rearrange("p (q j) f -> p q (j f)", q=Q)
                    if partial:
                        lastq = E - (NI - 1) * ITE - CHUNK
                        act.dma_start(ef_q[:, 0, :], efeat[E - lastq - CHUNK:E - lastq, :].rearrange("(p j) f -> p (j f)", j=J)).then_inc(ef_full[k], 16)
                        act.dma_start(ef_q[0:lastq // J, 1, :], efeat[E - lastq:E, :].rearrange("(p j) f -> p (j f)", j=J)).then_inc(ef_full[k], 16)
                    else:
                        for q in range(Q):
                            act.dma_start(ef_q[:, q, :], efv[it.i][q]).then_inc(ef_full[k], 16)
                    act.wait_ge(xs_stored[k], 16 * (it.use + 1))
                    act.dma_start(xs_b[:, k, :, :].rearrange("p (q j) f -> p q (j f)", q=Q), xs_v[it.i]).then_inc(xs_full[k], 16)

                def load_mask(it):
                    act.dma_start(mask_b[:, it.slot, :], row_slice(mask_d, it.i, P)).then_inc(mask_full[it.slot], 16)

                def x_part(it, part, src, pairs):
                    act.activation(xstage[:, it.slot, :, pairs, 0:F], src.unsqueeze(2).broadcast_to([P, T, pairs.stop - pairs.start, F]), ACT.Copy) \
                        .then_inc(x_p[part], 1)

                def x_first(it):
                    act.wait_ge(ef_full[it.slot], 32 * (it.use + 1))
                    if not (type(it.i) is int and it.i < 2):
                        act.wait_ge(tr_done, it.i - 1)
                    x_part(it, 0, ef_b[:, it.slot, :, :], slice(0, 3))

                def x_second(it):
                    act.wait_ge(x_l[0], it.i + 1)
                    x_part(it, 1, left[:, :, :], slice(3, 5))

                def x_third(it):
                    act.wait_ge(x_l[1], it.i + 1)
                    x_part(it, 2, left[:, :, :], slice(5, 6))

                def copy_rows(it):
                    act.wait_ge(tr_done, it.i + 1)
                    if not (type(it.i) is int and it.i < 2):
                        act.wait_ge(w_ready, UN * (it.i - 1))
                    act.activation(xrows[:, it.slot, :, :].rearrange("k q (p j) -> k q j p", j=J), p_x[:, :, :, :], ACT.Copy).then_inc(rows_done, 1)
                    act.activation(hrows[:, it.slot, :, :].rearrange("k q (p j) -> k q j p", j=J), p_h[:, :, :, :], ACT.Copy).then_inc(rows_done, 1)

                def copy_f(it, q):
                    act.wait_ge(f_sum[q], it.i + 1)
                    if q == 0:
                        act.wait_ge(f_stored[it.slot], 16 * it.use)
                    act.activation(f_b[:, it.slot, q, :], p_f[:, q, :, :].rearrange("p j f -> p (j f)"), ACT.Copy).then_inc(f_copied[q], 1)

                def store_f(it):
                    copy_f(it, 1)
                    act.wait_ge(f_copied[0], it.i + 1)
                    act.wait_ge(f_copied[1], it.i + 1)
                    act.dma_start(f_v[it.i], f_b[:, it.slot, :, :]).then_inc(f_stored[it.slot], 16)

                def copy_hb(it, u):
                    c = unit(it, u)
                    act.wait_ge(hb_ready, c)
                    if not static_first(it, u, 2):
                        act.wait_ge(e1_done, c - 2)
                    act.activation(hb[:, u % 2, :], p_hb[:, u % 2, :], ACT.Copy).then_inc(hb_done, 1)

                def exps(it, u):
                    c = unit(it, u)
                    k = u % 2
                    act.wait_ge(d_done, c)
                    if not static_first(it, u, 2):
                        act.wait_ge(n_done, c - 2)
                    act.activation(a[:, k, :], e2[:, k, :], ACT.Relu).then_inc(dpos_done, 1)
                    act.wait_ge(dpos_done, c)
                    act.activation(e2[:, k, :], e2[:, k, :], ACT.Relu, scale=-1.0).then_inc(dneg_done, 1)
                    act.activation(a[:, k, :], a[:, k, :], ACT.Exp, scale=-1.0).then_inc(a_done, 1)
                    act.wait_ge(dneg_done, c)
                    act.activation(e2[:, k, :], e2[:, k, :], ACT.Exp, scale=-1.0).then_inc(p_done, 1)

                def reciprocal(it, u):
                    c = unit(it, u)
                    act.wait_ge(s_done, c)
                    if not static_first(it, u, 2):
                        act.wait_ge(ratio_done, c - 2)
                    act.activation(rec[:, u % 2, :], s[:, u, :], ACT.Ln).then_inc(log_done, 1)
                    act.wait_ge(log_done, c)
                    act.activation(rec[:, u % 2, :], rec[:, u % 2, :], ACT.Exp, scale=-1.0).then_inc(rec_done, 1)

                for k in range(2):
                    load(It(0, k), False)
                    load_mask(It(0, k))
                act.wait_ge(cleared, 6)
                x_first(It(0, 0))
                x_second(It(0, 0))
                x_third(It(0, 0))
                layernorm_rstd(nc, act, ls, 1, ve[:, :], lnv[:, :], rs[:, :])
                copy_rows(It(0, 0))
                copy_hb(It(0, 0), 0)
                copy_hb(It(0, 0), 1)

                def body(it, left_over):
                    nxt = it.ahead(1)
                    if left_over:
                        x_first(nxt)
                    exps(it, 0)
                    if not static_first(it, 0, 1):
                        reciprocal(it.ahead(-1), 3)
                    copy_hb(it, 2)
                    if left_over:
                        x_second(nxt)
                        layernorm_rstd(nc, act, ls, nxt.i + 1, ve[:, :], lnv[:, :], rs[:, :])
                    exps(it, 1)
                    if left_over:
                        x_third(nxt)
                    reciprocal(it, 0)
                    copy_hb(it, 3)
                    if not static_first(it, 0, 1):
                        copy_f(it.ahead(-1), 0)
                    if left_over >= 2:
                        act.wait_ge(x_l[0], nxt.i + 1)
                        act.wait_ge(ls["cent"], nxt.i + 1)
                        load(it.ahead(2), left_over == 2 and type(it.i) is int and it.i == NI - 3)
                    if left_over:
                        copy_rows(nxt)
                    exps(it, 2)
                    reciprocal(it, 1)
                    if left_over:
                        copy_hb(nxt, 0)
                    exps(it, 3)
                    reciprocal(it, 2)
                    if left_over:
                        copy_hb(nxt, 1)
                    if not static_first(it, 0, 1):
                        store_f(it.ahead(-1))
                    if left_over >= 2:
                        act.wait_ge(w_done, unit(it, 3))
                        load_mask(it.ahead(2))
                run_loop(act, NI, body, 3)
                end = It((NI - 1) // 2, (NI - 1) % 2)
                reciprocal(end, 3)
                copy_f(end, 0)
                store_f(end)
                for k in range(2):
                    act.wait_ge(f_stored[k], 16 * ((NI + 1 - k) // 2))

            @block.tensor
            def _(pe):
                def transposes(it):
                    k = it.slot
                    pe.wait_ge(h_p[2], it.i + 1)
                    pe.wait_ge(x_p[2], it.i + 1)
                    if not static_first(it, 0, 1):
                        pe.wait_ge(rows_done, 2 * it.i)
                    pe.sem_inc(gate, 1)
                    for t in range(T):
                        nc.tensor.transpose(p_x[:, t // J, t % J, :], xstage[:, k, t, :, :].rearrange("p n f -> p (n f)"), identb[:, :])
                    for t in range(T):
                        last = nc.tensor.transpose(p_h[:, t // J, t % J, :], hstage[:, k, t, :, :].rearrange("p n f -> p (n f)"), identb[:, :])
                    last.then_inc(tr_done, 1)

                def h_product(it, u):
                    c = unit(it, u)
                    if u == 0:
                        pe.wait_ge(rows_done, 2 * (it.i + 1))
                    if not static_first(it, u, 2):
                        pe.wait_ge(hb_done, c - 2)
                    pe.sem_inc(gate, 1)
                    nc.tensor.matmul(p_hb[:, u % 2, :], in_sel[:, (u % 2) * P:(u % 2 + 1) * P], hrows[:, it.slot, u // 2, :],
                                     start=True, stop=True).then_inc(hb_ready, 1)

                def products(it, u):
                    c = unit(it, u)
                    if not static_first(it, u, 1):
                        pe.wait_ge(e1_done, c - 1)
                    pe.sem_inc(gate, 1)
                    cols = slice((u % 2) * P, (u % 2 + 1) * P)
                    nc.tensor.matmul(p_wa[:, :], wa[:, cols], xrows[:, it.slot, u // 2, :], start=True, stop=True)
                    nc.tensor.matmul(p_wm[:, :], wm[:, cols], xrows[:, it.slot, u // 2, :], start=True, stop=True).then_inc(w_ready, 1)

                def sums(it, q):
                    pe.wait_ge(ratio_done, unit(it, 2 * q + 1))
                    if not static_first(it, 0, 1):
                        pe.wait_ge(f_copied[q], it.i)
                    pe.sem_inc(gate, 1)
                    for j in range(J):
                        for half in range(2):
                            last = nc.tensor.matmul(p_f[:, q, j, :], ratio[:, 2 * q + half, j:CHUNK:J], out_sum[:, :],
                                                    start=(half == 0), stop=(half == 1))
                    last.then_inc(f_sum[q], 1)

                transposes(It(0, 0))
                h_product(It(0, 0), 0)
                products(It(0, 0), 0)
                h_product(It(0, 0), 1)

                def body(it, left_over):
                    nxt = it.ahead(1)
                    products(it, 1)
                    h_product(it, 2)
                    if not static_first(it, 0, 1):
                        sums(it.ahead(-1), 0)
                    products(it, 2)
                    h_product(it, 3)
                    if left_over:
                        transposes(nxt)
                    products(it, 3)
                    if left_over:
                        h_product(nxt, 0)
                    if not static_first(it, 0, 1):
                        sums(it.ahead(-1), 1)
                    if left_over:
                        products(nxt, 0)
                        h_product(nxt, 1)
                run_loop(pe, NI, body, 3)
                end = It((NI - 1) // 2, (NI - 1) % 2)
                sums(end, 0)
                sums(end, 1)

            @block.vector
            def _(dve):
                nc.vector.memset(xstage[:, :, :, :, :], 0.0).then_inc(cleared, 1)
                nc.vector.memset(w[:, :, :], -BIG).then_inc(cleared, 1)
                nc.vector.memset(s[:, :, :], 0.0).then_inc(cleared, 1)
                nc.vector.memset(n[:, :, :], 0.0).then_inc(cleared, 1)
                dve.wait_ge(cleared, 4)
                for k in range(2):
                    nc.vector.memset(xstage[:, k, :, 0:3, F:EK], 1.0).then_inc(cleared, 1)
                dve.wait_ge(cleared, 6)

                def front(it, u):
                    c = unit(it, u)
                    k, q = u % 2, u // 2
                    before = (u + 2) % UN
                    if not static_first(it, u, 2):
                        dve.wait_ge(w_done, c - 2)
                        dve.wait_ge(r_done, c - 2)
                        dve.wait_ge(n_done, c - 2)
                    nc.vector.tensor_copy(w[:, u, 0:1], w[:, before, CHUNK:CHUNK + 1]).then_inc(w0_done, 1)
                    dve.wait_ge(hb_done, c)
                    dve.wait_ge(w_ready, c)
                    nc.vector.tensor_tensor(e2[:, k, :], p_wa[:, :], hb[:, k, :], ALU.mult).then_inc(e2_done, 1)
                    nc.vector.tensor_tensor(r[:, k, :], p_wm[:, :], hb[:, k, :], ALU.mult).then_inc(e1_done, 1)
                    if u == 0:
                        dve.wait_ge(mask_full[it.slot], 16 * (it.use + 1))
                    dve.wait_ge(w0_done, c)
                    dve.wait_ge(e2_done, c)
                    nc.vector.tensor_tensor_scan(w[:, u, 1:CHUNK + 1], e2[:, k, :], mask_b[:, it.slot, q * CHUNK:(q + 1) * CHUNK],
                                                 w[:, u, 0:1], ALU.max, ALU.add).then_inc(w_done, 1)
                    dve.wait_ge(w_done, c)
                    nc.vector.tensor_tensor(e2[:, k, :], e2[:, k, :], w[:, u, 0:CHUNK], ALU.subtract).then_inc(d_done, 1)

                def back(it, u):
                    c = unit(it, u)
                    k = u % 2
                    before = (u + 2) % UN
                    dve.wait_ge(a_done, c)
                    dve.wait_ge(p_done, c)
                    dve.wait_ge(e1_done, c)
                    if not static_first(it, u, 2):
                        dve.wait_ge(s_done, c - 2)
                    nc.vector.tensor_tensor(r[:, k, :], r[:, k, :], e2[:, k, :], ALU.mult).then_inc(r_done, 1)
                    if not static_first(it, u, 4):
                        dve.wait_ge(rec_done, c - 4)
                        dve.wait_ge(ratio_done, c - 4)
                    nc.vector.tensor_tensor_scan(s[:, u, :], a[:, k, :], e2[:, k, :], s[:, before, CHUNK - 1:CHUNK], ALU.mult, ALU.add).then_inc(s_done, 1)
                    dve.wait_ge(r_done, c)
                    nc.vector.tensor_tensor_scan(n[:, u, :], a[:, k, :], r[:, k, :], n[:, before, CHUNK - 1:CHUNK], ALU.mult, ALU.add).then_inc(n_done, 1)

                def divide(it, u):
                    c = unit(it, u)
                    dve.wait_ge(rec_done, c)
                    dve.wait_ge(n_done, c)
                    if not static_first(it, 0, 1):
                        dve.wait_ge(f_sum[u // 2], it.i)
                    nc.vector.tensor_tensor(ratio[:, u, :], n[:, u, :], rec[:, u % 2, :], ALU.mult).then_inc(ratio_done, 1)

                def stats(it):
                    dve.wait_ge(xs_full[it.slot], 16 * (it.use + 1))
                    if not static_first(it, 0, 1):
                        dve.wait_ge(ls["h"], it.i)
                    layernorm_stats(nc, dve, ls, it.i + 1, xs_b[:, it.slot, :, :], sm[:, :], nm[:, :], cc[:, :, :], sq[:, :, :], vs[:, :], ve[:, :])

                def x_left(it, part):
                    dve.wait_ge(x_p[part], it.i + 1)
                    if part == 0:
                        if not static_first(it, 0, 1):
                            dve.wait_ge(x_p[2], it.i)
                        nc.vector.tensor_tensor(left[:, :, :], ef_b[:, it.slot, :, :], xstage[:, it.slot, :, 0, 0:F], ALU.subtract).then_inc(x_l[0], 1)
                    else:
                        nc.vector.tensor_tensor(left[:, :, :], left[:, :, :], xstage[:, it.slot, :, 3, 0:F], ALU.subtract).then_inc(x_l[1], 1)

                def normed(it):
                    if not static_first(it, 0, 1):
                        dve.wait_ge(h_p[2], it.i)
                    if not (type(it.i) is int and it.i < 2):
                        dve.wait_ge(tr_done, it.i - 1)
                    layernorm_out(nc, dve, ls, it.i + 1, hf[:, :, :], cc[:, :, :], rs[:, :])
                    c = it.i + 1
                    dve.wait_ge(ls["h"], c)
                    for part in range(3):
                        nc.vector.tensor_copy(hstage[:, it.slot, :, part, :], hf[:, :, :]).then_inc(h_p[part], 1)
                        if part < 2:
                            dve.wait_ge(h_p[part], c)
                            nc.vector.tensor_tensor(hf[:, :, :], hf[:, :, :], hstage[:, it.slot, :, part, :], ALU.subtract).then_inc(h_l[part], 1)
                            dve.wait_ge(h_l[part], c)

                x_left(It(0, 0), 0)
                x_left(It(0, 0), 1)
                stats(It(0, 0))
                normed(It(0, 0))

                def body(it, left_over):
                    nxt, last = it.ahead(1), it.ahead(-1)
                    started = not static_first(it, 0, 1)
                    front(it, 0)
                    if left_over:
                        stats(nxt)
                        x_left(nxt, 0)
                    if started:
                        back(last, 3)
                        divide(last, 2)
                    front(it, 1)
                    if left_over:
                        x_left(nxt, 1)
                        normed(nxt)
                    back(it, 0)
                    if started:
                        divide(last, 3)
                    front(it, 2)
                    back(it, 1)
                    divide(it, 0)
                    front(it, 3)
                    back(it, 2)
                    divide(it, 1)
                run_loop(dve, NI, body, 3)
                end = It((NI - 1) // 2, (NI - 1) % 2)
                back(end, 3)
                divide(end, 2)
                divide(end, 3)


def edge_view_part(t):
    whole = E // ITE
    return Chunks(t[0:whole * ITE, :].rearrange("(i q p j) f -> i q p j f", q=Q, p=P, j=J))


class Chunks:
    def __init__(self, view):
        self.view = view

    def __getitem__(self, i):
        return [self.view[i, q] for q in range(Q)]


def row_slice(row, i, parts):
    one = row.rearrange("o (i e) -> (o i) e", e=ITE)[i].rearrange("(o e) -> o e", o=1)
    return one.broadcast_to([parts, ITE])


def first_hop(nc, sem, gate, pool_gate, row_v, xs_v, h_v, a_v, rc_d, f_tab, keep_d, ident):
    ctx = ExitStack()
    with ctx:
        def sb(name, shape, dt=f32):
            return ctx.enter_context(nc.sbuf_tensor(name, shape, dt))

        row_b = sb("h1_row", [P, 2, Q, J], i32)
        g = sb("h1_g", [P, 2, T, F])
        xs_b = sb("h1_xs", [P, 2, T, F])
        keep_b = sb("h1_keep", [EK, 2, ITE])
        x1 = sb("h1_x1", [P, 2, T, F])
        h_b = sb("h1_h", [P, 2, T, EK])
        sm, nm, vs, ve, lnv, rs = (sb(f"h1_{n}", [P, T]) for n in ("sm", "nm", "vs", "ve", "lnv", "rs"))
        cc, sq = (sb(f"h1_{n}", [P, T, F]) for n in ("cc", "sq"))
        rows = sb("h1_rows", [EK, 2, ITE])
        acc = sb("h1_acc", [EK, 2, ITE])
        rc = sb("h1_rc", [P, 2, T])
        mean = sb("h1_mean", [P, 2, T, F])
        p_t = ctx.enter_context(nc.psum_tensor("h1_pt", [EK, Q, J, P], f32))
        p_b = ctx.enter_context(nc.psum_tensor("h1_pb", [P, T, EK], f32))

        row_full, g_full, xs_full, keep_full, h_stored, mean_stored, rc_stored = (
            [sem(f"h1_{n}{k}") for k in range(2)] for n in ("row_full", "g_full", "xs_full", "keep_full", "h_stored", "mean_stored", "rc_stored"))
        ls = layernorm_sems(sem, "h1")
        cleared, x1_done, tr_done, rows_done, acc_done, bk_done, rc_done, mean_done = (
            sem(f"h1_{n}") for n in ("cleared", "x1_done", "tr_done", "rows_done", "acc_done", "bk_done", "rc_done", "mean_done"))

        h_v2 = Chunks(h_d_view(h_v))
        with nc.Block() as block:
            @block.sync
            def _(sp):
                def load_rows(it):
                    sp.dma_start(row_b[:, it.slot, :, :], row_v[it.i]).then_inc(row_full[it.slot], 16)

                def load_xs(it):
                    sp.dma_start(xs_b[:, it.slot, :, :].rearrange("p (q j) f -> p q (j f)", q=Q), xs_v[it.i]).then_inc(xs_full[it.slot], 16)

                def load_keep(it):
                    sp.dma_start(keep_b[:, it.slot, :], row_slice(keep_d, it.i, EK)).then_inc(keep_full[it.slot], 16)

                for k in range(2):
                    load_rows(It(0, k))
                    load_xs(It(0, k))
                    load_keep(It(0, k))

                def body(it, left_over):
                    if left_over >= 2:
                        sp.wait_ge(g_full[it.slot], 16 * T * (it.use + 1))
                        load_rows(it.ahead(2))
                        sp.wait_ge(x1_done, it.i + 1)
                        load_xs(it.ahead(2))
                        sp.wait_ge(acc_done, it.i + 1)
                        load_keep(it.ahead(2))
                run_loop(sp, NI, body, 2)

            @block.gpsimd
            def _(pool):
                def body(it, left):
                    pool.wait_ge(row_full[it.slot], 16 * (it.use + 1))
                    if not (type(it.i) is int and it.i < 2):
                        pool.wait_ge(x1_done, it.i - 1)
                    pool.sem_inc(pool_gate, 1)
                    for t in range(T):
                        pool.indirect_dma_start(g[:, it.slot, t, :], None, f_tab,
                                                bass.IndirectOffsetOnAxis(ap=row_b[:, it.slot, t // J, t % J:t % J + 1], axis=0)) \
                            .then_inc(g_full[it.slot], 16)
                run_loop(pool, NI, body, 2)

            @block.scalar
            def _(act):
                def store_mean(it):
                    act.wait_ge(mean_done, it.i + 1)
                    act.dma_start(a_v[it.i], mean[:, it.slot, :, :].rearrange("p (q j) f -> p q (j f)", q=Q)).then_inc(mean_stored[it.slot], 16)
                    act.dma_start(rc_d[it.i], rc[:, it.slot, :]).then_inc(rc_stored[it.slot], 16)

                def body(it, left_over):
                    layernorm_rstd(nc, act, ls, it.i + 1, ve[:, :], lnv[:, :], rs[:, :])
                    act.wait_ge(tr_done, it.i + 1)
                    if not (type(it.i) is int and it.i < 2):
                        act.wait_ge(acc_done, it.i - 1)
                    for q in range(Q):
                        act.activation(rows[:, it.slot, q * CHUNK:(q + 1) * CHUNK].rearrange("k (p j) -> k j p", j=J), p_t[:, q, :, :], ACT.Copy) \
                            .then_inc(rows_done, 1)
                    for q in range(Q):
                        act.dma_start(h_v2[it.i][q], h_b[:, it.slot, q * J:(q + 1) * J, 0:F]).then_inc(h_stored[it.slot], 16)
                    if not (type(it.i) is int and it.i == 0):
                        store_mean(it.ahead(-1))
                run_loop(act, NI, body, 2)
                store_mean(It((NI - 1) // 2, (NI - 1) % 2))
                for k in range(2):
                    act.wait_ge(h_stored[k], 32 * ((NI + 1 - k) // 2))
                    act.wait_ge(mean_stored[k], 16 * ((NI + 1 - k) // 2))
                    act.wait_ge(rc_stored[k], 16 * ((NI + 1 - k) // 2))

            @block.tensor
            def _(pe):
                def forth(it):
                    pe.wait_ge(ls["h"], it.i + 1)
                    if not (type(it.i) is int and it.i == 0):
                        pe.wait_ge(rows_done, Q * it.i)
                    pe.sem_inc(gate, 1)
                    for t in range(T):
                        last = nc.tensor.transpose(p_t[:, t // J, t % J, :], h_b[:, it.slot, t, :], ident[:, :])
                    last.then_inc(tr_done, 1)

                def back(it):
                    pe.wait_ge(acc_done, it.i + 1)
                    if not (type(it.i) is int and it.i == 0):
                        pe.wait_ge(mean_done, it.i)
                    pe.sem_inc(gate, 1)
                    for t in range(T):
                        q, j = t // J, t % J
                        last = nc.tensor.transpose(p_b[:, t, :], acc[:, it.slot, q * CHUNK + j:(q + 1) * CHUNK:J], ident[0:EK, 0:EK])
                    last.then_inc(bk_done, 1)

                def body(it, left):
                    forth(it)
                    if not (type(it.i) is int and it.i == 0):
                        back(it.ahead(-1))
                run_loop(pe, NI, body, 2)
                back(It((NI - 1) // 2, (NI - 1) % 2))

            @block.vector
            def _(dve):
                nc.vector.memset(acc[:, :, :], 0.0).then_inc(cleared, 1)
                nc.vector.memset(h_b[:, :, :, F:EK], 1.0).then_inc(cleared, 1)
                dve.wait_ge(cleared, 2)

                def norm(it):
                    c = it.i + 1
                    first = type(it.i) is int and it.i == 0
                    dve.wait_ge(g_full[it.slot], 16 * T * (it.use + 1))
                    dve.wait_ge(xs_full[it.slot], 16 * (it.use + 1))
                    nc.vector.tensor_tensor(x1[:, it.slot, :, :], g[:, it.slot, :, :], xs_b[:, it.slot, :, :], ALU.add).then_inc(x1_done, 1)
                    dve.wait_ge(x1_done, c)
                    if not first:
                        dve.wait_ge(ls["h"], it.i)
                    layernorm_stats(nc, dve, ls, c, x1[:, it.slot, :, :], sm[:, :], nm[:, :], cc[:, :, :], sq[:, :, :], vs[:, :], ve[:, :])

                def normed(it):
                    dve.wait_ge(h_stored[it.slot], 32 * it.use)
                    if not (type(it.i) is int and it.i < 2):
                        dve.wait_ge(tr_done, it.i - 1)
                    layernorm_out(nc, dve, ls, it.i + 1, h_b[:, it.slot, :, 0:F], cc[:, :, :], rs[:, :])

                def scan(it):
                    c = it.i + 1
                    dve.wait_ge(rows_done, Q * c)
                    dve.wait_ge(keep_full[it.slot], 16 * (it.use + 1))
                    if not (type(it.i) is int and it.i < 2):
                        dve.wait_ge(bk_done, it.i - 1)
                    if not (type(it.i) is int and it.i == 0):
                        dve.wait_ge(acc_done, it.i)
                    nc.vector.tensor_tensor_scan(acc[:, it.slot, :], keep_b[:, it.slot, :], rows[:, it.slot, :],
                                                 acc[:, 1 - it.slot, ITE - 1:ITE], ALU.mult, ALU.add).then_inc(acc_done, 1)

                def means(it):
                    c = it.i + 1
                    k = it.slot
                    dve.wait_ge(bk_done, c)
                    dve.wait_ge(rc_stored[k], 16 * it.use)
                    if not (type(it.i) is int and it.i < 2):
                        dve.wait_ge(mean_done, it.i - 1)
                    nc.vector.reciprocal(rc[:, k, :].unsqueeze(2), p_b[:, :, F:EK]).then_inc(rc_done, 1)
                    dve.wait_ge(rc_done, c)
                    dve.wait_ge(mean_stored[k], 16 * it.use)
                    nc.vector.tensor_tensor(mean[:, k, :, :], p_b[:, :, 0:F], spread(rc[:, k, :], F), ALU.mult).then_inc(mean_done, 1)

                def body(it, left):
                    norm(it)
                    if not (type(it.i) is int and it.i == 0):
                        scan(it.ahead(-1))
                    normed(it)
                    if not (type(it.i) is int and it.i == 0):
                        means(it.ahead(-1))
                run_loop(dve, NI, body, 2)
                end = It((NI - 1) // 2, (NI - 1) % 2)
                scan(end)
                means(end)


def h_d_view(h_v):
    return h_v.rearrange("i p q (j f) -> i q p j f", f=F)


def second_hop(nc, sem, gate, pool_gate, row_v, meta_v, h_v, f_v, a_v, rc_d, a_tab, keep_d, node_tab, ident, w1, b1c, w2g):
    ctx = ExitStack()
    with ctx:
        def sb(name, shape, dt=f32):
            return ctx.enter_context(nc.sbuf_tensor(name, shape, dt))

        def ps(name, shape):
            return ctx.enter_context(nc.psum_tensor(name, shape, f32))

        row_b = sb("h2_row", [P, 2, Q, J], i32)
        meta_b = sb("h2_meta", [P, 2, Q, 3 * J], i32)
        stage = sb("h2_stage", [P, 2, T, LK])
        keep_b = sb("h2_keep", [F, 2, ITE])
        node_b = sb("h2_node", [P, 2, T, RW])
        rows = sb("h2_rows", [P, Q, P])
        hid = sb("h2_hid", [P, Q, P])
        acc = sb("h2_acc", [F, 2, ITE])
        rc = sb("h2_rc", [P, 2, T])
        p_t = ps("h2_pt", [P, CHUNK])[:, 0:Q * P].rearrange("k (q e) -> k q e", q=Q)
        p_h = ps("h2_ph", [P, CHUNK])[:, 0:Q * P].rearrange("k (q e) -> k q e", q=Q)
        p_g = ps("h2_pg", [F, Q, CHUNK])
        p_b = ps("h2_pb", [P, CHUNK])[:, 0:T * F].rearrange("p (t f) -> p t f", t=T)

        row_full, meta_full, h_full, g_full, keep_full, node_full, rc_full, sent = (
            [sem(f"h2_{n}{k}") for k in range(2)] for n in ("row_full", "meta_full", "h_full", "g_full", "keep_full", "node_full", "rc_full", "sent"))
        cleared, tr_done, rows_done, hid_ready, hid_done, g_ready, acc_done, bk_done, mean_done = (
            sem(f"h2_{n}") for n in ("cleared", "tr_done", "rows_done", "hid_ready", "hid_done", "g_ready", "acc_done", "bk_done", "mean_done"))
        uses = [(NI + 1) // 2, NI // 2]
        hc, fc, ac = Chunks(h_d_view(h_v)), Chunks(h_d_view(f_v)), Chunks(h_d_view(a_v))

        with nc.Block() as block:
            @block.sync
            def _(sp):
                def load_in(it):
                    k = it.slot
                    sp.dma_start(row_b[:, k, :, :], row_v[it.i]).then_inc(row_full[k], 16)
                    for q in range(Q):
                        sp.dma_start(stage[:, k, q * J:(q + 1) * J, 0:F], hc[it.i][q]).then_inc(h_full[k], 16)
                    sp.dma_start(keep_b[:, k, :], row_slice(keep_d, it.i, F)).then_inc(keep_full[k], 16)

                def load_out(it):
                    k = it.slot
                    sp.dma_start(meta_b[:, k, :, :], meta_v[it.i]).then_inc(meta_full[k], 16)
                    sp.dma_start(rc[:, k, :], rc_d[it.i]).then_inc(rc_full[k], 16)
                    for q in range(Q):
                        sp.dma_start(node_b[:, k, q * J:(q + 1) * J, 0:F], fc[it.i][q]).then_inc(node_full[k], 16)
                        sp.dma_start(node_b[:, k, q * J:(q + 1) * J, F:2 * F], ac[it.i][q]).then_inc(node_full[k], 16)
                for k in range(2):
                    load_in(It(0, k))
                    load_out(It(0, k))

                def body(it, left):
                    if left >= 2:
                        sp.wait_ge(g_full[it.slot], 16 * T * (it.use + 1))
                        sp.wait_ge(tr_done, it.i + 1)
                        sp.wait_ge(acc_done, it.i + 1)
                        load_in(it.ahead(2))
                        sp.wait_ge(sent[it.slot], 16 * T * (it.use + 1))
                        load_out(it.ahead(2))
                run_loop(sp, NI, body, 2)

            @block.gpsimd
            def _(pool):
                def gather(it):
                    k = it.slot
                    pool.wait_ge(row_full[k], 16 * (it.use + 1))
                    if not (type(it.i) is int and it.i < 2):
                        pool.wait_ge(tr_done, it.i - 1)
                    pool.sem_inc(pool_gate, 1)
                    for t in range(T):
                        pool.indirect_dma_start(stage[:, k, t, F:2 * F], None, a_tab,
                                                bass.IndirectOffsetOnAxis(ap=row_b[:, k, t // J, t % J:t % J + 1], axis=0)) \
                            .then_inc(g_full[k], 16)

                def scatter(it):
                    k = it.slot
                    pool.wait_ge(meta_full[k], 16 * (it.use + 1))
                    pool.wait_ge(node_full[k], 64 * (it.use + 1))
                    pool.wait_ge(mean_done, it.i + 1)
                    pool.sem_inc(pool_gate, 1)
                    for t in range(T):
                        pool.indirect_dma_start(node_tab, bass.IndirectOffsetOnAxis(ap=meta_b[:, k, t // J, J + t % J:J + t % J + 1], axis=0),
                                                node_b[:, k, t, :], None).then_inc(sent[k], 16)

                def body(it, left):
                    gather(it)
                    if not (type(it.i) is int and it.i == 0):
                        scatter(it.ahead(-1))
                pool.wait_ge(cleared, 1)
                run_loop(pool, NI, body, 2)
                scatter(It((NI - 1) // 2, (NI - 1) % 2))
                for k in range(2):
                    pool.wait_ge(sent[k], 16 * T * uses[k])

            @block.scalar
            def _(act):
                def body(it, left):
                    c = it.i + 1
                    first = type(it.i) is int and it.i == 0
                    act.wait_ge(tr_done, c)
                    if not first:
                        act.wait_ge(hid_ready, it.i)
                    act.activation(rows[:, :, :], p_t[:, :, :], ACT.Copy).then_inc(rows_done, 1)
                    act.wait_ge(hid_ready, c)
                    if not first:
                        act.wait_ge(g_ready, it.i)
                    act.activation(hid[:, :, :], p_h[:, :, :], ACT.Relu, bias=b1c[:, :]).then_inc(hid_done, 1)
                run_loop(act, NI, body, 2)

            @block.tensor
            def _(pe):
                def forth(it):
                    c = it.i + 1
                    first = type(it.i) is int and it.i == 0
                    pe.wait_ge(g_full[it.slot], 16 * T * (it.use + 1))
                    pe.wait_ge(h_full[it.slot], 32 * (it.use + 1))
                    if not first:
                        pe.wait_ge(rows_done, it.i)
                    pe.sem_inc(gate, 1)
                    for q in range(Q):
                        last = nc.tensor.transpose(p_t[:, q, :], stage[:, it.slot, q * J:(q + 1) * J, :].rearrange("p j k -> p (j k)"), ident[:, :])
                    last.then_inc(tr_done, 1)
                    pe.wait_ge(rows_done, c)
                    if not first:
                        pe.wait_ge(hid_done, it.i)
                    pe.sem_inc(gate, 1)
                    nc.tensor.matmul(p_h[:, :, :], w1[:, :], rows[:, :, :], start=True, stop=True).then_inc(hid_ready, 1)
                    pe.wait_ge(hid_done, c)
                    if not first:
                        pe.wait_ge(acc_done, it.i)
                    pe.sem_inc(gate, 1)
                    for q in range(Q):
                        for j in range(J):
                            last = nc.tensor.matmul(p_g[:, q, j:CHUNK:J], w2g[:, j, :], hid[:, q, :], start=True, stop=True)
                    last.then_inc(g_ready, 1)

                def back(it):
                    pe.wait_ge(acc_done, it.i + 1)
                    if not (type(it.i) is int and it.i == 0):
                        pe.wait_ge(mean_done, it.i)
                    pe.sem_inc(gate, 1)
                    for t in range(T):
                        q, j = t // J, t % J
                        last = nc.tensor.transpose(p_b[:, t, :], acc[:, it.slot, q * CHUNK + j:(q + 1) * CHUNK:J], ident[0:F, 0:F])
                    last.then_inc(bk_done, 1)

                pe.wait_ge(cleared, 1)

                def body(it, left):
                    forth(it)
                    back(it)
                run_loop(pe, NI, body, 2)

            @block.vector
            def _(dve):
                nc.vector.memset(acc[:, :, :], 0.0).then_inc(cleared, 1)
                dve.wait_ge(cleared, 1)

                def body(it, left):
                    c = it.i + 1
                    first = type(it.i) is int and it.i == 0
                    dve.wait_ge(g_ready, c)
                    dve.wait_ge(keep_full[it.slot], 16 * (it.use + 1))
                    if not first:
                        dve.wait_ge(acc_done, it.i)
                    nc.vector.tensor_tensor_scan(acc[:, it.slot, :], keep_b[:, it.slot, :], p_g[:, :, :].rearrange("k q e -> k (q e)"),
                                                 acc[:, 1 - it.slot, ITE - 1:ITE], ALU.mult, ALU.add).then_inc(acc_done, 1)
                    dve.wait_ge(bk_done, c)
                    dve.wait_ge(rc_full[it.slot], 16 * (it.use + 1))
                    dve.wait_ge(sent[it.slot], 16 * T * it.use)
                    nc.vector.tensor_tensor(node_b[:, it.slot, :, 2 * F:RW], p_b[:, :, :], spread(rc[:, it.slot, :], F), ALU.mult).then_inc(mean_done, 1)
                run_loop(dve, NI, body, 2)


def node_pass(nc, sem, gate, pool_gate, x, node_tab, out, ident, ones_row, w1, b1c, w2n, b2r):
    K = NK
    KG = K // G
    whole = N // (P * K)
    rest = (N - whole * P * K) // K
    xv = x[0:whole * P * K, :].rearrange("(i p k) f -> i p (k f)", p=P, k=K)
    ov = out[0:whole * P * K, :].rearrange("(i p k) f -> i p (k f)", p=P, k=K)
    nv = node_tab[0:whole * P * K, :].rearrange("(i p k) f -> i p (k f)", p=P, k=K)
    tail_of = lambda t: t[whole * P * K:N, :].rearrange("(p k) f -> p (k f)", k=K)
    ctx = ExitStack()
    with ctx:
        def sb(name, shape, dt=f32):
            return ctx.enter_context(nc.sbuf_tensor(name, shape, dt))

        def ps(name, shape):
            return ctx.enter_context(nc.psum_tensor(name, shape, f32))

        x_b = sb("n_x", [P, 2, K, F])
        t_b = sb("n_t", [P, 2, K, RW])
        x1 = sb("n_x1", [P, 2, K, F])
        x2 = sb("n_x2", [P, 2, K, F])
        stage = sb("n_stage", [P, 2, K, LK])
        sm, nm, vs, ve, lnv, rs = (sb(f"n_{n}", [P, K]) for n in ("sm", "nm", "vs", "ve", "lnv", "rs"))
        cc, sq = (sb(f"n_{n}", [P, K, F]) for n in ("cc", "sq"))
        rows = sb("n_rows", [P, 2, KG * P])
        hid = sb("n_hid", [P, 2, KG * P])
        o_b = sb("n_o", [P, 2, K, F])
        p_t = ps("n_pt", [P, KG * P])
        p_h = ps("n_ph", [P, KG * P])
        p_o = ps("n_po", [P, K, F])

        x_full, t_full, stored = ([sem(f"n_{n}{k}") for k in range(2)] for n in ("x_full", "t_full", "stored"))
        ls = layernorm_sems(sem, "n")
        x1_done, x2_done, mean_done, tr_done, rows_done, hid_ready, hid_done, o_ready, o_done = (
            sem(f"n_{n}") for n in ("x1_done", "x2_done", "mean_done", "tr_done", "rows_done", "hid_ready", "hid_done", "o_ready", "o_done"))
        uses = [(NT + 1) // 2, NT // 2]

        def is_last(it):
            return type(it.i) is int and it.i == NT - 1

        with nc.Block() as block:
            @block.sync
            def _(sp):
                def load(it):
                    k = it.slot
                    if is_last(it):
                        sp.dma_start(x_b[0:rest, k, :, :].rearrange("p k f -> p (k f)"), tail_of(x)).then_inc(x_full[k], 16)
                        sp.dma_start(t_b[0:rest, k, :, :].rearrange("p k f -> p (k f)"), tail_of(node_tab)).then_inc(t_full[k], 16)
                    else:
                        sp.dma_start(x_b[:, k, :, :].rearrange("p k f -> p (k f)"), xv[it.i]).then_inc(x_full[k], 16)
                        sp.dma_start(t_b[:, k, :, :].rearrange("p k f -> p (k f)"), nv[it.i]).then_inc(t_full[k], 16)
                load(It(0, 0))
                load(It(0, 1))

                def body(it, left):
                    if left >= 2:
                        sp.wait_ge(x2_done, it.i + 1)
                        sp.wait_ge(mean_done, it.i + 1)
                        load(it.ahead(2))
                run_loop(sp, NT, body, 3)

            @block.scalar
            def _(act):
                def tops(it):
                    c = it.i + 1
                    layernorm_rstd(nc, act, ls, c, ve[:, :], lnv[:, :], rs[:, :])
                    act.wait_ge(tr_done, c)
                    if not (type(it.i) is int and it.i < 2):
                        act.wait_ge(hid_ready, it.i - 1)
                    act.activation(rows[:, it.slot, :], p_t[:, :], ACT.Copy).then_inc(rows_done, 1)
                    act.wait_ge(hid_ready, c)
                    if not (type(it.i) is int and it.i < 2):
                        act.wait_ge(o_ready, it.i - 1)
                    act.activation(hid[:, it.slot, :], p_h[:, :], ACT.Relu, bias=b1c[:, :]).then_inc(hid_done, 1)

                def store(it):
                    act.wait_ge(o_done, it.i + 1)
                    k = it.slot
                    if is_last(it):
                        act.dma_start(tail_of(out), o_b[0:rest, k, :, :].rearrange("p k f -> p (k f)")).then_inc(stored[k], 16)
                    else:
                        act.dma_start(ov[it.i], o_b[:, k, :, :].rearrange("p k f -> p (k f)")).then_inc(stored[k], 16)

                def body(it, left):
                    tops(it)
                    if not (type(it.i) is int and it.i == 0):
                        store(it.ahead(-1))
                run_loop(act, NT, body, 3)
                store(It((NT - 1) // 2, (NT - 1) % 2))
                for k in range(2):
                    act.wait_ge(stored[k], 16 * uses[k])

            @block.gpsimd
            def _(pool):
                def body(it, left):
                    c = it.i + 1
                    k = it.slot
                    pool.wait_ge(t_full[k], 16 * (it.use + 1))
                    if not (type(it.i) is int and it.i < 2):
                        pool.wait_ge(tr_done, it.i - 1)
                        pool.wait_ge(o_done, it.i - 1)
                    pool.sem_inc(pool_gate, 1)
                    nc.gpsimd.tensor_copy(stage[:, k, :, F:2 * F], t_b[:, k, :, F:2 * F]).then_inc(mean_done, 1)
                    pool.wait_ge(x1_done, c)
                    pool.sem_inc(pool_gate, 1)
                    nc.gpsimd.tensor_tensor(x2[:, k, :, :], x1[:, k, :, :], t_b[:, k, :, 2 * F:RW], ALU.add).then_inc(x2_done, 1)
                run_loop(pool, NT, body, 3)

            @block.tensor
            def _(pe):
                def hidden(it):
                    c = it.i + 1
                    first = type(it.i) is int and it.i == 0
                    pe.wait_ge(ls["h"], c)
                    pe.wait_ge(mean_done, c)
                    if not first:
                        pe.wait_ge(rows_done, it.i)
                    pe.sem_inc(gate, 1)
                    for t in range(KG):
                        last = nc.tensor.transpose(p_t[:, t * P:(t + 1) * P], stage[:, it.slot, t * G:(t + 1) * G, :].rearrange("p g k -> p (g k)"), ident[:, :])
                    last.then_inc(tr_done, 1)
                    pe.wait_ge(rows_done, c)
                    if not first:
                        pe.wait_ge(hid_done, it.i)
                    pe.sem_inc(gate, 1)
                    for t in range(KG * P // CHUNK):
                        cols = slice(t * CHUNK, (t + 1) * CHUNK)
                        last = nc.tensor.matmul(p_h[:, cols], w1[:, :], rows[:, it.slot, cols], start=True, stop=True)
                    last.then_inc(hid_ready, 1)

                def finish(it):
                    pe.wait_ge(hid_done, it.i + 1)
                    if not (type(it.i) is int and it.i == 0):
                        pe.wait_ge(o_done, it.i)
                    pe.sem_inc(gate, 1)
                    nc.tensor.matmul(p_o[:, :, :].rearrange("p k f -> p (k f)"), ones_row[:, :], b2r[:, :], start=True, stop=False)
                    for t in range(KG):
                        last = nc.tensor.matmul(p_o[:, t * G:(t + 1) * G, :].rearrange("p g f -> p (g f)"), hid[:, it.slot, t * P:(t + 1) * P], w2n[:, :],
                                                start=False, stop=(t == KG - 1))
                    last.then_inc(o_ready, 1)

                def body(it, left):
                    hidden(it)
                    finish(it)
                run_loop(pe, NT, body, 3)

            @block.vector
            def _(dve):
                def norm(it):
                    c = it.i + 1
                    k = it.slot
                    dve.wait_ge(x_full[k], 16 * (it.use + 1))
                    dve.wait_ge(t_full[k], 16 * (it.use + 1))
                    if not (type(it.i) is int and it.i < 2):
                        dve.wait_ge(x2_done, it.i - 1)
                        dve.wait_ge(tr_done, it.i - 1)
                    nc.vector.tensor_tensor(x1[:, k, :, :], x_b[:, k, :, :], t_b[:, k, :, 0:F], ALU.add).then_inc(x1_done, 1)
                    dve.wait_ge(x1_done, c)
                    if not (type(it.i) is int and it.i == 0):
                        dve.wait_ge(ls["h"], it.i)
                    layernorm_stats(nc, dve, ls, c, x1[:, k, :, :], sm[:, :], nm[:, :], cc[:, :, :], sq[:, :, :], vs[:, :], ve[:, :])
                    layernorm_out(nc, dve, ls, c, stage[:, k, :, 0:F], cc[:, :, :], rs[:, :])

                def finish(it):
                    k = it.slot
                    dve.wait_ge(o_ready, it.i + 1)
                    dve.wait_ge(x2_done, it.i + 1)
                    dve.wait_ge(stored[k], 16 * it.use)
                    nc.vector.tensor_tensor(o_b[:, k, :, :], p_o[:, :, :], x2[:, k, :, :], ALU.add).then_inc(o_done, 1)

                def body(it, left):
                    norm(it)
                    if not (type(it.i) is int and it.i == 0):
                        finish(it.ahead(-1))
                run_loop(dve, NT, body, 3)
                finish(It((NT - 1) // 2, (NT - 1) % 2))


_INS = ["x", "src", "dst", "edge_attr_16", "L0_gnn_W_msg", "L0_gnn_b_msg", "L0_gnn_W_attn", "L0_gnn_b_attn",
        "L1_gnn_W1_l", "L1_gnn_b1", "L1_gnn_W1_r", "L1_gnn_W2_l", "L1_gnn_b2", "L1_gnn_W2_r"]


def kernel(**inputs):
    import numpy as _np
    import concourse.bacc as _bacc
    from concourse import mybir as _mybir
    from concourse.bass_utils import run_bass_kernel_spmd as _run

    nc = _bacc.Bacc("TRN2", target_bir_lowering=False, num_devices=1)
    arrays, args = {}, []
    for name in _INS:
        arr = _np.ascontiguousarray(inputs[name])
        arrays[f"in_{name}"] = arr
        args.append(nc.dram_tensor(f"in_{name}", arr.shape, _mybir.dt.from_np(arr.dtype), kind="ExternalInput").ap())
    args.append(nc.dram_tensor("out_0", (N, F), _mybir.dt.float32, kind="ExternalOutput").ap())
    gnn_program(nc, *args)
    r = _run(nc, [arrays], core_ids=[0])
    return r.results[0]["out_0"]
```

```python
from contextlib import ExitStack

import concourse.bass as bass
from concourse import mybir
import numpy as np

f32 = mybir.dt.float32
bf16 = mybir.dt.bfloat16
i32 = mybir.dt.int32
ALU = mybir.AluOpType
ACT = mybir.ActivationFunctionType
AX = mybir.AxisListType

P = 128
N, E, F = 100000, 50000, 16
HID = 32
CH = F * F
CHUNK = 512
J = CHUNK // P
Q = 2
T = Q * J
ITE = Q * CHUNK
NI = -(-E // ITE)
EP = NI * ITE
NC = EP // CHUNK
EK = F + 1
X_PARTS = (0, 0, 0, 1, 1, 2)
W_PARTS = (0, 1, 2, 0, 1, 0)
NP = len(X_PARTS)
XK = NP * EK
HS = 3 * F
LK = 2 * F
G = P // LK
RW = 3 * F
NK = 32
NT = -(-N // (P * NK))
MW = 4 * J
XW = F + 1
EARLY = 28
HANDED = 27
PIECES = 8
NW = 125
BIG = 1.0e30
EPS = 1.0e-5


class It:

    def __init__(self, use, slot, depth=2):
        self.use, self.slot, self.depth = use, slot, depth
        self.i = depth * use + slot

    def ahead(self, d):
        more, slot = divmod(self.slot + d, self.depth)
        return It(self.use + more if more else self.use, slot, self.depth)


def run_loop(eng, total, body, tail, head=3, depth=2, start=0, end=None):
    end = total if end is None else end

    def nth(n, rounds=0):
        return It(rounds + n // depth, n % depth, depth)

    loops = (end - start - head - (tail if end == total else 0)) // depth
    looped = start + head
    for n in range(start, looped):
        body(nth(n), tail)
    with eng.Fori(0, loops) as k:
        for n in range(looped, looped + depth):
            body(nth(n, k), tail)
    for n in range(looped + depth * loops, end):
        body(nth(n), min(tail, total - 1 - n))


def edge_view(t):
    return t[0:EP, :].rearrange("(i q p j) f -> i p q (j f)", q=Q, p=P, j=J)


def spread(ap, n):
    return ap.unsqueeze(2).broadcast_to([ap.shape[0], ap.shape[1], n])


def gnn_program(nc, x, src, dst, efeat, w_msg, b_msg, w_attn, b_attn, w1l, b1, w1r, w2l, b2, w2r, out):
    meta = nc.dram_tensor("meta", (NC * P, MW), i32).ap()
    keep_d = nc.dram_tensor("keep_d", (1, EP), f32).ap()
    mask_d = nc.dram_tensor("mask_d", (1, EP), f32).ap()
    rc_d = nc.dram_tensor("rc_d", (NI, P, T), f32).ap()
    wide = nc.dram_tensor("wide", ((N + EP) * XW, 1), f32).ap()
    xs_d = nc.dram_tensor("xs_d", (NI, P, T * XW), f32).ap()
    h_d = nc.dram_tensor("h_d", (EP, F), f32).ap()
    f_tab = nc.dram_tensor("f_tab", (EP + P, F), f32).ap()
    a_tab = nc.dram_tensor("a_tab", (EP + P, F), f32).ap()
    node_tab = nc.dram_tensor("node_tab", (N + EP, RW), f32).ap()

    meta_v = meta.rearrange("(i q p) f -> i p q f", q=Q, p=P)
    h_v = edge_view(h_d)
    f_v, a_v = edge_view(f_tab), edge_view(a_tab)

    with ExitStack() as ctx:
        def sb(name, shape, dt=f32):
            return ctx.enter_context(nc.sbuf_tensor(name, shape, dt))

        def sem(name):
            return ctx.enter_context(nc.semaphore(name))

        gate, pool_gate = sem("gate"), sem("pool_gate")
        m_loaded = sem("m_loaded")
        ident = sb("ident", [P, P])
        identb = sb("identb", [P, P], bf16)
        ones3 = sb("ones3", [3, P], bf16)
        in_sel = sb("in_sel", [HS, CH], bf16)
        out_sum = sb("out_sum", [P, F])
        wam = sb("wam", [XK, 2, CH], bf16)
        w1 = sb("w1", [P, P])
        b1c = sb("b1c", [P, 1])
        w2g = sb("w2g", [P, G, F])
        w2n = sb("w2n", [P, G * F])
        b2r = sb("b2r", [3, NK * F], bf16)

        setup(nc, m_loaded, x, src, dst, meta, keep_d, mask_d, f_tab, a_tab,
              w_msg, b_msg, w_attn, b_attn, w1l, b1, w1r, w2l, b2, w2r,
              ident, identb, ones3, in_sel, out_sum, wam, w1, b1c, w2g, w2n, b2r)
        edge_softmax(nc, sem, gate, pool_gate, x, efeat, meta_v, xs_d, wide, f_v, mask_d, node_tab,
                     identb, in_sel, out_sum, wam)
        first_hop(nc, sem, gate, pool_gate, xs_d, h_v, a_v, rc_d, f_tab, keep_d, ident)
        second_hop(nc, sem, gate, pool_gate, xs_d, meta_v, h_v, f_v, a_v, rc_d, a_tab, keep_d, node_tab, ident, w1, b1c, w2g)
        node_pass(nc, sem, gate, pool_gate, x, node_tab, out, ident, ones3, w1, b1c, w2n, b2r)


def setup(nc, m_loaded, x, src, dst, meta, keep_d, mask_d, f_tab, a_tab,
          w_msg, b_msg, w_attn, b_attn, w1l, b1, w1r, w2l, b2, w2r,
          ident, identb, ones3, in_sel, out_sum, wam, w1, b1c, w2g, w2n, b2r):
    full = E // CHUNK
    rest = E - full * CHUNK
    with ExitStack() as ctx:
        used = []

        def sb(name, shape, dt=f32):
            return ctx.enter_context(nc.sbuf_tensor(name, shape, dt))

        def sem(name):
            used.append(ctx.enter_context(nc.semaphore(name)))
            return used[-1]

        dstn = sb("dstn", [NC, CHUNK + 2], i32)
        srcn = sb("srcn", [NC, CHUNK], i32)
        keep = sb("keep", [NC, CHUNK])
        mask = sb("mask", [NC, CHUNK])
        wf = sb("wf", [EK, 2, CH])
        wp = sb("wp", [EK, 3, 2, CH], bf16)
        sel = sb("sel", [F, CH], bf16)
        is_end = sb("is_end", [NC, CHUNK])
        edge_no = sb("edge_no", [NC, CHUNK], i32)
        off = sb("off", [NC, CHUNK])
        b2f = sb("b2f", [1, NK * F])
        b2p = sb("b2p", [1, 3, NK * F], bf16)
        metan = sb("metan", [NC, P, 4, J], i32)
        zrow = sb("zrow", [P, F])

        filled, loaded, w_loaded, iotas, selected = (sem(n) for n in ("filled", "loaded", "w_loaded", "iotas", "selected"))
        v_keep, v_end, v_off, v_offn, v_prod, v_row, v_idn, v_out, v_part, v_left = (
            sem(n) for n in ("v_keep", "v_end", "v_off", "v_offn", "v_prod", "v_row", "v_idn", "v_out", "v_part", "v_left"))
        v_b2, v_b2left, b2_loaded, l_loaded = (sem(n) for n in ("v_b2", "v_b2left", "b2_loaded", "l_loaded"))
        stored, stacked = sem("setup_stored"), sem("stacked")

        def layer_weights(groups):
            for g in groups:
                lo = g * LK
                yield w1[lo:lo + F, lo:lo + HID], w1r
                yield w1[lo + F:lo + LK, lo:lo + HID], w1l
                yield b1c[lo:lo + HID, :], b1.rearrange("(k o) -> k o", o=1)
                yield w2g[lo:lo + HID, g, :], w2l
                yield w2n[lo:lo + HID, g * F:(g + 1) * F], w2r

        ctx.enter_context(nc.allow_non_contiguous_dma(reason="one edge before and after each chunk"))
        with nc.Block() as block:
            @block.sync
            def _(sp):
                sp.wait_ge(filled, 2)
                sp.dma_start(dstn[0:full, 1:CHUNK + 1], dst[0:full * CHUNK].rearrange("(c e) -> c e", e=CHUNK)).then_inc(loaded, 16)
                sp.dma_start(dstn[full:NC, 1:rest + 1], dst[full * CHUNK:E].rearrange("(c e) -> c e", c=1)).then_inc(loaded, 16)
                sp.dma_start(dstn[1:NC, 0:1], dst[CHUNK - 1:CHUNK * (NC - 1):CHUNK].rearrange("(c e) -> c e", e=1)).then_inc(loaded, 16)
                sp.dma_start(dstn[0:NC - 1, CHUNK + 1:CHUNK + 2], dst[CHUNK:CHUNK * (NC - 1) + 1:CHUNK].rearrange("(c e) -> c e", e=1)).then_inc(loaded, 16)
                sp.dma_start(srcn[0:full, :], src[0:full * CHUNK].rearrange("(c e) -> c e", e=CHUNK)).then_inc(loaded, 16)
                sp.dma_start(srcn[full:NC, 0:rest], src[full * CHUNK:E].rearrange("(c e) -> c e", c=1)).then_inc(loaded, 16)
                sp.wait_ge(filled, 6)
                sp.dma_start(f_tab[EP:EP + P, :], zrow[:, :]).then_inc(stored, 16)
                sp.dma_start(a_tab[EP:EP + P, :], zrow[:, :]).then_inc(stored, 16)
                sp.wait_ge(v_keep, 1)
                sp.wait_ge(v_out, 5)
                sp.dma_start(meta.rearrange("(c p) f -> c (p f)", p=P), metan[:, :, :, :].rearrange("c p f j -> c (p f j)")).then_inc(stored, 16)
                sp.dma_start(keep_d.rearrange("o (c e) -> (o c) e", e=CHUNK), keep[:, :]).then_inc(stored, 16)
                sp.dma_start(mask_d.rearrange("o (c e) -> (o c) e", e=CHUNK), mask[:, :]).then_inc(stored, 16)
                sp.wait_ge(stored, 16 * 5)

            @block.scalar
            def _(act):
                loads = [(wf[0:F, 0, :], w_attn), (wf[F:EK, 0, :], b_attn.rearrange("(o c) -> o c", o=1)),
                         (wf[0:F, 1, :], w_msg), (wf[F:EK, 1, :], b_msg.rearrange("(o c) -> o c", o=1))]
                for to, frm in loads:
                    act.dma_start(to, frm).then_inc(w_loaded, 16)
                act.dma_start(b2f[:, :].rearrange("o (k f) -> o k f", f=F), b2.rearrange("(o k f) -> o k f", o=1, k=1).broadcast_to([1, NK, F])).then_inc(b2_loaded, 16)
                act.wait_ge(v_part, 3)
                for k, part in enumerate(W_PARTS):
                    act.dma_start(wam[k * EK:(k + 1) * EK, :, :].rearrange("k w c -> k (w c)"), wp[:, part, :, :].rearrange("k w c -> k (w c)")) \
                        .then_inc(stacked, 16)
                act.wait_ge(v_idn, 3)
                for k in range(3):
                    act.dma_start(in_sel[k * F:(k + 1) * F, :], sel[:, :]).then_inc(stacked, 16)
                act.wait_ge(v_b2, 3)
                for k in range(3):
                    act.dma_start(b2r[k:k + 1, :], b2p[:, k, :]).then_inc(stacked, 16)
                act.wait_ge(filled, 6)
                for to, frm in layer_weights([0]):
                    act.dma_start(to, frm).then_inc(l_loaded, 16)
                act.wait_ge(stacked, 16 * (NP + 6))
                act.wait_ge(l_loaded, 16 * 5)

            @block.gpsimd
            def _(pool):
                nc.gpsimd.iota(edge_no[:, :], [[1, CHUNK]], base=0, channel_multiplier=CHUNK).then_inc(iotas, 1)
                nc.gpsimd.memset(ident[:, :], 0.0).then_inc(selected, 1)
                pool.wait_ge(selected, 1)
                nc.gpsimd.affine_select(out=ident[:, :], in_=ident[:, :], compare_op=ALU.not_equal, fill=1.0,
                                        base=0, pattern=[[-1, P]], channel_multiplier=1).then_inc(selected, 1)
                pool.wait_ge(filled, 6)
                for to, frm in layer_weights(range(1, G)):
                    pool.dma_start(to, frm).then_inc(m_loaded, 16)
                pool.wait_ge(m_loaded, 16 * 5 * (G - 1))

            @block.vector
            def _(dve):
                nc.vector.memset(dstn[:, :], -2).then_inc(filled, 1)
                nc.vector.memset(srcn[:, :], 0).then_inc(filled, 1)
                nc.vector.memset(w1[:, :], 0.0).then_inc(filled, 1)
                nc.vector.memset(w2g[:, :, :], 0.0).then_inc(filled, 1)
                nc.vector.memset(w2n[:, :], 0.0).then_inc(filled, 1)
                nc.vector.memset(zrow[:, :], 0.0).then_inc(filled, 1)
                nc.vector.memset(ones3[:, :], 1.0)
                dve.wait_ge(w_loaded, 16 * 4)
                for part in range(3):
                    nc.vector.tensor_copy(wp[:, part, :, :], wf[:, :, :]).then_inc(v_part, 1)
                    dve.wait_ge(v_part, part + 1)
                    if part < 2:
                        nc.vector.tensor_tensor(wf[:, :, :], wf[:, :, :], wp[:, part, :, :], ALU.subtract).then_inc(v_left, 1)
                        dve.wait_ge(v_left, part + 1)
                dve.wait_ge(selected, 2)
                nc.vector.tensor_copy(identb[:, :], ident[:, :]).then_inc(v_idn, 1)
                nc.vector.tensor_reduce(out_sum[:, :], ident[:, :].rearrange("p (i o) -> p o i", o=F), AX.X, ALU.add).then_inc(v_idn, 1)
                nc.vector.tensor_copy(sel[:, :].rearrange("k (i o) -> k i o", o=F), spread(ident[0:F, 0:F], F)).then_inc(v_idn, 1)
                dve.wait_ge(loaded, 16 * 6)
                dve.wait_ge(iotas, 1)
                here = dstn[:, 1:CHUNK + 1]
                nc.vector.tensor_tensor(keep[:, :], here, dstn[:, 0:CHUNK], ALU.is_equal).then_inc(v_keep, 1)
                nc.vector.tensor_tensor(is_end[:, :], here, dstn[:, 2:CHUNK + 2], ALU.not_equal).then_inc(v_end, 1)
                nc.vector.tensor_tensor(off[:, :], here, edge_no[:, :], ALU.subtract).then_inc(v_off, 1)
                dve.wait_ge(v_off, 1)
                nc.vector.tensor_scalar(off[:, :], off[:, :], -float(N), None, ALU.add).then_inc(v_offn, 1)
                dve.wait_ge(v_offn, 1)
                dve.wait_ge(v_end, 1)
                nc.vector.tensor_tensor(off[:, :], off[:, :], is_end[:, :], ALU.mult).then_inc(v_prod, 1)
                dve.wait_ge(v_prod, 1)
                nc.vector.tensor_tensor(off[:, :], off[:, :], edge_no[:, :], ALU.add).then_inc(v_row, 1)
                dve.wait_ge(v_row, 1)
                fold = lambda ap: ap.rearrange("c (p j) -> c p j", j=J)
                nc.vector.tensor_scalar(metan[:, :, 1, :], fold(off[:, :]), float(N), None, ALU.add).then_inc(v_out, 1)
                nc.vector.tensor_scalar(metan[:, :, 3, :], fold(off[:, :]), float(XW), float(N * XW + F), ALU.mult, ALU.add).then_inc(v_out, 1)
                nc.vector.tensor_copy(metan[:, :, 0, :], fold(srcn[:, :])).then_inc(v_out, 1)
                nc.vector.tensor_copy(metan[:, :, 2, :], fold(edge_no[:, :])).then_inc(v_out, 1)
                dve.wait_ge(v_end, 1)
                nc.vector.tensor_scalar(mask[:, :], is_end[:, :], -BIG, None, ALU.mult).then_inc(v_out, 1)
                dve.wait_ge(b2_loaded, 16)
                for part in range(3):
                    nc.vector.tensor_copy(b2p[:, part, :], b2f[:, :]).then_inc(v_b2, 1)
                    dve.wait_ge(v_b2, part + 1)
                    if part < 2:
                        nc.vector.tensor_tensor(b2f[:, :], b2f[:, :], b2p[:, part, :], ALU.subtract).then_inc(v_b2left, 1)
                        dve.wait_ge(v_b2left, part + 1)
        with nc.Block() as block:
            @block.sync
            def _(sp):
                for one in used:
                    sp.sem_clear(one)


def layernorm_sems(sem, tag):
    return {k: sem(f"{tag}_{k}") for k in ("sum", "mean", "cent", "sq", "sqsum", "var", "ln", "rstd", "h")}


def layernorm_steps(nc, dve, s, sm, nm, cc, sq, vs, ve):
    def sum_of(n, rows):
        nc.vector.tensor_reduce(sm, rows, AX.X, ALU.add).then_inc(s["sum"], 1)

    def mean_of(n, rows):
        dve.wait_ge(s["sum"], n)
        nc.vector.tensor_scalar(nm, sm, -1.0 / F, None, ALU.mult).then_inc(s["mean"], 1)

    def centre(n, rows):
        dve.wait_ge(s["mean"], n)
        nc.vector.tensor_tensor(cc, rows, spread(nm, F), ALU.add).then_inc(s["cent"], 1)

    def square(n, rows):
        dve.wait_ge(s["cent"], n)
        nc.vector.tensor_tensor(sq, cc, cc, ALU.mult).then_inc(s["sq"], 1)

    def square_sum(n, rows):
        dve.wait_ge(s["sq"], n)
        nc.vector.tensor_reduce(vs, sq, AX.X, ALU.add).then_inc(s["sqsum"], 1)

    def variance(n, rows):
        dve.wait_ge(s["sqsum"], n)
        nc.vector.tensor_scalar(ve, vs, 1.0 / F, EPS, ALU.mult, ALU.add).then_inc(s["var"], 1)
    return {"sum": sum_of, "mean": mean_of, "cent": centre, "sq": square, "sqsum": square_sum, "var": variance}


def layernorm_stats(nc, dve, s, n, rows, sm, nm, cc, sq, vs, ve):
    steps = layernorm_steps(nc, dve, s, sm, nm, cc, sq, vs, ve)
    for name in ("sum", "mean", "cent", "sq", "sqsum", "var"):
        steps[name](n, rows)


def layernorm_rstd(nc, act, s, n, ve, ln, rs):
    act.wait_ge(s["var"], n)
    nc.scalar.activation(ln, ve, ACT.Ln).then_inc(s["ln"], 1)
    act.wait_ge(s["ln"], n)
    nc.scalar.activation(rs, ln, ACT.Exp, scale=-0.5).then_inc(s["rstd"], 1)


def layernorm_out(nc, dve, s, n, h, cc, rs):
    dve.wait_ge(s["rstd"], n)
    nc.vector.scalar_tensor_tensor(h, cc, 0.0, spread(rs, F), ALU.max, ALU.mult).then_inc(s["h"], 1)


def edge_softmax(nc, sem, gate, pool_gate, x, efeat, meta_v, xs_d, wide, f_v, mask_d, node_tab,
                 identb, in_sel, out_sum, wam):
    wide_rows = wide[0:N * XW, :].rearrange("(n f) o -> n (f o)", f=XW)
    NPN = N // NW // PIECES
    wide_v = wide_rows.rearrange("(p c n) f -> c p (n f)", p=NW, c=PIECES)
    x_v = x.rearrange("(p c n) f -> c p (n f)", p=NW, c=PIECES)
    again = [(NI + 1 - k) // 2 for k in range(2)]
    UN = 2 * Q
    ZN = -(-N // (NI * P))
    zero_v = node_tab[0:NI * P * ZN, :].rearrange("(i p a) f -> i p (a f)", p=P, a=ZN)
    ctx = ExitStack()
    with ctx:
        def sb(name, shape, dt=f32):
            return ctx.enter_context(nc.sbuf_tensor(name, shape, dt))

        def ps(name, shape):
            return ctx.enter_context(nc.psum_tensor(name, shape, f32))

        meta_b = sb("meta_b", [P, 2, Q, MW], i32)
        gx = sb("gx", [P, 2, T, XW])
        piece = sb("piece", [NW, 2, NPN, F])
        piece_w = sb("piece_w", [NW, 2, NPN, XW])
        zeros = sb("zeros", [P, ZN * RW])
        xs_b = sb("xs_b", [P, 2, T, XW])
        ef_b = sb("ef_b", [P, 2, T, F])
        left = sb("left", [P, T, F])
        hf = sb("hf", [P, T, F])
        xstage = sb("xstage", [P, 2, T, NP, EK], bf16)
        hstage = sb("hstage", [P, 2, T, 3, F], bf16)
        mask_b = sb("mask_b", [P, 2, ITE])
        xrows = sb("xrows", [XK, 2, Q, CHUNK], bf16)
        hrows = sb("hrows", [HS, 2, Q, CHUNK], bf16)
        sm, nm, vs, ve, lnv, rs = (sb(f"l0_{n}", [P, T]) for n in ("sm", "nm", "vs", "ve", "lnv", "rs"))
        cc, sq = (sb(f"l0_{n}", [P, T, F]) for n in ("cc", "sq"))
        hb = sb("hb", [P, 2, CHUNK])
        e2 = sb("e2", [P, 2, CHUNK])
        r = sb("r", [P, 2, CHUNK])
        ap = sb("ap", [P, 2, 2, CHUNK])
        w = sb("w", [P, 2, ITE + 1])
        s = sb("s", [P, UN, CHUNK])
        n = sb("n", [P, UN, CHUNK])
        rec = sb("rec", [P, UN, CHUNK])
        ratio = sb("ratio", [P, UN, CHUNK])
        f_b = sb("f_b", [P, 2, Q, J * F])

        p_wa = ps("p_wa", [P, CHUNK])
        p_wm = ps("p_wm", [P, CHUNK])
        p_hb = ps("p_hb", [P, 2, CHUNK])
        p_x = ctx.enter_context(nc.psum_tensor("p_x", [XK, Q, J, P], bf16))
        p_h = ctx.enter_context(nc.psum_tensor("p_h", [HS, Q, J, P], bf16))
        p_fb = ps("p_f", [P, Q, CHUNK])
        p_f = p_fb[:, :, 0:J * F].rearrange("p q (j f) -> p q j f", f=F)

        meta_full, gx_full, xs_stored, pos_done, piece_full, wide_stored, ef_full, xs_full, mask_full, f_stored = (
            [sem(f"{nm}{k}") for k in range(2)] for nm in
            ("meta_full", "gx_full", "xs_stored", "pos_done", "piece_full", "wide_stored", "ef_full", "xs_full",
             "mask_full", "f_stored"))
        none_set, widened, gx_set = sem("none_set"), sem("widened"), sem("gx_set")
        zeros_set, zero_stored, cleared = sem("zeros_set"), sem("zero_stored"), sem("cleared")
        ls = layernorm_sems(sem, "l0")
        tr_done, rows_done = sem("tr_done"), sem("rows_done")
        x_p, x_l, h_p, h_l = ([sem(f"{nm}{k}") for k in range(3)] for nm in ("x_part", "x_left", "h_part", "h_left"))
        hb_ready = sem("u_hb_ready")
        w_ready, hb_done, e2_done, e1_done, w0_done, w_done, d_done, dpos_done, dneg_done = (
            sem(f"u_{k}") for k in ("w_ready", "hb_done", "e2_done", "e1_done", "w0_done", "w_done", "d_done", "pos_dn", "neg_dn"))
        p_done, r_done, s_done, n_done, log_done, rec_done, ratio_done = (
            sem(f"u_{k}") for k in ("p_done", "r_done", "s_done", "n_done", "log_done", "rec_done", "ratio_done"))
        f_sum, f_copied = ([sem(f"{k}{q}") for q in range(Q)] for k in ("f_sum", "f_copied"))

        def unit(it, u):
            return it.i * UN + u + 1

        with nc.Block() as block:
            @block.sync
            def _(sp):
                def load_meta(it):
                    sp.dma_start(meta_b[:, it.slot, :, :], meta_v[it.i]).then_inc(meta_full[it.slot], 16)

                def stores(k, uses_before):
                    def body(it, left):
                        real = It(it.use + k, it.slot)
                        sp.wait_ge(gx_full[it.slot], 16 * T * (real.use + 1 + uses_before[it.slot]))
                        if uses_before[0]:
                            sp.wait_ge(xs_full[it.slot], 16 * (real.use + 1))
                        sp.dma_start(xs_d[real.i], gx[:, it.slot, :, :].rearrange("p t f -> p (t f)")).then_inc(xs_stored[it.slot], 16)
                        if left >= 2:
                            load_meta(real.ahead(2))
                    return body

                for k in range(2):
                    load_meta(It(0, k))
                run_loop(sp, EARLY, stores(0, [0, 0]), 2)

                sp.wait_ge(zeros_set, 1)
                for k in range(2):
                    load_meta(It(0, k))

                def zero_and_load(it, left):
                    sp.dma_start(zero_v[it.i], zeros[:, :]).then_inc(zero_stored, 16)
                    if left >= 2:
                        sp.wait_ge(pos_done[it.slot], 16 * T * (it.use + 1))
                        load_meta(it.ahead(2))
                run_loop(sp, NI, zero_and_load, 2)
                for k in range(2):
                    sp.wait_ge(pos_done[(EARLY + k) % 2], 16 * T * again[(EARLY + k) % 2])
                    load_meta(It(EARLY // 2, k))
                run_loop(sp, NI - EARLY, stores(EARLY // 2, [0, 0]), 2)
                for k in range(2):
                    load_meta(It(0, k))
                run_loop(sp, EARLY, stores(0, again), 2)
                for k in range(2):
                    sp.wait_ge(xs_stored[k], 16 * (again[k] + EARLY // 2))
                sp.wait_ge(zero_stored, 16 * NI)

            @block.gpsimd
            def _(pool):
                nc.gpsimd.iota(piece_w[:, :, :, F:XW].bitcast(i32), [[0, 2], [0, NPN], [0, 1]], base=EP, channel_multiplier=1).then_inc(none_set, 1)
                nc.gpsimd.memset(zeros[:, :], 0.0).then_inc(zeros_set, 1)
                nc.gpsimd.memset(gx[:, :, :, :], 0.0).then_inc(gx_set, 1)
                pool.wait_ge(gx_set, 1)

                def x_alone(it, left):
                    pool.wait_ge(meta_full[it.slot], 16 * (it.use + 1))
                    pool.wait_ge(xs_stored[it.slot], 16 * it.use)
                    pool.sem_inc(pool_gate, 1)
                    for t in range(T):
                        pool.indirect_dma_start(gx[:, it.slot, t, 0:F], None, x,
                                                bass.IndirectOffsetOnAxis(ap=meta_b[:, it.slot, t // J, t % J:t % J + 1], axis=0)) \
                            .then_inc(gx_full[it.slot], 16)
                half = EARLY // 2
                run_loop(pool, EARLY, x_alone, 2)

                for k in range(2):
                    pool.wait_ge(wide_stored[k], 16 * PIECES // 2)

                def scatter(it, left):
                    pool.wait_ge(meta_full[it.slot], 16 * (it.use + 1 + half))
                    pool.sem_inc(pool_gate, 1)
                    for t in range(T):
                        q, j = t // J, t % J
                        pool.indirect_dma_start(wide, bass.IndirectOffsetOnAxis(ap=meta_b[:, it.slot, q, 3 * J + j:3 * J + j + 1], axis=0),
                                                meta_b[:, it.slot, q, 2 * J + j:2 * J + j + 1].bitcast(f32), None) \
                            .then_inc(pos_done[it.slot], 16)
                run_loop(pool, NI, scatter, 2)
                for k in range(2):
                    pool.wait_ge(pos_done[k], 16 * T * again[k])

                def rows_half(real, uses_before, metas_before, h):
                    slot = real.slot
                    if h == 0:
                        pool.wait_ge(meta_full[slot], 16 * (real.use + 1 + metas_before[slot]))
                        pool.wait_ge(xs_stored[slot], 16 * (real.use + uses_before[slot]))
                        pool.sem_inc(pool_gate, 1)
                    for t in range(h * T // 2, (h + 1) * T // 2):
                        pool.indirect_dma_start(gx[:, slot, t, :], None, wide_rows,
                                                bass.IndirectOffsetOnAxis(ap=meta_b[:, slot, t // J, t % J:t % J + 1], axis=0)) \
                            .then_inc(gx_full[slot], 16)

                def ratio_of(i, u):
                    c = i * UN + u + 1
                    pool.wait_ge(rec_done, c)
                    pool.wait_ge(n_done, c)
                    pool.wait_ge(f_sum[u // 2], i)
                    pool.wait_ge(ratio_done, c - 1)
                    pool.sem_inc(pool_gate, 1)
                    nc.gpsimd.tensor_tensor(ratio[:, u, :], n[:, u, :], rec[:, u, :], ALU.mult).then_inc(ratio_done, 1)

                def turn(reals, uses_before, metas_before, i):
                    for m, real in enumerate(reals):
                        for h in range(2):
                            rows_half(real, uses_before, metas_before, h)
                            if i is not None:
                                ratio_of(i, 2 * m + h)

                twice = [2 * again[k] for k in range(2)]
                pairs = (NI - EARLY) // 2
                alone = pairs + half - (NI - HANDED)
                turn([It(half, 0)], [0, 0], again, None)
                for k in range(alone):
                    turn([It(half + k, 1), It(half + k + 1, 0)], [0, 0], again, None)
                with pool.Fori(0, pairs - alone) as k:
                    turn([It(k + half + alone, 1), It(k + half + alone + 1, 0)], [0, 0], again, k + HANDED)
                with pool.Fori(0, half) as k:
                    turn([It(k, 0), It(k, 1)], again, twice, k + HANDED + pairs - alone)

            def static_first(it, u, n):
                return type(it.i) is int and it.i * UN + u < n

            @block.scalar
            def _(act):
                act.preload_act_table_set("natural_log_exp_and_others")
                efv = edge_view_part(efeat)

                def load_ef(it, partial):
                    k = it.slot
                    ef_q = ef_b[:, k, :, :].rearrange("p (q j) f -> p q (j f)", q=Q)
                    if partial:
                        lastq = E - (NI - 1) * ITE - CHUNK
                        act.dma_start(ef_q[:, 0, :], efeat[E - lastq - CHUNK:E - lastq, :].rearrange("(p j) f -> p (j f)", j=J)).then_inc(ef_full[k], 16)
                        act.dma_start(ef_q[0:lastq // J, 1, :], efeat[E - lastq:E, :].rearrange("(p j) f -> p (j f)", j=J)).then_inc(ef_full[k], 16)
                    else:
                        for q in range(Q):
                            act.dma_start(ef_q[:, q, :], efv[it.i][q]).then_inc(ef_full[k], 16)

                def load_xs(it):
                    k = it.slot
                    act.wait_ge(xs_stored[k], 16 * (it.use + 1))
                    act.dma_start(xs_b[:, k, :, :].rearrange("p t f -> p (t f)"), xs_d[it.i]).then_inc(xs_full[k], 16)

                def load_piece(c):
                    act.dma_start(piece[:, c % 2, :, :].rearrange("p n f -> p (n f)"), x_v[c]).then_inc(piece_full[c % 2], 16)

                def widen(c):
                    k = c % 2
                    act.wait_ge(piece_full[k], 16 * (c // 2 + 1))
                    act.wait_ge(none_set, 1)
                    if c >= 2:
                        act.wait_ge(wide_stored[k], 16 * (c // 2))
                    act.activation(piece_w[:, k, :, 0:F], piece[:, k, :, :], ACT.Copy).then_inc(widened, 1)
                    act.wait_ge(widened, c + 1)
                    act.dma_start(wide_v[c], piece_w[:, k, :, :].rearrange("p n f -> p (n f)")).then_inc(wide_stored[k], 16)
                    if c + 2 < PIECES:
                        load_piece(c + 2)

                def load_mask(it):
                    act.dma_start(mask_b[:, it.slot, :], row_slice(mask_d, it.i, P)).then_inc(mask_full[it.slot], 16)

                def x_part(it, part, src, pairs):
                    act.activation(xstage[:, it.slot, :, pairs, 0:F], src.unsqueeze(2).broadcast_to([P, T, pairs.stop - pairs.start, F]), ACT.Copy) \
                        .then_inc(x_p[part], 1)

                def x_first(it):
                    act.wait_ge(ef_full[it.slot], 32 * (it.use + 1))
                    if not (type(it.i) is int and it.i < 2):
                        act.wait_ge(tr_done, it.i - 1)
                    x_part(it, 0, ef_b[:, it.slot, :, :], slice(0, 3))

                def x_second(it):
                    act.wait_ge(x_l[0], it.i + 1)
                    x_part(it, 1, left[:, :, :], slice(3, 5))

                def x_third(it):
                    act.wait_ge(x_l[1], it.i + 1)
                    x_part(it, 2, left[:, :, :], slice(5, 6))

                def copy_rows(it):
                    act.wait_ge(tr_done, it.i + 1)
                    if not (type(it.i) is int and it.i < 2):
                        act.wait_ge(w_ready, UN * (it.i - 1))
                    act.activation(hrows[:, it.slot, :, :].rearrange("k q (p j) -> k q j p", j=J), p_h[:, :, :, :], ACT.Copy).then_inc(rows_done, 1)
                    act.activation(xrows[:, it.slot, :, :].rearrange("k q (p j) -> k q j p", j=J), p_x[:, :, :, :], ACT.Copy).then_inc(rows_done, 1)

                def copy_f(it, q):
                    act.wait_ge(f_sum[q], it.i + 1)
                    if q == 0:
                        act.wait_ge(f_stored[it.slot], 16 * it.use)
                    act.activation(f_b[:, it.slot, q, :], p_f[:, q, :, :].rearrange("p j f -> p (j f)"), ACT.Copy).then_inc(f_copied[q], 1)

                def store_f(it):
                    copy_f(it, 1)
                    act.wait_ge(f_copied[0], it.i + 1)
                    act.wait_ge(f_copied[1], it.i + 1)
                    act.dma_start(f_v[it.i], f_b[:, it.slot, :, :]).then_inc(f_stored[it.slot], 16)

                def copy_hb(it, u):
                    c = unit(it, u)
                    act.wait_ge(hb_ready, c)
                    if not static_first(it, u, 2):
                        act.wait_ge(e1_done, c - 2)
                    act.activation(hb[:, u % 2, :], p_hb[:, u % 2, :], ACT.Copy).then_inc(hb_done, 1)

                def exps(it, u):
                    c = unit(it, u)
                    k = u % 2
                    act.wait_ge(d_done, c)
                    if not static_first(it, u, 2):
                        act.wait_ge(n_done, c - 2)
                        act.wait_ge(s_done, c - 2)
                    act.activation(ap[:, k, 0, :], e2[:, k, :], ACT.Relu).then_inc(dpos_done, 1)
                    act.activation(ap[:, k, 1, :], e2[:, k, :], ACT.Relu, scale=-1.0).then_inc(dneg_done, 1)
                    act.wait_ge(dpos_done, c)
                    act.wait_ge(dneg_done, c)
                    act.activation(ap[:, k, :, :], ap[:, k, :, :], ACT.Exp, scale=-1.0).then_inc(p_done, 1)

                def reciprocal(it, u):
                    c = unit(it, u)
                    act.wait_ge(s_done, c)
                    if not static_first(it, u, UN):
                        act.wait_ge(ratio_done, c - UN)
                    act.activation(rec[:, u, :], s[:, u, :], ACT.Ln).then_inc(log_done, 1)
                    act.wait_ge(log_done, c)
                    act.activation(rec[:, u, :], rec[:, u, :], ACT.Exp, scale=-1.0).then_inc(rec_done, 1)

                load_ef(It(0, 0), False)
                load_mask(It(0, 0))
                for c in range(2):
                    load_piece(c)
                act.wait_ge(cleared, 6)
                x_first(It(0, 0))
                widen(0)
                x_second(It(0, 0))
                widen(1)
                x_third(It(0, 0))
                widen(2)
                load_xs(It(0, 0))
                load_ef(It(0, 1), False)
                load_mask(It(0, 1))
                layernorm_rstd(nc, act, ls, 1, ve[:, :], lnv[:, :], rs[:, :])
                copy_rows(It(0, 0))
                copy_hb(It(0, 0), 0)
                copy_hb(It(0, 0), 1)
                load_xs(It(0, 1))
                widen(3)

                def body(it, left_over):
                    nxt = it.ahead(1)
                    if left_over:
                        x_first(nxt)
                    exps(it, 0)
                    if not static_first(it, 0, 1):
                        reciprocal(it.ahead(-1), 3)
                    copy_hb(it, 2)
                    if left_over:
                        layernorm_rstd(nc, act, ls, nxt.i + 1, ve[:, :], lnv[:, :], rs[:, :])
                    exps(it, 1)
                    if left_over:
                        x_second(nxt)
                    reciprocal(it, 0)
                    copy_hb(it, 3)
                    if not static_first(it, 0, 1):
                        copy_f(it.ahead(-1), 0)
                    else:
                        widen(4)
                    if left_over >= 2:
                        act.wait_ge(x_l[0], nxt.i + 1)
                        act.wait_ge(ls["cent"], nxt.i + 1)
                        load_ef(it.ahead(2), left_over == 2 and type(it.i) is int and it.i == NI - 3)
                        load_xs(it.ahead(2))
                    if not static_first(it, 0, UN + 1):
                        store_f(it.ahead(-2))
                    if left_over and not static_first(it, 0, 1):
                        act.wait_ge(w_done, unit(it, 0) - 1)
                        load_mask(nxt)
                    if left_over:
                        x_third(nxt)
                    exps(it, 2)
                    reciprocal(it, 1)
                    if left_over:
                        copy_rows(nxt)
                        copy_hb(nxt, 0)
                    exps(it, 3)
                    reciprocal(it, 2)
                    if left_over:
                        copy_hb(nxt, 1)
                    if type(it.i) is int and 5 + it.i < PIECES:
                        widen(5 + it.i)
                run_loop(act, NI, body, 3)
                end = It((NI - 1) // 2, (NI - 1) % 2)
                store_f(It((NI - 2) // 2, (NI - 2) % 2))
                reciprocal(end, 3)
                copy_f(end, 0)
                store_f(end)
                for k in range(2):
                    act.wait_ge(f_stored[k], 16 * ((NI + 1 - k) // 2))

            @block.tensor
            def _(pe):
                def transposes(it):
                    k = it.slot
                    pe.wait_ge(h_p[2], it.i + 1)
                    pe.wait_ge(x_p[2], it.i + 1)
                    if not static_first(it, 0, 1):
                        pe.wait_ge(rows_done, 2 * it.i)
                    pe.sem_inc(gate, 1)
                    for t in range(T):
                        nc.tensor.transpose(p_x[:, t // J, t % J, :], xstage[:, k, t, :, :].rearrange("p n f -> p (n f)"), identb[:, :])
                    for t in range(T):
                        last = nc.tensor.transpose(p_h[:, t // J, t % J, :], hstage[:, k, t, :, :].rearrange("p n f -> p (n f)"), identb[:, :])
                    last.then_inc(tr_done, 1)

                def h_product(it, u):
                    c = unit(it, u)
                    if u == 0:
                        pe.wait_ge(rows_done, 2 * it.i + 1)
                    if not static_first(it, u, 2):
                        pe.wait_ge(hb_done, c - 2)
                    pe.sem_inc(gate, 1)
                    nc.tensor.matmul(p_hb[:, u % 2, :], in_sel[:, (u % 2) * P:(u % 2 + 1) * P], hrows[:, it.slot, u // 2, :],
                                     start=True, stop=True).then_inc(hb_ready, 1)

                def products(it, u):
                    c = unit(it, u)
                    if u == 0:
                        pe.wait_ge(rows_done, 2 * (it.i + 1))
                    if not static_first(it, u, 1):
                        pe.wait_ge(e1_done, c - 1)
                    pe.sem_inc(gate, 1)
                    cols = slice((u % 2) * P, (u % 2 + 1) * P)
                    nc.tensor.matmul(p_wa[:, :], wam[:, 0, cols], xrows[:, it.slot, u // 2, :], start=True, stop=True)
                    nc.tensor.matmul(p_wm[:, :], wam[:, 1, cols], xrows[:, it.slot, u // 2, :], start=True, stop=True).then_inc(w_ready, 1)

                def sums(it, q):
                    pe.wait_ge(ratio_done, unit(it, 2 * q + 1))
                    if not static_first(it, 0, 1):
                        pe.wait_ge(f_copied[q], it.i)
                    pe.sem_inc(gate, 1)
                    for j in range(J):
                        for half in range(2):
                            last = nc.tensor.matmul(p_f[:, q, j, :], ratio[:, 2 * q + half, j:CHUNK:J], out_sum[:, :],
                                                    start=(half == 0), stop=(half == 1))
                    last.then_inc(f_sum[q], 1)

                transposes(It(0, 0))
                h_product(It(0, 0), 0)
                products(It(0, 0), 0)
                h_product(It(0, 0), 1)

                def body(it, left_over):
                    nxt = it.ahead(1)
                    products(it, 1)
                    h_product(it, 2)
                    if not static_first(it, 0, 1):
                        sums(it.ahead(-1), 0)
                    products(it, 2)
                    h_product(it, 3)
                    products(it, 3)
                    if left_over:
                        transposes(nxt)
                        h_product(nxt, 0)
                        products(nxt, 0)
                        h_product(nxt, 1)
                    if not static_first(it, 0, 1):
                        sums(it.ahead(-1), 1)
                run_loop(pe, NI, body, 3)
                end = It((NI - 1) // 2, (NI - 1) % 2)
                sums(end, 0)
                sums(end, 1)

            @block.vector
            def _(dve):
                nc.vector.memset(xstage[:, :, :, :, :], 0.0).then_inc(cleared, 1)
                nc.vector.memset(w[:, :, :], -BIG).then_inc(cleared, 1)
                nc.vector.memset(s[:, :, :], 0.0).then_inc(cleared, 1)
                nc.vector.memset(n[:, :, :], 0.0).then_inc(cleared, 1)
                dve.wait_ge(cleared, 4)
                for k in range(2):
                    nc.vector.memset(xstage[:, k, :, 0:3, F:EK], 1.0).then_inc(cleared, 1)
                dve.wait_ge(cleared, 6)

                def carry(it, u):
                    if not static_first(it, 0, 1):
                        dve.wait_ge(w_done, unit(it, u) - 2)
                        dve.wait_ge(d_done, unit(it, u) - 4)
                    nc.vector.tensor_copy(w[:, u, 0:1], w[:, u, ITE:ITE + 1]).then_inc(w0_done, 1)

                def e2_in(it, u):
                    c = unit(it, u)
                    if not static_first(it, u, 2):
                        dve.wait_ge(p_done, c - 2)
                    dve.wait_ge(hb_done, c)
                    dve.wait_ge(w_ready, c)
                    nc.vector.tensor_tensor(e2[:, u % 2, :], p_wa[:, :], hb[:, u % 2, :], ALU.mult).then_inc(e2_done, 1)

                def e1_in(it, u):
                    if not static_first(it, u, 2):
                        dve.wait_ge(n_done, unit(it, u) - 2)
                    nc.vector.tensor_tensor(r[:, u % 2, :], p_wm[:, :], hb[:, u % 2, :], ALU.mult).then_inc(e1_done, 1)

                def max_scan(it, u):
                    c = unit(it, u)
                    lo = u // 2 * CHUNK
                    if u == 0:
                        dve.wait_ge(mask_full[it.slot], 16 * (it.use + 1))
                    dve.wait_ge(w0_done, 2 * it.i + u % 2 + 1)
                    if u >= 2:
                        dve.wait_ge(w_done, c - 2)
                    if not static_first(it, u, 4):
                        dve.wait_ge(d_done, c - 4)
                    dve.wait_ge(e2_done, c)
                    nc.vector.tensor_tensor_scan(w[:, u % 2, lo + 1:lo + CHUNK + 1], e2[:, u % 2, :], mask_b[:, it.slot, lo:lo + CHUNK],
                                                 w[:, u % 2, lo:lo + 1], ALU.max, ALU.add).then_inc(w_done, 1)

                def difference(it, u):
                    lo = u // 2 * CHUNK
                    dve.wait_ge(w_done, unit(it, u))
                    nc.vector.tensor_tensor(e2[:, u % 2, :], e2[:, u % 2, :], w[:, u % 2, lo:lo + CHUNK], ALU.subtract).then_inc(d_done, 1)

                def weigh(it, u):
                    c = unit(it, u)
                    dve.wait_ge(p_done, c)
                    dve.wait_ge(e1_done, c)
                    nc.vector.tensor_tensor(r[:, u % 2, :], r[:, u % 2, :], ap[:, u % 2, 1, :], ALU.mult).then_inc(r_done, 1)

                def s_scan(it, u):
                    c = unit(it, u)
                    if not static_first(it, u, 2):
                        dve.wait_ge(s_done, c - 2)
                    if not static_first(it, u, 4):
                        dve.wait_ge(rec_done, c - 4)
                    nc.vector.tensor_tensor_scan(s[:, u, :], ap[:, u % 2, 0, :], ap[:, u % 2, 1, :], s[:, (u + 2) % UN, CHUNK - 1:CHUNK], ALU.mult, ALU.add) \
                        .then_inc(s_done, 1)

                def n_scan(it, u):
                    c = unit(it, u)
                    dve.wait_ge(r_done, c)
                    if not static_first(it, u, 4):
                        dve.wait_ge(ratio_done, c - 4)
                    nc.vector.tensor_tensor_scan(n[:, u, :], ap[:, u % 2, 0, :], r[:, u % 2, :], n[:, (u + 2) % UN, CHUNK - 1:CHUNK], ALU.mult, ALU.add) \
                        .then_inc(n_done, 1)

                def back(it, u):
                    weigh(it, u)
                    s_scan(it, u)
                    n_scan(it, u)

                def divide(it, u):
                    c = unit(it, u)
                    dve.wait_ge(rec_done, c)
                    dve.wait_ge(n_done, c)
                    if not static_first(it, 0, 1):
                        dve.wait_ge(f_sum[u // 2], it.i)
                    nc.vector.tensor_tensor(ratio[:, u, :], n[:, u, :], rec[:, u, :], ALU.mult).then_inc(ratio_done, 1)

                ln = layernorm_steps(nc, dve, ls, sm[:, :], nm[:, :], cc[:, :, :], sq[:, :, :], vs[:, :], ve[:, :])

                def stats_first(it):
                    dve.wait_ge(xs_full[it.slot], 16 * (it.use + 1))
                    if not static_first(it, 0, 1):
                        dve.wait_ge(ls["h"], it.i)
                    ln["sum"](it.i + 1, xs_b[:, it.slot, :, 0:F])

                def x_left(it, part):
                    dve.wait_ge(x_p[part], it.i + 1)
                    if part == 0:
                        if not static_first(it, 0, 1):
                            dve.wait_ge(x_p[2], it.i)
                        nc.vector.tensor_tensor(left[:, :, :], ef_b[:, it.slot, :, :], xstage[:, it.slot, :, 0, 0:F], ALU.subtract).then_inc(x_l[0], 1)
                    else:
                        nc.vector.tensor_tensor(left[:, :, :], left[:, :, :], xstage[:, it.slot, :, 3, 0:F], ALU.subtract).then_inc(x_l[1], 1)

                def h_out(it):
                    if not static_first(it, 0, 1):
                        dve.wait_ge(h_p[2], it.i)
                    if not (type(it.i) is int and it.i < 2):
                        dve.wait_ge(tr_done, it.i - 1)
                    layernorm_out(nc, dve, ls, it.i + 1, hf[:, :, :], cc[:, :, :], rs[:, :])

                def h_part(it, part):
                    dve.wait_ge(ls["h"] if part == 0 else h_l[part - 1], it.i + 1)
                    nc.vector.tensor_copy(hstage[:, it.slot, :, part, :], hf[:, :, :]).then_inc(h_p[part], 1)

                def h_left(it, part):
                    dve.wait_ge(h_p[part], it.i + 1)
                    nc.vector.tensor_tensor(hf[:, :, :], hf[:, :, :], hstage[:, it.slot, :, part, :], ALU.subtract).then_inc(h_l[part], 1)

                start = It(0, 0)
                x_left(start, 0)
                x_left(start, 1)
                stats_first(start)
                for step in ("mean", "cent", "sq", "sqsum", "var"):
                    ln[step](1, xs_b[:, 0, :, 0:F])
                h_out(start)
                for part in range(3):
                    h_part(start, part)
                    if part < 2:
                        h_left(start, part)

                def body(it, left_over, ratios="both"):
                    nxt, last = it.ahead(1), it.ahead(-1)
                    c = nxt.i + 1
                    rows = xs_b[:, nxt.slot, :, 0:F]
                    started = not static_first(it, 0, 1)
                    e2_in(it, 0)
                    carry(it, 0)
                    e1_in(it, 0)
                    carry(it, 1)
                    max_scan(it, 0)
                    if left_over:
                        stats_first(nxt)
                    difference(it, 0)
                    if started and ratios:
                        divide(last, 2)
                    if started:
                        weigh(last, 3)
                    if left_over:
                        ln["mean"](c, rows)
                    if started:
                        s_scan(last, 3)
                    if left_over:
                        ln["cent"](c, rows)
                    if started:
                        n_scan(last, 3)
                    if left_over:
                        ln["sq"](c, rows)
                    e2_in(it, 1)
                    if left_over:
                        ln["sqsum"](c, rows)
                    e1_in(it, 1)
                    if left_over:
                        ln["var"](c, rows)
                    max_scan(it, 1)
                    if left_over:
                        x_left(nxt, 0)
                    if started and ratios:
                        divide(last, 3)
                    difference(it, 1)
                    if left_over:
                        h_out(nxt)
                    weigh(it, 0)
                    if left_over:
                        h_part(nxt, 0)
                    s_scan(it, 0)
                    if left_over:
                        h_left(nxt, 0)
                    n_scan(it, 0)
                    if left_over:
                        h_part(nxt, 1)
                    e2_in(it, 2)
                    if left_over:
                        h_left(nxt, 1)
                    e1_in(it, 2)
                    if left_over:
                        h_part(nxt, 2)
                    max_scan(it, 2)
                    if left_over:
                        x_left(nxt, 1)
                    if ratios == "both":
                        divide(it, 0)
                    difference(it, 2)
                    back(it, 1)
                    e2_in(it, 3)
                    e1_in(it, 3)
                    max_scan(it, 3)
                    if ratios == "both":
                        divide(it, 1)
                    difference(it, 3)
                    back(it, 2)
                run_loop(dve, NI, body, 3, end=HANDED)
                body(It(HANDED // 2, HANDED % 2), 3, "last")
                run_loop(dve, NI, lambda it, left_over: body(it, left_over, None), 3, start=HANDED + 1)
                end = It((NI - 1) // 2, (NI - 1) % 2)
                back(end, 3)


def edge_view_part(t):
    whole = E // ITE
    return Chunks(t[0:whole * ITE, :].rearrange("(i q p j) f -> i q p j f", q=Q, p=P, j=J))


class Chunks:
    def __init__(self, view):
        self.view = view

    def __getitem__(self, i):
        return [self.view[i, q] for q in range(Q)]


def row_slice(row, i, parts):
    one = row.rearrange("o (i e) -> (o i) e", e=ITE)[i].rearrange("(o e) -> o e", o=1)
    return one.broadcast_to([parts, ITE])


def first_hop(nc, sem, gate, pool_gate, xs_d, h_v, a_v, rc_d, f_tab, keep_d, ident):
    ctx = ExitStack()
    with ctx:
        def sb(name, shape, dt=f32):
            return ctx.enter_context(nc.sbuf_tensor(name, shape, dt))

        g = sb("h1_g", [P, 2, T, F])
        xs_b = sb("h1_xs", [P, 2, T, XW])
        keep_b = sb("h1_keep", [EK, 2, ITE])
        x1 = sb("h1_x1", [P, 2, T, F])
        h_b = sb("h1_h", [P, 2, T, EK])
        sm, nm, vs, ve, lnv, rs = (sb(f"h1_{n}", [P, T]) for n in ("sm", "nm", "vs", "ve", "lnv", "rs"))
        cc, sq = (sb(f"h1_{n}", [P, T, F]) for n in ("cc", "sq"))
        rows = sb("h1_rows", [EK, 2, ITE])
        acc = sb("h1_acc", [EK, 2, ITE])
        rc = sb("h1_rc", [P, 2, T])
        mean = sb("h1_mean", [P, 2, T, F])
        p_t = ctx.enter_context(nc.psum_tensor("h1_pt", [EK, Q, J, P], f32))
        p_b = ctx.enter_context(nc.psum_tensor("h1_pb", [P, T, EK], f32))

        g_full, xs_full, keep_full, h_stored, mean_stored, rc_stored = (
            [sem(f"h1_{n}{k}") for k in range(2)] for n in ("g_full", "xs_full", "keep_full", "h_stored", "mean_stored", "rc_stored"))
        ls = layernorm_sems(sem, "h1")
        cleared, x1_done, tr_done, rows_done, acc_done, bk_done, rc_done, mean_done = (
            sem(f"h1_{n}") for n in ("cleared", "x1_done", "tr_done", "rows_done", "acc_done", "bk_done", "rc_done", "mean_done"))

        h_v2 = Chunks(h_d_view(h_v))
        with nc.Block() as block:
            @block.sync
            def _(sp):
                def load_xs(it):
                    sp.dma_start(xs_b[:, it.slot, :, :].rearrange("p t f -> p (t f)"), xs_d[it.i]).then_inc(xs_full[it.slot], 16)

                def load_keep(it):
                    sp.dma_start(keep_b[:, it.slot, :], row_slice(keep_d, it.i, EK)).then_inc(keep_full[it.slot], 16)

                for k in range(2):
                    load_xs(It(0, k))
                    load_keep(It(0, k))

                def body(it, left_over):
                    if left_over >= 2:
                        sp.wait_ge(g_full[it.slot], 16 * T * (it.use + 1))
                        sp.wait_ge(x1_done, it.i + 1)
                        load_xs(it.ahead(2))
                        sp.wait_ge(acc_done, it.i + 1)
                        load_keep(it.ahead(2))
                run_loop(sp, NI, body, 2)

            @block.gpsimd
            def _(pool):
                def body(it, left):
                    pool.wait_ge(xs_full[it.slot], 16 * (it.use + 1))
                    if not (type(it.i) is int and it.i < 2):
                        pool.wait_ge(x1_done, it.i - 1)
                    pool.sem_inc(pool_gate, 1)
                    for t in range(T):
                        pool.indirect_dma_start(g[:, it.slot, t, :], None, f_tab,
                                                bass.IndirectOffsetOnAxis(ap=xs_b[:, it.slot, t, F:XW].bitcast(i32), axis=0)) \
                            .then_inc(g_full[it.slot], 16)
                run_loop(pool, NI, body, 2)

            @block.scalar
            def _(act):
                def store_mean(it):
                    act.wait_ge(mean_done, it.i + 1)
                    act.dma_start(a_v[it.i], mean[:, it.slot, :, :].rearrange("p (q j) f -> p q (j f)", q=Q)).then_inc(mean_stored[it.slot], 16)
                    act.dma_start(rc_d[it.i], rc[:, it.slot, :]).then_inc(rc_stored[it.slot], 16)

                def body(it, left_over):
                    layernorm_rstd(nc, act, ls, it.i + 1, ve[:, :], lnv[:, :], rs[:, :])
                    act.wait_ge(tr_done, it.i + 1)
                    if not (type(it.i) is int and it.i < 2):
                        act.wait_ge(acc_done, it.i - 1)
                    for q in range(Q):
                        act.activation(rows[:, it.slot, q * CHUNK:(q + 1) * CHUNK].rearrange("k (p j) -> k j p", j=J), p_t[:, q, :, :], ACT.Copy) \
                            .then_inc(rows_done, 1)
                    for q in range(Q):
                        act.dma_start(h_v2[it.i][q], h_b[:, it.slot, q * J:(q + 1) * J, 0:F]).then_inc(h_stored[it.slot], 16)
                    if not (type(it.i) is int and it.i == 0):
                        store_mean(it.ahead(-1))
                run_loop(act, NI, body, 2)
                store_mean(It((NI - 1) // 2, (NI - 1) % 2))
                for k in range(2):
                    act.wait_ge(h_stored[k], 32 * ((NI + 1 - k) // 2))
                    act.wait_ge(mean_stored[k], 16 * ((NI + 1 - k) // 2))
                    act.wait_ge(rc_stored[k], 16 * ((NI + 1 - k) // 2))

            @block.tensor
            def _(pe):
                def forth(it):
                    pe.wait_ge(ls["h"], it.i + 1)
                    if not (type(it.i) is int and it.i == 0):
                        pe.wait_ge(rows_done, Q * it.i)
                    pe.sem_inc(gate, 1)
                    for t in range(T):
                        last = nc.tensor.transpose(p_t[:, t // J, t % J, :], h_b[:, it.slot, t, :], ident[:, :])
                    last.then_inc(tr_done, 1)

                def back(it):
                    pe.wait_ge(acc_done, it.i + 1)
                    if not (type(it.i) is int and it.i == 0):
                        pe.wait_ge(mean_done, it.i)
                    pe.sem_inc(gate, 1)
                    for t in range(T):
                        q, j = t // J, t % J
                        last = nc.tensor.transpose(p_b[:, t, :], acc[:, it.slot, q * CHUNK + j:(q + 1) * CHUNK:J], ident[0:EK, 0:EK])
                    last.then_inc(bk_done, 1)

                def body(it, left):
                    forth(it)
                    if not (type(it.i) is int and it.i == 0):
                        back(it.ahead(-1))
                run_loop(pe, NI, body, 2)
                back(It((NI - 1) // 2, (NI - 1) % 2))

            @block.vector
            def _(dve):
                nc.vector.memset(acc[:, :, :], 0.0).then_inc(cleared, 1)
                nc.vector.memset(h_b[:, :, :, F:EK], 1.0).then_inc(cleared, 1)
                dve.wait_ge(cleared, 2)

                def norm(it):
                    c = it.i + 1
                    first = type(it.i) is int and it.i == 0
                    dve.wait_ge(g_full[it.slot], 16 * T * (it.use + 1))
                    dve.wait_ge(xs_full[it.slot], 16 * (it.use + 1))
                    nc.vector.tensor_tensor(x1[:, it.slot, :, :], g[:, it.slot, :, :], xs_b[:, it.slot, :, 0:F], ALU.add).then_inc(x1_done, 1)
                    dve.wait_ge(x1_done, c)
                    if not first:
                        dve.wait_ge(ls["h"], it.i)
                    layernorm_stats(nc, dve, ls, c, x1[:, it.slot, :, :], sm[:, :], nm[:, :], cc[:, :, :], sq[:, :, :], vs[:, :], ve[:, :])

                def normed(it):
                    dve.wait_ge(h_stored[it.slot], 32 * it.use)
                    if not (type(it.i) is int and it.i < 2):
                        dve.wait_ge(tr_done, it.i - 1)
                    layernorm_out(nc, dve, ls, it.i + 1, h_b[:, it.slot, :, 0:F], cc[:, :, :], rs[:, :])

                def scan(it):
                    c = it.i + 1
                    dve.wait_ge(rows_done, Q * c)
                    dve.wait_ge(keep_full[it.slot], 16 * (it.use + 1))
                    if not (type(it.i) is int and it.i < 2):
                        dve.wait_ge(bk_done, it.i - 1)
                    if not (type(it.i) is int and it.i == 0):
                        dve.wait_ge(acc_done, it.i)
                    nc.vector.tensor_tensor_scan(acc[:, it.slot, :], keep_b[:, it.slot, :], rows[:, it.slot, :],
                                                 acc[:, 1 - it.slot, ITE - 1:ITE], ALU.mult, ALU.add).then_inc(acc_done, 1)

                def means(it):
                    c = it.i + 1
                    k = it.slot
                    dve.wait_ge(bk_done, c)
                    dve.wait_ge(rc_stored[k], 16 * it.use)
                    if not (type(it.i) is int and it.i < 2):
                        dve.wait_ge(mean_done, it.i - 1)
                    nc.vector.reciprocal(rc[:, k, :].unsqueeze(2), p_b[:, :, F:EK]).then_inc(rc_done, 1)
                    dve.wait_ge(rc_done, c)
                    dve.wait_ge(mean_stored[k], 16 * it.use)
                    nc.vector.tensor_tensor(mean[:, k, :, :], p_b[:, :, 0:F], spread(rc[:, k, :], F), ALU.mult).then_inc(mean_done, 1)

                def body(it, left):
                    norm(it)
                    if not (type(it.i) is int and it.i == 0):
                        scan(it.ahead(-1))
                    normed(it)
                    if not (type(it.i) is int and it.i == 0):
                        means(it.ahead(-1))
                run_loop(dve, NI, body, 2)
                end = It((NI - 1) // 2, (NI - 1) % 2)
                scan(end)
                means(end)


def h_d_view(h_v):
    return h_v.rearrange("i p q (j f) -> i q p j f", f=F)


def second_hop(nc, sem, gate, pool_gate, xs_d, meta_v, h_v, f_v, a_v, rc_d, a_tab, keep_d, node_tab, ident, w1, b1c, w2g):
    ctx = ExitStack()
    with ctx:
        def sb(name, shape, dt=f32):
            return ctx.enter_context(nc.sbuf_tensor(name, shape, dt))

        def ps(name, shape):
            return ctx.enter_context(nc.psum_tensor(name, shape, f32))

        row_b = sb("h2_row", [P, 2, T, XW])
        meta_b = sb("h2_meta", [P, 2, Q, MW], i32)
        stage = sb("h2_stage", [P, 2, T, LK])
        keep_b = sb("h2_keep", [F, 2, ITE])
        node_b = sb("h2_node", [P, 2, T, RW])
        rows = sb("h2_rows", [P, Q, P])
        hid = sb("h2_hid", [P, Q, P])
        acc = sb("h2_acc", [F, 2, ITE])
        rc = sb("h2_rc", [P, 2, T])
        p_t = ps("h2_pt", [P, CHUNK])[:, 0:Q * P].rearrange("k (q e) -> k q e", q=Q)
        p_h = ps("h2_ph", [P, CHUNK])[:, 0:Q * P].rearrange("k (q e) -> k q e", q=Q)
        p_g = ps("h2_pg", [F, Q, CHUNK])
        p_b = ps("h2_pb", [P, CHUNK])[:, 0:T * F].rearrange("p (t f) -> p t f", t=T)

        row_full, meta_full, h_full, g_full, keep_full, node_full, rc_full, sent = (
            [sem(f"h2_{n}{k}") for k in range(2)] for n in ("row_full", "meta_full", "h_full", "g_full", "keep_full", "node_full", "rc_full", "sent"))
        cleared, tr_done, rows_done, hid_ready, hid_done, g_ready, acc_done, bk_done, mean_done = (
            sem(f"h2_{n}") for n in ("cleared", "tr_done", "rows_done", "hid_ready", "hid_done", "g_ready", "acc_done", "bk_done", "mean_done"))
        uses = [(NI + 1) // 2, NI // 2]
        hc, fc, ac = Chunks(h_d_view(h_v)), Chunks(h_d_view(f_v)), Chunks(h_d_view(a_v))

        with nc.Block() as block:
            @block.sync
            def _(sp):
                def load_in(it):
                    k = it.slot
                    sp.dma_start(row_b[:, k, :, :].rearrange("p t f -> p (t f)"), xs_d[it.i]).then_inc(row_full[k], 16)
                    for q in range(Q):
                        sp.dma_start(stage[:, k, q * J:(q + 1) * J, 0:F], hc[it.i][q]).then_inc(h_full[k], 16)
                    sp.dma_start(keep_b[:, k, :], row_slice(keep_d, it.i, F)).then_inc(keep_full[k], 16)

                def load_out(it):
                    k = it.slot
                    sp.dma_start(meta_b[:, k, :, :], meta_v[it.i]).then_inc(meta_full[k], 16)
                    sp.dma_start(rc[:, k, :], rc_d[it.i]).then_inc(rc_full[k], 16)
                    for q in range(Q):
                        sp.dma_start(node_b[:, k, q * J:(q + 1) * J, 0:F], fc[it.i][q]).then_inc(node_full[k], 16)
                        sp.dma_start(node_b[:, k, q * J:(q + 1) * J, F:2 * F], ac[it.i][q]).then_inc(node_full[k], 16)
                for k in range(2):
                    load_in(It(0, k))
                    load_out(It(0, k))

                def body(it, left):
                    if left >= 2:
                        sp.wait_ge(g_full[it.slot], 16 * T * (it.use + 1))
                        sp.wait_ge(tr_done, it.i + 1)
                        sp.wait_ge(acc_done, it.i + 1)
                        load_in(it.ahead(2))
                        sp.wait_ge(sent[it.slot], 16 * T * (it.use + 1))
                        load_out(it.ahead(2))
                run_loop(sp, NI, body, 2)

            @block.gpsimd
            def _(pool):
                def gather(it):
                    k = it.slot
                    pool.wait_ge(row_full[k], 16 * (it.use + 1))
                    if not (type(it.i) is int and it.i < 2):
                        pool.wait_ge(tr_done, it.i - 1)
                    pool.sem_inc(pool_gate, 1)
                    for t in range(T):
                        pool.indirect_dma_start(stage[:, k, t, F:2 * F], None, a_tab,
                                                bass.IndirectOffsetOnAxis(ap=row_b[:, k, t, F:XW].bitcast(i32), axis=0)) \
                            .then_inc(g_full[k], 16)

                def scatter(it):
                    k = it.slot
                    pool.wait_ge(meta_full[k], 16 * (it.use + 1))
                    pool.wait_ge(node_full[k], 64 * (it.use + 1))
                    pool.wait_ge(mean_done, it.i + 1)
                    pool.sem_inc(pool_gate, 1)
                    for t in range(T):
                        pool.indirect_dma_start(node_tab, bass.IndirectOffsetOnAxis(ap=meta_b[:, k, t // J, J + t % J:J + t % J + 1], axis=0),
                                                node_b[:, k, t, :], None).then_inc(sent[k], 16)

                def body(it, left):
                    gather(it)
                    if not (type(it.i) is int and it.i == 0):
                        scatter(it.ahead(-1))
                pool.wait_ge(cleared, 1)
                run_loop(pool, NI, body, 2)
                scatter(It((NI - 1) // 2, (NI - 1) % 2))
                for k in range(2):
                    pool.wait_ge(sent[k], 16 * T * uses[k])

            @block.scalar
            def _(act):
                def body(it, left):
                    c = it.i + 1
                    first = type(it.i) is int and it.i == 0
                    act.wait_ge(tr_done, c)
                    if not first:
                        act.wait_ge(hid_ready, it.i)
                    act.activation(rows[:, :, :], p_t[:, :, :], ACT.Copy).then_inc(rows_done, 1)
                    act.wait_ge(hid_ready, c)
                    if not first:
                        act.wait_ge(g_ready, it.i)
                    act.activation(hid[:, :, :], p_h[:, :, :], ACT.Relu, bias=b1c[:, :]).then_inc(hid_done, 1)
                run_loop(act, NI, body, 2)

            @block.tensor
            def _(pe):
                def forth(it):
                    c = it.i + 1
                    first = type(it.i) is int and it.i == 0
                    pe.wait_ge(g_full[it.slot], 16 * T * (it.use + 1))
                    pe.wait_ge(h_full[it.slot], 32 * (it.use + 1))
                    if not first:
                        pe.wait_ge(rows_done, it.i)
                    pe.sem_inc(gate, 1)
                    for q in range(Q):
                        last = nc.tensor.transpose(p_t[:, q, :], stage[:, it.slot, q * J:(q + 1) * J, :].rearrange("p j k -> p (j k)"), ident[:, :])
                    last.then_inc(tr_done, 1)
                    pe.wait_ge(rows_done, c)
                    if not first:
                        pe.wait_ge(hid_done, it.i)
                    pe.sem_inc(gate, 1)
                    nc.tensor.matmul(p_h[:, :, :], w1[:, :], rows[:, :, :], start=True, stop=True).then_inc(hid_ready, 1)
                    pe.wait_ge(hid_done, c)
                    if not first:
                        pe.wait_ge(acc_done, it.i)
                    pe.sem_inc(gate, 1)
                    for q in range(Q):
                        for j in range(J):
                            last = nc.tensor.matmul(p_g[:, q, j:CHUNK:J], w2g[:, j, :], hid[:, q, :], start=True, stop=True)
                    last.then_inc(g_ready, 1)

                def back(it):
                    pe.wait_ge(acc_done, it.i + 1)
                    if not (type(it.i) is int and it.i == 0):
                        pe.wait_ge(mean_done, it.i)
                    pe.sem_inc(gate, 1)
                    for t in range(T):
                        q, j = t // J, t % J
                        last = nc.tensor.transpose(p_b[:, t, :], acc[:, it.slot, q * CHUNK + j:(q + 1) * CHUNK:J], ident[0:F, 0:F])
                    last.then_inc(bk_done, 1)

                pe.wait_ge(cleared, 1)

                def body(it, left):
                    forth(it)
                    back(it)
                run_loop(pe, NI, body, 2)

            @block.vector
            def _(dve):
                nc.vector.memset(acc[:, :, :], 0.0).then_inc(cleared, 1)
                dve.wait_ge(cleared, 1)

                def body(it, left):
                    c = it.i + 1
                    first = type(it.i) is int and it.i == 0
                    dve.wait_ge(g_ready, c)
                    dve.wait_ge(keep_full[it.slot], 16 * (it.use + 1))
                    if not first:
                        dve.wait_ge(acc_done, it.i)
                    nc.vector.tensor_tensor_scan(acc[:, it.slot, :], keep_b[:, it.slot, :], p_g[:, :, :].rearrange("k q e -> k (q e)"),
                                                 acc[:, 1 - it.slot, ITE - 1:ITE], ALU.mult, ALU.add).then_inc(acc_done, 1)
                    dve.wait_ge(bk_done, c)
                    dve.wait_ge(rc_full[it.slot], 16 * (it.use + 1))
                    dve.wait_ge(sent[it.slot], 16 * T * it.use)
                    nc.vector.tensor_tensor(node_b[:, it.slot, :, 2 * F:RW], p_b[:, :, :], spread(rc[:, it.slot, :], F), ALU.mult).then_inc(mean_done, 1)
                run_loop(dve, NI, body, 2)


def node_pass(nc, sem, gate, pool_gate, x, node_tab, out, ident, ones3, w1, b1c, w2n, b2r):
    K = NK
    KG = K // G
    S = 3
    whole = N // (P * K)
    rest = (N - whole * P * K) // K
    xv = x[0:whole * P * K, :].rearrange("(i p k) f -> i p (k f)", p=P, k=K)
    ov = out[0:whole * P * K, :].rearrange("(i p k) f -> i p (k f)", p=P, k=K)
    nv = node_tab[0:whole * P * K, :].rearrange("(i p k) f -> i p (k f)", p=P, k=K)
    tail_of = lambda t: t[whole * P * K:N, :].rearrange("(p k) f -> p (k f)", k=K)
    ctx = ExitStack()
    with ctx:
        def sb(name, shape, dt=f32):
            return ctx.enter_context(nc.sbuf_tensor(name, shape, dt))

        def ps(name, shape):
            return ctx.enter_context(nc.psum_tensor(name, shape, f32))

        x_b = sb("n_x", [P, S, K, F])
        t_b = sb("n_t", [P, S, K, RW])
        x1 = sb("n_x1", [P, S, K, F])
        x2 = sb("n_x2", [P, S, K, F])
        stage = sb("n_stage", [P, S, K, LK])
        sm, nm, vs, ve, lnv, rs = (sb(f"n_{n}", [P, K]) for n in ("sm", "nm", "vs", "ve", "lnv", "rs"))
        cc, sq = (sb(f"n_{n}", [P, K, F]) for n in ("cc", "sq"))
        rows = sb("n_rows", [P, KG * P])
        hid = sb("n_hid", [P, KG * P])
        o_b = sb("n_o", [P, S, K, F])
        p_t = ps("n_pt", [P, KG * P])
        p_h = ps("n_ph", [P, KG * P])
        p_o = ps("n_po", [P, K, F])

        x_full, t_full, stored = ([sem(f"n_{n}{k}") for k in range(S)] for n in ("x_full", "t_full", "stored"))
        ls = layernorm_sems(sem, "n")
        x1_done, x2_done, mean_done, tr_done, rows_done, hid_ready, hid_done, o_ready, o_done = (
            sem(f"n_{n}") for n in ("x1_done", "x2_done", "mean_done", "tr_done", "rows_done", "hid_ready", "hid_done", "o_ready", "o_done"))

        parts = KG * P // CHUNK
        part_cols = [slice(q * CHUNK, (q + 1) * CHUNK) for q in range(parts)]

        def is_last(it):
            return type(it.i) is int and it.i == NT - 1

        def at_least(it, n):
            return not (type(it.i) is int and it.i < n)

        def nth(n):
            return It(n // S, n % S, S)

        with nc.Block() as block:
            @block.sync
            def _(sp):
                def load(it):
                    k = it.slot
                    if is_last(it):
                        sp.dma_start(x_b[0:rest, k, :, :].rearrange("p k f -> p (k f)"), tail_of(x)).then_inc(x_full[k], 16)
                        sp.dma_start(t_b[0:rest, k, :, :].rearrange("p k f -> p (k f)"), tail_of(node_tab)).then_inc(t_full[k], 16)
                    else:
                        sp.dma_start(x_b[:, k, :, :].rearrange("p k f -> p (k f)"), xv[it.i]).then_inc(x_full[k], 16)
                        sp.dma_start(t_b[:, k, :, :].rearrange("p k f -> p (k f)"), nv[it.i]).then_inc(t_full[k], 16)

                def store(it):
                    sp.wait_ge(o_done, it.i + 1)
                    k = it.slot
                    if is_last(it):
                        sp.dma_start(tail_of(out), o_b[0:rest, k, :, :].rearrange("p k f -> p (k f)")).then_inc(stored[k], 16)
                    else:
                        sp.dma_start(ov[it.i], o_b[:, k, :, :].rearrange("p k f -> p (k f)")).then_inc(stored[k], 16)

                for n in range(S):
                    load(nth(n))

                def body(it, left):
                    if left >= S:
                        sp.wait_ge(x2_done, it.i + 1)
                        sp.wait_ge(mean_done, it.i + 1)
                        load(it.ahead(S))
                    if at_least(it, 2):
                        store(it.ahead(-2))
                run_loop(sp, NT, body, S, S, S)
                store(nth(NT - 2))
                store(nth(NT - 1))
                for k in range(S):
                    sp.wait_ge(stored[k], 16 * ((NT + S - 1 - k) // S))

            @block.gpsimd
            def _(pool):
                def body(it, left):
                    c = it.i + 1
                    k = it.slot
                    pool.wait_ge(x_full[k], 16 * (it.use + 1))
                    pool.wait_ge(t_full[k], 16 * (it.use + 1))
                    if at_least(it, S):
                        pool.wait_ge(ls["cent"], c - S)
                    pool.sem_inc(pool_gate, 1)
                    nc.gpsimd.tensor_tensor(x1[:, k, :, :], x_b[:, k, :, :], t_b[:, k, :, 0:F], ALU.add).then_inc(x1_done, 1)
                    pool.wait_ge(x1_done, c)
                    if at_least(it, S):
                        pool.wait_ge(o_done, c - S)
                    pool.sem_inc(pool_gate, 1)
                    nc.gpsimd.tensor_tensor(x2[:, k, :, :], x1[:, k, :, :], t_b[:, k, :, 2 * F:RW], ALU.add).then_inc(x2_done, 1)
                run_loop(pool, NT, body, S, S, S)

            @block.scalar
            def _(act):
                def mean_in(it):
                    k = it.slot
                    act.wait_ge(t_full[k], 16 * (it.use + 1))
                    if at_least(it, S):
                        act.wait_ge(tr_done, it.i + 1 - S)
                    act.activation(stage[:, k, :, F:2 * F], t_b[:, k, :, F:2 * F], ACT.Copy).then_inc(mean_done, 1)

                def rows_out(it):
                    act.wait_ge(tr_done, it.i + 1)
                    if at_least(it, 1):
                        act.wait_ge(hid_ready, parts * it.i)
                    act.activation(rows[:, :], p_t[:, :], ACT.Copy).then_inc(rows_done, 1)

                def relu(it):
                    if at_least(it, 1):
                        act.wait_ge(o_ready, it.i)
                    for q, cols in enumerate(part_cols):
                        act.wait_ge(hid_ready, parts * it.i + q + 1)
                        act.activation(hid[:, cols], p_h[:, cols], ACT.Relu, bias=b1c[:, :]).then_inc(hid_done, 1)

                def body(it, left):
                    mean_in(it)
                    layernorm_rstd(nc, act, ls, it.i + 1, ve[:, :], lnv[:, :], rs[:, :])
                    if at_least(it, 1):
                        relu(it.ahead(-1))
                    rows_out(it)
                run_loop(act, NT, body, S, S, S)
                relu(nth(NT - 1))

            @block.tensor
            def _(pe):
                def turn(it):
                    pe.wait_ge(ls["h"], it.i + 1)
                    pe.wait_ge(mean_done, it.i + 1)
                    if at_least(it, 1):
                        pe.wait_ge(rows_done, it.i)
                    pe.sem_inc(gate, 1)
                    for t in range(KG):
                        last = nc.tensor.transpose(p_t[:, t * P:(t + 1) * P], stage[:, it.slot, t * G:(t + 1) * G, :].rearrange("p g k -> p (g k)"), ident[:, :])
                    last.then_inc(tr_done, 1)

                def hidden(it):
                    pe.wait_ge(rows_done, it.i + 1)
                    if at_least(it, 1):
                        pe.wait_ge(hid_done, parts * it.i)
                    pe.sem_inc(gate, 1)
                    for cols in part_cols:
                        nc.tensor.matmul(p_h[:, cols], w1[:, :], rows[:, cols], start=True, stop=True).then_inc(hid_ready, 1)

                def finish(it):
                    pe.wait_ge(hid_done, parts * (it.i + 1))
                    if at_least(it, 1):
                        pe.wait_ge(o_done, it.i)
                    pe.sem_inc(gate, 1)
                    nc.tensor.matmul(p_o[:, :, :].rearrange("p k f -> p (k f)"), ones3[:, :], b2r[:, :], start=True, stop=False)
                    for t in range(KG):
                        last = nc.tensor.matmul(p_o[:, t * G:(t + 1) * G, :].rearrange("p g f -> p (g f)"), hid[:, t * P:(t + 1) * P], w2n[:, :],
                                                start=False, stop=(t == KG - 1))
                    last.then_inc(o_ready, 1)

                def body(it, left):
                    turn(it)
                    if at_least(it, 1):
                        finish(it.ahead(-1))
                    hidden(it)
                run_loop(pe, NT, body, S, S, S)
                finish(nth(NT - 1))

            @block.vector
            def _(dve):
                def stats(it):
                    c = it.i + 1
                    dve.wait_ge(x1_done, c)
                    if at_least(it, 1):
                        dve.wait_ge(ls["h"], it.i)
                    layernorm_stats(nc, dve, ls, c, x1[:, it.slot, :, :], sm[:, :], nm[:, :], cc[:, :, :], sq[:, :, :], vs[:, :], ve[:, :])

                def normed(it):
                    if at_least(it, S):
                        dve.wait_ge(tr_done, it.i + 1 - S)
                    layernorm_out(nc, dve, ls, it.i + 1, stage[:, it.slot, :, 0:F], cc[:, :, :], rs[:, :])

                def add(it):
                    k = it.slot
                    dve.wait_ge(o_ready, it.i + 1)
                    dve.wait_ge(x2_done, it.i + 1)
                    dve.wait_ge(stored[k], 16 * it.use)
                    nc.vector.tensor_tensor(o_b[:, k, :, :], p_o[:, :, :], x2[:, k, :, :], ALU.add).then_inc(o_done, 1)

                def body(it, left):
                    stats(it)
                    if at_least(it, 2):
                        add(it.ahead(-2))
                    normed(it)
                run_loop(dve, NT, body, S, S, S)
                add(nth(NT - 2))
                add(nth(NT - 1))


_INS = ["x", "src", "dst", "edge_attr_16", "L0_gnn_W_msg", "L0_gnn_b_msg", "L0_gnn_W_attn", "L0_gnn_b_attn",
        "L1_gnn_W1_l", "L1_gnn_b1", "L1_gnn_W1_r", "L1_gnn_W2_l", "L1_gnn_b2", "L1_gnn_W2_r"]


def kernel(**inputs):
    import numpy as _np
    import concourse.bacc as _bacc
    from concourse import mybir as _mybir
    from concourse.bass_utils import run_bass_kernel_spmd as _run

    nc = _bacc.Bacc("TRN2", target_bir_lowering=False, num_devices=1)
    arrays, args = {}, []
    for name in _INS:
        arr = _np.ascontiguousarray(inputs[name])
        arrays[f"in_{name}"] = arr
        args.append(nc.dram_tensor(f"in_{name}", arr.shape, _mybir.dt.from_np(arr.dtype), kind="ExternalInput").ap())
    args.append(nc.dram_tensor("out_0", (N, F), _mybir.dt.float32, kind="ExternalOutput").ap())
    gnn_program(nc, *args)
    r = _run(nc, [arrays], core_ids=[0])
    return r.results[0]["out_0"]
```
